# Optimizing a Trainium2 kernel written in Bass

```python
import numpy as np
import jax
import jax.numpy as jnp

def _softmax(x, axis=-1):
    return jax.nn.softmax(x, axis=axis)

def _gelu(x):
    return jax.nn.gelu(x, approximate=True)

def _silu(x):
    return jax.nn.silu(x)

def _sigmoid(x):
    return jax.nn.sigmoid(x)

def _layernorm(x, axis=-1, eps=1e-05):
    m = jnp.mean(x, axis=axis, keepdims=True)
    v = jnp.var(x, axis=axis, keepdims=True)
    return (x - m) / jnp.sqrt(v + eps)

def _scatter_add(tgt, idx, src, axis=0):
    return tgt.at[idx].add(src)

def _segment_sum(src, seg, n):
    return jax.ops.segment_sum(src, seg, n)
kernel_name = 'mk_seq_postln_d2_jaxref_r4_f5a761'

def setup_inputs(seed: int=0):
    np.random.seed(seed)
    _w = jnp.asarray

    def _L0_attn_setup():
        import jax, jax.numpy as jnp
        import numpy as np
        L, D, HS, E, ED, FE = (2, 256, 64, 32, 64, 3)
        H = D // HS
        B, T = (4, 512)
        EPS = 1e-05

        def _ln(x, w):
            mu = x.mean(-1, keepdims=True)
            var = ((x - mu) ** 2).mean(-1, keepdims=True)
            return (x - mu) / jnp.sqrt(var + EPS) * w

        def _shift(x):
            return jnp.concatenate([jnp.zeros_like(x[:, :1]), x[:, :-1]], axis=1)

        def _wkv(r, k, v, w, u):

            def step(state, inp):
                rt, kt, vt, wt = inp
                kv = kt[..., :, None] * vt[..., None, :]
                out = jnp.einsum('bhk,bhkv->bhv', rt, state + u[None, :, :, None] * kv)
                return (state * wt[..., None] + kv, out)
            init = jnp.zeros((r.shape[0], r.shape[1], r.shape[3], v.shape[3]), r.dtype)
            xs = tuple((jnp.moveaxis(a, 2, 0) for a in (r, k, v, w)))
            _, outs = jax.lax.scan(step, init, xs)
            return jnp.moveaxis(outs, 0, 2)

        def _time_mix(x, p):
            b, t, d = x.shape
            sx = _shift(x) - x
            xxx = x + sx * p['x_maa']
            mix = jnp.tanh(xxx @ p['tm_w1']).reshape(b * t, 5, E)
            mix = jnp.einsum('nfe,fed->fnd', mix, p['tm_w2']).reshape(5, b, t, d)
            mw, mk, mv, mr, mg = mix
            wx = x + sx * (p['w_maa'] + mw)
            kx = x + sx * (p['k_maa'] + mk)
            vx = x + sx * (p['v_maa'] + mv)
            rx = x + sx * (p['r_maa'] + mr)
            gx = x + sx * (p['g_maa'] + mg)
            r = jax.nn.sigmoid(rx @ p['Wr'])
            k = kx @ p['Wk']
            v = vx @ p['Wv']
            g = jax.nn.silu(gx @ p['Wg'])
            w = jnp.tanh(wx @ p['td_w1']) @ p['td_w2']
            w = jnp.exp(-jnp.exp(p['time_decay'][None, :, None, :] + w.reshape(b, t, H, HS).transpose(0, 2, 1, 3)))
            r4 = r.reshape(b, t, H, HS).transpose(0, 2, 1, 3)
            k4 = k.reshape(b, t, H, HS).transpose(0, 2, 1, 3)
            v4 = v.reshape(b, t, H, HS).transpose(0, 2, 1, 3)
            out = _wkv(r4, k4, v4, w, p['time_first']).transpose(0, 2, 1, 3).reshape(b * t, H, HS)
            mu = out.mean(-1, keepdims=True)
            var = ((out - mu) ** 2).mean(-1, keepdims=True)
            out = ((out - mu) / jnp.sqrt(var + EPS)).reshape(b * t, d) * p['gn_w'] + p['gn_b']
            return out.reshape(b, t, d) * g @ p['Wo']

        def _channel_mix(x, p):
            sx = _shift(x) - x
            k = jnp.square(jax.nn.relu((x + sx * p['ck_maa']) @ p['cWk']))
            return jax.nn.sigmoid((x + sx * p['cr_maa']) @ p['cWr']) * (k @ p['cWv'])
        PER_LAYER = ['ln1_w', 'ln2_w', 'x_maa', 'w_maa', 'k_maa', 'v_maa', 'r_maa', 'g_maa', 'tm_w1', 'tm_w2', 'td_w1', 'td_w2', 'time_decay', 'time_first', 'Wr', 'Wk', 'Wv', 'Wo', 'Wg', 'gn_w', 'gn_b', 'ck_maa', 'cr_maa', 'cWk', 'cWv', 'cWr']

        def _forward(x, params):
            for i in range(L):
                p = {n: params[n][i] for n in PER_LAYER}
                x = x + _time_mix(_ln(x, p['ln1_w']), p)
                x = x + _channel_mix(_ln(x, p['ln2_w']), p)
            return _ln(x, params['ln_out_w'])
        key = jax.random.key(seed)
        ks = jax.random.split(key, 20)

        def nrm(k, shape, s=0.02):
            return jax.random.normal(k, shape, dtype=jnp.float32) * s

        def uni(k, shape):
            return jax.random.uniform(k, shape, dtype=jnp.float32)
        return dict(x=jax.random.normal(ks[0], (B, T, D), dtype=jnp.float32), ln1_w=jnp.ones((L, D), jnp.float32), ln2_w=jnp.ones((L, D), jnp.float32), x_maa=uni(ks[1], (L, D)), w_maa=uni(ks[2], (L, D)), k_maa=uni(ks[3], (L, D)), v_maa=uni(ks[4], (L, D)), r_maa=uni(ks[5], (L, D)), g_maa=uni(ks[6], (L, D)), tm_w1=nrm(ks[7], (L, D, 5 * E)), tm_w2=nrm(ks[8], (L, 5, E, D)), td_w1=nrm(ks[9], (L, D, ED)), td_w2=nrm(ks[10], (L, ED, D)), time_decay=jax.random.uniform(ks[11], (L, H, HS), jnp.float32, -6.0, -1.0), time_first=nrm(ks[12], (L, H, HS), 0.3), Wr=nrm(ks[13], (L, D, D)), Wk=nrm(ks[14], (L, D, D)), Wv=nrm(ks[15], (L, D, D)), Wo=nrm(ks[16], (L, D, D)), Wg=nrm(ks[17], (L, D, D)), gn_w=jnp.ones((L, D), jnp.float32), gn_b=jnp.zeros((L, D), jnp.float32), ck_maa=uni(ks[18], (L, D)), cr_maa=uni(ks[19], (L, D)), cWk=nrm(jax.random.fold_in(key, 100), (L, D, FE * D)), cWv=nrm(jax.random.fold_in(key, 101), (L, FE * D, D)), cWr=nrm(jax.random.fold_in(key, 102), (L, D, D)), ln_out_w=jnp.ones((D,), jnp.float32))
    _L0_attn_in = _L0_attn_setup()

    def _L0_ffn_setup():
        import jax, jax.numpy as jnp
        import numpy as np
        B, S, H, NH, E, F = (4, 256, 256, 16, 8, 1024)
        D = H // NH
        EPS = 1e-05

        def _layernorm(x, g, b):
            mu = jnp.mean(x, axis=-1, keepdims=True)
            var = jnp.var(x, axis=-1, keepdims=True)
            return (x - mu) * jax.lax.rsqrt(var + EPS) * g + b
        key = jax.random.key(seed)
        ks = jax.random.split(key, 16)
        s = 0.02
        return {'x': jax.random.normal(ks[0], (B, S, H), jnp.float32), 'ln1_g': jnp.ones((H,), jnp.float32), 'ln1_b': jnp.zeros((H,), jnp.float32), 'ln2_g': jnp.ones((H,), jnp.float32), 'ln2_b': jnp.zeros((H,), jnp.float32), 'wq': jax.random.normal(ks[1], (H, H), jnp.float32) * s, 'bq': jnp.zeros((H,), jnp.float32), 'wk': jax.random.normal(ks[2], (H, H), jnp.float32) * s, 'bk': jnp.zeros((H,), jnp.float32), 'wv': jax.random.normal(ks[3], (H, H), jnp.float32) * s, 'bv': jnp.zeros((H,), jnp.float32), 'wo': jax.random.normal(ks[4], (H, H), jnp.float32) * s, 'bo': jnp.zeros((H,), jnp.float32), 'gate_w': jax.random.normal(ks[5], (H, E), jnp.float32) * s, 'gate_b': jnp.zeros((E,), jnp.float32), 'w1': jax.random.normal(ks[6], (E, H, F), jnp.float32) * s, 'b1': jnp.zeros((E, F), jnp.float32), 'w2': jax.random.normal(ks[7], (E, F, H), jnp.float32) * s, 'b2': jnp.zeros((E, H), jnp.float32)}
    _L0_ffn_in = _L0_ffn_setup()

    def _L1_attn_setup():
        import jax, jax.numpy as jnp
        import numpy as np
        B, S, D = (4, 512, 256)
        H, C = (16, 64)
        HID = H * C
        key = jax.random.key(seed)
        ks = jax.random.split(key, 9)
        scale = 0.02
        return {'x': jax.random.normal(ks[0], (B, S, D), dtype=jnp.float32), 'Wq': jax.random.normal(ks[1], (D, HID), dtype=jnp.float32) * scale, 'bq': jnp.zeros((HID,), dtype=jnp.float32), 'Wk': jax.random.normal(ks[2], (D, HID), dtype=jnp.float32) * scale, 'bk': jnp.zeros((HID,), dtype=jnp.float32), 'Wv': jax.random.normal(ks[3], (D, HID), dtype=jnp.float32) * scale, 'bv': jnp.zeros((HID,), dtype=jnp.float32), 'Wo': jax.random.normal(ks[4], (HID, D), dtype=jnp.float32) * scale, 'bo': jnp.zeros((D,), dtype=jnp.float32)}
    _L1_attn_in = _L1_attn_setup()

    def _L1_ffn_setup():
        import jax, jax.numpy as jnp
        import numpy as np
        BLOCK = 16
        _GRID = jnp.array([0.0, 0.5, 1.0, 1.5, 2.0, 3.0, 4.0, 6.0], dtype=jnp.float32)
        _MID = jnp.array([0.25, 0.75, 1.25, 1.75, 2.5, 3.5, 5.0], dtype=jnp.float32)

        def fp4_quant_dequant(x):
            shape = x.shape
            xb = x.reshape(shape[:-1] + (shape[-1] // BLOCK, BLOCK))
            scale = jnp.max(jnp.abs(xb), axis=-1, keepdims=True) / 6.0
            scale = jnp.maximum(scale, jnp.float32(1e-12))
            xn = xb / scale
            idx = jnp.searchsorted(_MID, jnp.abs(xn))
            q = _GRID[idx] * jnp.sign(xn) * scale
            return q.reshape(shape)

        def fp4_linear(x, w):
            xq = fp4_quant_dequant(x)
            wq = fp4_quant_dequant(w)
            return jnp.einsum('bsk,nk->bsn', xq, wq)
        key = jax.random.key(seed)
        k1, k2, k3, k4 = jax.random.split(key, 4)
        H, I = (256, 704)
        x = jax.random.normal(k1, (4, 1024, H), dtype=jnp.float32)
        w_gate = jax.random.normal(k2, (I, H), dtype=jnp.float32) * 0.02
        w_up = jax.random.normal(k3, (I, H), dtype=jnp.float32) * 0.02
        w_down = jax.random.normal(k4, (H, I), dtype=jnp.float32) * 0.02
        return {'x': x, 'w_gate': w_gate, 'w_up': w_up, 'w_down': w_down}
    _L1_ffn_in = _L1_ffn_setup()
    _d = {'L0_attn_x': _L0_attn_in['x'], 'L0_attn_ln1_w': _L0_attn_in['ln1_w'], 'L0_attn_ln2_w': _L0_attn_in['ln2_w'], 'L0_attn_x_maa': _L0_attn_in['x_maa'], 'L0_attn_w_maa': _L0_attn_in['w_maa'], 'L0_attn_k_maa': _L0_attn_in['k_maa'], 'L0_attn_v_maa': _L0_attn_in['v_maa'], 'L0_attn_r_maa': _L0_attn_in['r_maa'], 'L0_attn_g_maa': _L0_attn_in['g_maa'], 'L0_attn_tm_w1': _L0_attn_in['tm_w1'], 'L0_attn_tm_w2': _L0_attn_in['tm_w2'], 'L0_attn_td_w1': _L0_attn_in['td_w1'], 'L0_attn_td_w2': _L0_attn_in['td_w2'], 'L0_attn_time_decay': _L0_attn_in['time_decay'], 'L0_attn_time_first': _L0_attn_in['time_first'], 'L0_attn_Wr': _L0_attn_in['Wr'], 'L0_attn_Wk': _L0_attn_in['Wk'], 'L0_attn_Wv': _L0_attn_in['Wv'], 'L0_attn_Wo': _L0_attn_in['Wo'], 'L0_attn_Wg': _L0_attn_in['Wg'], 'L0_attn_gn_w': _L0_attn_in['gn_w'], 'L0_attn_gn_b': _L0_attn_in['gn_b'], 'L0_attn_ck_maa': _L0_attn_in['ck_maa'], 'L0_attn_cr_maa': _L0_attn_in['cr_maa'], 'L0_attn_cWk': _L0_attn_in['cWk'], 'L0_attn_cWv': _L0_attn_in['cWv'], 'L0_attn_cWr': _L0_attn_in['cWr'], 'L0_attn_ln_out_w': _L0_attn_in['ln_out_w'], 'L0_ffn_ln1_g': _L0_ffn_in['ln1_g'], 'L0_ffn_ln1_b': _L0_ffn_in['ln1_b'], 'L0_ffn_ln2_g': _L0_ffn_in['ln2_g'], 'L0_ffn_ln2_b': _L0_ffn_in['ln2_b'], 'L0_ffn_wq': _L0_ffn_in['wq'], 'L0_ffn_bq': _L0_ffn_in['bq'], 'L0_ffn_wk': _L0_ffn_in['wk'], 'L0_ffn_bk': _L0_ffn_in['bk'], 'L0_ffn_wv': _L0_ffn_in['wv'], 'L0_ffn_bv': _L0_ffn_in['bv'], 'L0_ffn_wo': _L0_ffn_in['wo'], 'L0_ffn_bo': _L0_ffn_in['bo'], 'L0_ffn_gate_w': _L0_ffn_in['gate_w'], 'L0_ffn_gate_b': _L0_ffn_in['gate_b'], 'L0_ffn_w1': _L0_ffn_in['w1'], 'L0_ffn_b1': _L0_ffn_in['b1'], 'L0_ffn_w2': _L0_ffn_in['w2'], 'L0_ffn_b2': _L0_ffn_in['b2'], 'L1_attn_Wq': _L1_attn_in['Wq'], 'L1_attn_bq': _L1_attn_in['bq'], 'L1_attn_Wk': _L1_attn_in['Wk'], 'L1_attn_bk': _L1_attn_in['bk'], 'L1_attn_Wv': _L1_attn_in['Wv'], 'L1_attn_bv': _L1_attn_in['bv'], 'L1_attn_Wo': _L1_attn_in['Wo'], 'L1_attn_bo': _L1_attn_in['bo'], 'L1_ffn_w_gate': _L1_ffn_in['w_gate'], 'L1_ffn_w_up': _L1_ffn_in['w_up'], 'L1_ffn_w_down': _L1_ffn_in['w_down']}
    _x0 = _d['L0_attn_x']
    _d['L0_attn_x'] = jax.random.normal(jax.random.fold_in(jax.random.key(seed), 1), (4, 1024, 256), dtype=_x0.dtype)
    del _x0
    return _d

def reference(L0_attn_x, L0_attn_ln1_w, L0_attn_ln2_w, L0_attn_x_maa, L0_attn_w_maa, L0_attn_k_maa, L0_attn_v_maa, L0_attn_r_maa, L0_attn_g_maa, L0_attn_tm_w1, L0_attn_tm_w2, L0_attn_td_w1, L0_attn_td_w2, L0_attn_time_decay, L0_attn_time_first, L0_attn_Wr, L0_attn_Wk, L0_attn_Wv, L0_attn_Wo, L0_attn_Wg, L0_attn_gn_w, L0_attn_gn_b, L0_attn_ck_maa, L0_attn_cr_maa, L0_attn_cWk, L0_attn_cWv, L0_attn_cWr, L0_attn_ln_out_w, L0_ffn_ln1_g, L0_ffn_ln1_b, L0_ffn_ln2_g, L0_ffn_ln2_b, L0_ffn_wq, L0_ffn_bq, L0_ffn_wk, L0_ffn_bk, L0_ffn_wv, L0_ffn_bv, L0_ffn_wo, L0_ffn_bo, L0_ffn_gate_w, L0_ffn_gate_b, L0_ffn_w1, L0_ffn_b1, L0_ffn_w2, L0_ffn_b2, L1_attn_Wq, L1_attn_bq, L1_attn_Wk, L1_attn_bk, L1_attn_Wv, L1_attn_bv, L1_attn_Wo, L1_attn_bo, L1_ffn_w_gate, L1_ffn_w_up, L1_ffn_w_down):

    def _L0_attn_ref(x, ln1_w, ln2_w, x_maa, w_maa, k_maa, v_maa, r_maa, g_maa, tm_w1, tm_w2, td_w1, td_w2, time_decay, time_first, Wr, Wk, Wv, Wo, Wg, gn_w, gn_b, ck_maa, cr_maa, cWk, cWv, cWr, ln_out_w):
        import jax, jax.numpy as jnp
        import numpy as np
        L, D, HS, E, ED, FE = (2, 256, 64, 32, 64, 3)
        H = D // HS
        B, T = (4, 512)
        EPS = 1e-05

        def _ln(x, w):
            mu = x.mean(-1, keepdims=True)
            var = ((x - mu) ** 2).mean(-1, keepdims=True)
            return (x - mu) / jnp.sqrt(var + EPS) * w

        def _shift(x):
            return jnp.concatenate([jnp.zeros_like(x[:, :1]), x[:, :-1]], axis=1)

        def _wkv(r, k, v, w, u):

            def step(state, inp):
                rt, kt, vt, wt = inp
                kv = kt[..., :, None] * vt[..., None, :]
                out = jnp.einsum('bhk,bhkv->bhv', rt, state + u[None, :, :, None] * kv)
                return (state * wt[..., None] + kv, out)
            init = jnp.zeros((r.shape[0], r.shape[1], r.shape[3], v.shape[3]), r.dtype)
            xs = tuple((jnp.moveaxis(a, 2, 0) for a in (r, k, v, w)))
            _, outs = jax.lax.scan(step, init, xs)
            return jnp.moveaxis(outs, 0, 2)

        def _time_mix(x, p):
            b, t, d = x.shape
            sx = _shift(x) - x
            xxx = x + sx * p['x_maa']
            mix = jnp.tanh(xxx @ p['tm_w1']).reshape(b * t, 5, E)
            mix = jnp.einsum('nfe,fed->fnd', mix, p['tm_w2']).reshape(5, b, t, d)
            mw, mk, mv, mr, mg = mix
            wx = x + sx * (p['w_maa'] + mw)
            kx = x + sx * (p['k_maa'] + mk)
            vx = x + sx * (p['v_maa'] + mv)
            rx = x + sx * (p['r_maa'] + mr)
            gx = x + sx * (p['g_maa'] + mg)
            r = jax.nn.sigmoid(rx @ p['Wr'])
            k = kx @ p['Wk']
            v = vx @ p['Wv']
            g = jax.nn.silu(gx @ p['Wg'])
            w = jnp.tanh(wx @ p['td_w1']) @ p['td_w2']
            w = jnp.exp(-jnp.exp(p['time_decay'][None, :, None, :] + w.reshape(b, t, H, HS).transpose(0, 2, 1, 3)))
            r4 = r.reshape(b, t, H, HS).transpose(0, 2, 1, 3)
            k4 = k.reshape(b, t, H, HS).transpose(0, 2, 1, 3)
            v4 = v.reshape(b, t, H, HS).transpose(0, 2, 1, 3)
            out = _wkv(r4, k4, v4, w, p['time_first']).transpose(0, 2, 1, 3).reshape(b * t, H, HS)
            mu = out.mean(-1, keepdims=True)
            var = ((out - mu) ** 2).mean(-1, keepdims=True)
            out = ((out - mu) / jnp.sqrt(var + EPS)).reshape(b * t, d) * p['gn_w'] + p['gn_b']
            return out.reshape(b, t, d) * g @ p['Wo']

        def _channel_mix(x, p):
            sx = _shift(x) - x
            k = jnp.square(jax.nn.relu((x + sx * p['ck_maa']) @ p['cWk']))
            return jax.nn.sigmoid((x + sx * p['cr_maa']) @ p['cWr']) * (k @ p['cWv'])
        PER_LAYER = ['ln1_w', 'ln2_w', 'x_maa', 'w_maa', 'k_maa', 'v_maa', 'r_maa', 'g_maa', 'tm_w1', 'tm_w2', 'td_w1', 'td_w2', 'time_decay', 'time_first', 'Wr', 'Wk', 'Wv', 'Wo', 'Wg', 'gn_w', 'gn_b', 'ck_maa', 'cr_maa', 'cWk', 'cWv', 'cWr']

        def _forward(x, params):
            for i in range(L):
                p = {n: params[n][i] for n in PER_LAYER}
                x = x + _time_mix(_ln(x, p['ln1_w']), p)
                x = x + _channel_mix(_ln(x, p['ln2_w']), p)
            return _ln(x, params['ln_out_w'])
        params = dict(ln1_w=ln1_w, ln2_w=ln2_w, x_maa=x_maa, w_maa=w_maa, k_maa=k_maa, v_maa=v_maa, r_maa=r_maa, g_maa=g_maa, tm_w1=tm_w1, tm_w2=tm_w2, td_w1=td_w1, td_w2=td_w2, time_decay=time_decay, time_first=time_first, Wr=Wr, Wk=Wk, Wv=Wv, Wo=Wo, Wg=Wg, gn_w=gn_w, gn_b=gn_b, ck_maa=ck_maa, cr_maa=cr_maa, cWk=cWk, cWv=cWv, cWr=cWr, ln_out_w=ln_out_w)
        return _forward(x, params)

    def _L0_ffn_ref(x, ln1_g, ln1_b, ln2_g, ln2_b, wq, bq, wk, bk, wv, bv, wo, bo, gate_w, gate_b, w1, b1, w2, b2):
        import jax, jax.numpy as jnp
        import numpy as np
        B, S, H, NH, E, F = (4, 256, 256, 16, 8, 1024)
        D = H // NH
        EPS = 1e-05

        def _layernorm(x, g, b):
            mu = jnp.mean(x, axis=-1, keepdims=True)
            var = jnp.var(x, axis=-1, keepdims=True)
            return (x - mu) * jax.lax.rsqrt(var + EPS) * g + b
        b, s, h = x.shape
        hn = _layernorm(x, ln1_g, ln1_b)
        q = (hn @ wq + bq).reshape(b, s, NH, D).transpose(0, 2, 1, 3)
        k = (hn @ wk + bk).reshape(b, s, NH, D).transpose(0, 2, 1, 3)
        v = (hn @ wv + bv).reshape(b, s, NH, D).transpose(0, 2, 1, 3)
        scores = jnp.einsum('bhqd,bhkd->bhqk', q, k) / jnp.sqrt(jnp.float32(D))
        attn = jax.nn.softmax(scores, axis=-1)
        o = jnp.einsum('bhqk,bhkd->bhqd', attn, v)
        o = o.transpose(0, 2, 1, 3).reshape(b, s, h)
        x = x + (o @ wo + bo)
        hn2 = _layernorm(x, ln2_g, ln2_b).reshape(-1, h)
        logits = hn2 @ gate_w + gate_b
        idx = jnp.argmax(logits, axis=-1)
        mid = jax.nn.relu(jnp.einsum('th,ehf->etf', hn2, w1) + b1[:, None, :])
        y = jnp.einsum('etf,efh->eth', mid, w2) + b2[:, None, :]
        moe = y[idx, jnp.arange(hn2.shape[0])]
        return x + moe.reshape(b, s, h)

    def _L1_attn_ref(x, Wq, bq, Wk, bk, Wv, bv, Wo, bo):
        import jax, jax.numpy as jnp
        import numpy as np
        B, S, D = (4, 512, 256)
        H, C = (16, 64)
        HID = H * C
        b, s, _ = x.shape
        inv_sqrt_c = jnp.asarray(1.0 / C ** 0.5, dtype=x.dtype)
        Q = (x @ Wq + bq).reshape(b, s, H, C) * inv_sqrt_c
        K = (x @ Wk + bk).reshape(b, s, H, C)
        V = (x @ Wv + bv).reshape(b, s, H, C)
        scores = jnp.einsum('bshq,bshk->bshqk', Q, K)
        mask = jnp.triu(jnp.ones((C, C), dtype=bool), 1)
        scores = jnp.where(mask, jnp.asarray(-jnp.inf, scores.dtype), scores)
        w = jax.nn.softmax(scores, axis=-1)
        attn = jnp.einsum('bshqk,bshk->bshq', w, V)
        attn = attn.reshape(b, s, HID)
        return attn @ Wo + bo

    def _L1_ffn_ref(x, w_gate, w_up, w_down):
        import jax, jax.numpy as jnp
        import numpy as np
        BLOCK = 16
        _GRID = jnp.array([0.0, 0.5, 1.0, 1.5, 2.0, 3.0, 4.0, 6.0], dtype=jnp.float32)
        _MID = jnp.array([0.25, 0.75, 1.25, 1.75, 2.5, 3.5, 5.0], dtype=jnp.float32)

        def fp4_quant_dequant(x):
            shape = x.shape
            xb = x.reshape(shape[:-1] + (shape[-1] // BLOCK, BLOCK))
            scale = jnp.max(jnp.abs(xb), axis=-1, keepdims=True) / 6.0
            scale = jnp.maximum(scale, jnp.float32(1e-12))
            xn = xb / scale
            idx = jnp.searchsorted(_MID, jnp.abs(xn))
            q = _GRID[idx] * jnp.sign(xn) * scale
            return q.reshape(shape)

        def fp4_linear(x, w):
            xq = fp4_quant_dequant(x)
            wq = fp4_quant_dequant(w)
            return jnp.einsum('bsk,nk->bsn', xq, wq)
        gate = fp4_linear(x, w_gate)
        y = fp4_linear(x, w_up)
        h = jax.nn.silu(gate) * y
        return fp4_linear(h, w_down)
    x = L0_attn_x
    x = _layernorm(x + _L0_attn_ref(x, L0_attn_ln1_w, L0_attn_ln2_w, L0_attn_x_maa, L0_attn_w_maa, L0_attn_k_maa, L0_attn_v_maa, L0_attn_r_maa, L0_attn_g_maa, L0_attn_tm_w1, L0_attn_tm_w2, L0_attn_td_w1, L0_attn_td_w2, L0_attn_time_decay, L0_attn_time_first, L0_attn_Wr, L0_attn_Wk, L0_attn_Wv, L0_attn_Wo, L0_attn_Wg, L0_attn_gn_w, L0_attn_gn_b, L0_attn_ck_maa, L0_attn_cr_maa, L0_attn_cWk, L0_attn_cWv, L0_attn_cWr, L0_attn_ln_out_w), axis=-1)
    x = _layernorm(x + _L0_ffn_ref(x, L0_ffn_ln1_g, L0_ffn_ln1_b, L0_ffn_ln2_g, L0_ffn_ln2_b, L0_ffn_wq, L0_ffn_bq, L0_ffn_wk, L0_ffn_bk, L0_ffn_wv, L0_ffn_bv, L0_ffn_wo, L0_ffn_bo, L0_ffn_gate_w, L0_ffn_gate_b, L0_ffn_w1, L0_ffn_b1, L0_ffn_w2, L0_ffn_b2), axis=-1)
    x = _layernorm(x + _L1_attn_ref(x, L1_attn_Wq, L1_attn_bq, L1_attn_Wk, L1_attn_bk, L1_attn_Wv, L1_attn_bv, L1_attn_Wo, L1_attn_bo), axis=-1)
    x = _layernorm(x + _L1_ffn_ref(x, L1_ffn_w_gate, L1_ffn_w_up, L1_ffn_w_down), axis=-1)
    return x

_drawn_inputs = setup_inputs


def setup_inputs(seed=0):
    import zlib

    import numpy as np

    out = dict(_drawn_inputs(seed))
    spreads = {'L0_attn_ln1_w': (1.0, 0.6),
     'L0_attn_ln2_w': (1.0, 0.6),
     'L0_attn_gn_w': (1.0, 0.6),
     'L0_attn_gn_b': (0.0, 0.8),
     'L0_attn_ln_out_w': (1.0, 0.2),
     'L0_ffn_ln1_g': (1.0, 0.6),
     'L0_ffn_ln1_b': (0.0, 0.657),
     'L0_ffn_ln2_g': (1.0, 0.2),
     'L0_ffn_ln2_b': (0.0, 0.1),
     'L0_ffn_bq': (0.0, 0.8),
     'L0_ffn_bk': (0.0, 2.0),
     'L0_ffn_bv': (0.0, 0.377),
     'L0_ffn_bo': (0.0, 0.1),
     'L0_ffn_gate_b': (0.0, 0.1),
     'L0_ffn_b1': (0.0, 0.361),
     'L0_ffn_b2': (0.0, 0.1),
     'L1_attn_bq': (0.0, 2.0),
     'L1_attn_bk': (0.0, 2.0),
     'L1_attn_bv': (0.0, 0.411),
     'L1_attn_bo': (0.0, 0.1)}
    factors = {'L0_attn_x_maa': 8.0,
     'L0_attn_w_maa': 8.0,
     'L0_attn_k_maa': 3.603,
     'L0_attn_v_maa': 3.405,
     'L0_attn_r_maa': 8.0,
     'L0_attn_g_maa': 2.685,
     'L0_attn_tm_w1': 8.0,
     'L0_attn_tm_w2': 8.0,
     'L0_attn_td_w1': 8.0,
     'L0_attn_td_w2': 8.0,
     'L0_attn_time_first': 8.0,
     'L0_attn_Wr': 6.532,
     'L0_attn_ck_maa': 4.272,
     'L0_attn_cr_maa': 8.0,
     'L0_attn_cWk': 2.834,
     'L0_attn_cWr': 8.0,
     'L0_ffn_wq': 8.0,
     'L0_ffn_wk': 8.0,
     'L0_ffn_wv': 4.982,
     'L1_attn_Wq': 8.0,
     'L1_attn_Wk': 8.0}
    for name, (base, spread) in spreads.items():
        noise = np.random.default_rng([zlib.crc32(name.encode()), seed]).standard_normal(out[name].shape)
        drawn = base * np.exp(spread * noise) if base else spread * noise
        out[name] = jnp.asarray(drawn.astype(out[name].dtype))
    for name, factor in factors.items():
        out[name] = (out[name] * factor).astype(out[name].dtype)
    return out
```

```python
from contextlib import ExitStack

import numpy as np
import concourse.bass as bass
from concourse import mybir

F32 = mybir.dt.float32
BF16 = mybir.dt.bfloat16
U8 = mybir.dt.uint8
ALU = mybir.AluOpType
ACT = mybir.ActivationFunctionType
AX = mybir.AxisListType

P = 128
B, T, D = 4, 1024, 256
DC = D // P
N = B * T
EPS = 1e-5
BIG = 3.0e38


class Steps:

    def __init__(self, eng, sem, per_pass, n):
        self.eng, self.sem, self.per, self.n, self.k = eng, sem, per_pass, n, 0

    def done(self, ins):
        self.k += 1
        ins.then_inc(self.sem, 1)
        self.eng.wait_ge(self.sem, self.n * self.per + self.k)

    def close(self):
        assert self.k == self.per, (self.k, self.per)


def allocators(nc, ctx, tag):
    def sb(name, shape, dt=F32):
        return ctx.enter_context(nc.sbuf_tensor(f"{tag}_{name}", shape, dt))

    def psum(name, shape, dt=F32):
        return ctx.enter_context(nc.psum_tensor(f"{tag}_{name}", shape, dt))

    held = []

    def clear():
        nc.clear_and_free_semaphores(held)
        nc.all_engine_barrier()

    ctx.callback(clear)

    def sem(name):
        held.append(nc.alloc_semaphore(f"{tag}_{name}"))
        return held[-1]

    return sb, psum, sem


def feature_attention(nc, x_fm, wq, bq, wk, bk, wv, bv, wo, bo, out_tm):
    H, C = 16, 64
    HID = H * C
    TILES = N // P
    HC = HID // P
    GROUP_MAX = 3072
    groups, cur, size = [], [], 0
    for j in range(C):
        w = H * (C - j)
        if cur and size + w > GROUP_MAX:
            groups.append(cur)
            cur, size = [], 0
        cur.append(j)
        size += w
    groups.append(cur)
    NG = len(groups)
    place = {}
    size_of = []
    for g in groups:
        o = 0
        for j in g:
            place[j] = o
            o += H * (C - j)
        size_of.append(o)
    SB, TB = 4, 3

    with ExitStack() as ctx:
        sb, psum, sem = allocators(nc, ctx, "fa")
        wq_sb = sb("wq", [P, DC, HID])
        wk_sb = sb("wk", [P, DC, HID])
        wv_sb = sb("wv", [P, DC, HID])
        wo_sb = sb("wo", [P, HC, D])
        bq_sb = sb("bq", [P, HID])
        bk_sb = sb("bk", [P, HID])
        bv_sb = sb("bv", [P, HID])
        bo_sb = sb("bo", [P, D])
        ident = sb("ident", [P, P])
        lift = sb("lift", [P, 2, HID])
        eps = sb("eps", [P, 1])
        xT = sb("xT", [P, 2, DC, P])
        Q = sb("Q", [P, HID])
        K = sb("K", [P, HID])
        V = sb("V", [P, HID])
        kmax = sb("kmax", [P, HID])
        kmin = sb("kmin", [P, HID])
        M = sb("M", [P, HID])
        S = sb("S", [P, SB, GROUP_MAX])
        PV = sb("PV", [P, TB, GROUP_MAX])
        rden = sb("rden", [P, HID])
        att = sb("att", [P, HID])
        attT = sb("attT", [P, HC, P])
        res = sb("res", [P, D])
        y = sb("y", [P, D])
        stats = sb("stats", [P, 6])
        mv = sb("mv", [P, 2])
        spare = sb("spare", [P, 1])
        std = sb("std", [P, 1])
        rstd = sb("rstd", [P, 1])
        yn = sb("yn", [P, 2, D])

        num = psum("num", [P, HID])
        den = psum("den", [P, HID])
        pa = psum("pa", [P, HID])
        pb = psum("pb", [P, HID])

        weights_in = sem("weights_in")
        consts = sem("consts")
        consts_v = sem("consts_v")
        x_in = [sem("x_in0"), sem("x_in1")]
        x_used = sem("x_used")
        q_mm = sem("q_mm")
        k_mm = sem("k_mm")
        v_mm = sem("v_mm")
        q_out = sem("q_out")
        k_out = sem("k_out")
        v_out = sem("v_out")
        max_ready = sem("max_ready")
        scores = sem("scores")
        shifted = sem("shifted")
        probs = sem("probs")
        weighted = sem("weighted")
        den_used = sem("den_used")
        num_used = sem("num_used")
        att_ready = sem("att_ready")
        attT_mm = sem("attT_mm")
        attT_out = sem("attT_out")
        y_mm = sem("y_mm")
        y_ready = sem("y_ready")
        var_ready = sem("var_ready")
        std_ready = sem("std_ready")
        yn_ready = sem("yn_ready")
        stored = [sem("stored0"), sem("stored1")]
        vec = sem("vec")
        block = ctx.enter_context(nc.Block())
        U = 2
        NI = TILES // U

        @block.sync
        def _(sp):
            for w_sb, w in ((wq_sb, wq), (wk_sb, wk), (wv_sb, wv), (wo_sb, wo)):
                sp.dma_start(w_sb[:], w.rearrange("(c p) n -> p c n", p=P)).then_inc(weights_in, 16)
            for b_sb, b_ in ((bq_sb, bq), (bk_sb, bk), (bv_sb, bv), (bo_sb, bo)):
                sp.dma_start(b_sb[:], b_.rearrange("(a n) -> a n", a=1).broadcast_to([P, b_.shape[0]]))\
                    .then_inc(weights_in, 16)
            x_v = x_fm.rearrange("(c p) t -> p c t", p=P)
            with sp.Fori(0, NI) as i:
                for u in range(U):
                    sp.wait_ge(x_used, i * U)
                    sp.dma_start(xT[:, u], x_v[:, :, bass.ds((i * U + u) * P, P)]).then_inc(x_in[u], 16)

        @block.gpsimd
        def _(pool):
            pool.memset(ident[:], 0.0).then_inc(consts, 1)
            pool.wait_ge(consts, 1)
            pool.affine_select(out=ident[:], in_=ident[:], compare_op=ALU.not_equal, fill=1.0, base=0,
                               pattern=[[-1, P]], channel_multiplier=1).then_inc(consts, 1)
            out_v = out_tm
            with pool.Fori(0, NI) as i:
                for u in range(U):
                    n = i * U + u
                    for g, js in enumerate(groups):
                        pool.wait_ge(scores, n * NG + g + 1)
                        if g == 0:
                            pool.wait_ge(max_ready, n + 1)
                        s = (g) % SB
                        for j in js:
                            w = C - j
                            run = S[:, s, place[j]:place[j] + H * w].rearrange("p (h w) -> p h w", h=H)
                            mm = M[:].rearrange("p (h c) -> p h c", h=H)[:, :, j:C]
                            ins = pool.tensor_tensor(run, run, mm, ALU.subtract)
                        ins.then_inc(shifted, 1)

        @block.scalar
        def _(act):
            with act.Fori(0, NI) as i:
                for u in range(U):
                    n = i * U + u
                    for g in range(NG):
                        act.wait_ge(shifted, n * NG + g + 1)
                        s = g % SB
                        nc.scalar.activation(S[:, s, 0:size_of[g]], S[:, s, 0:size_of[g]],
                                             ACT.Exp).then_inc(probs, 1)
                    for h2 in range(2):
                        act.wait_ge(attT_mm, n * 2 + h2 + 1)
                        nc.scalar.activation(attT[:, 4 * h2:4 * h2 + 4].rearrange("p c t -> p (c t)"),
                                             pb[:, 512 * h2:512 * h2 + 512], ACT.Copy).then_inc(attT_out, 1)
                    act.wait_ge(var_ready, n + 1)
                    nc.scalar.activation(std[:], mv[:, 1:2], ACT.Sqrt, bias=eps[:, 0:1]).then_inc(std_ready, 1)
                    act.wait_ge(yn_ready, n + 1)
                    act.dma_start(out_tm[bass.ds(n * P, P), :], yn[:, u]).then_inc(stored[u], 16)
            act.wait_ge(stored[0], 16 * NI)
            act.wait_ge(stored[1], 16 * NI)

        @block.vector
        def _(dve):
            nc.vector.memset(eps[:], EPS).then_inc(consts_v, 1)
            nc.vector.memset(lift[:], 0.0).then_inc(consts_v, 1)
            dve.wait_ge(consts_v, 2)
            lv = lift[:].rearrange("p a (h c) -> p a h c", h=H)
            nc.vector.memset(lv[:, 0, :, 0:1], -BIG).then_inc(consts_v, 1)
            nc.vector.memset(lv[:, 1, :, 0:1], BIG).then_inc(consts_v, 1)
            dve.wait_ge(consts_v, 4)
            dve.wait_ge(weights_in, 16 * 8)
            with dve.Fori(0, NI) as i:
                own = Steps(dve, vec, U * 10, i)
                for u in range(U):
                    n = i * U + u
                    dve.wait_ge(k_mm, n * 2 + 2)
                    ins = nc.vector.tensor_tensor(K[:], pb[:], bk_sb[:], ALU.add)
                    ins.then_inc(k_out, 1)
                    dve.wait_ge(k_out, n + 1)
                    own.done(nc.vector.tensor_tensor_scan(kmax[:], lift[:, 0], K[:], 0.0, ALU.add, ALU.max))
                    own.done(nc.vector.tensor_tensor_scan(kmin[:], lift[:, 1], K[:], 0.0, ALU.add, ALU.min))
                    dve.wait_ge(q_mm, n * 2 + 2)
                    own.done(nc.vector.tensor_tensor(Q[:], pa[:], bq_sb[:], ALU.add))
                    ins = nc.vector.tensor_scalar(Q[:], Q[:], C ** -0.5, None, ALU.mult)
                    ins.then_inc(q_out, 1)
                    dve.wait_ge(q_out, n + 1)
                    own.done(nc.vector.tensor_tensor(kmax[:], kmax[:], Q[:], ALU.mult))
                    own.done(nc.vector.tensor_tensor(kmin[:], kmin[:], Q[:], ALU.mult))
                    nc.vector.tensor_tensor(M[:], kmax[:], kmin[:], ALU.max).then_inc(max_ready, 1)
                    dve.wait_ge(v_mm, n * 2 + 2)
                    nc.vector.tensor_tensor(V[:], pa[:], bv_sb[:], ALU.add).then_inc(v_out, 1)
                    dve.wait_ge(v_out, n + 1)
                    Qh = Q[:].rearrange("p (h c) -> p h c", h=H)
                    Kh = K[:].rearrange("p (h c) -> p h c", h=H)
                    Vh = V[:].rearrange("p (h c) -> p h c", h=H)

                    def make_scores(g):
                        if g >= SB:
                            dve.wait_ge(den_used, n * NG + g - SB + 1)
                            dve.wait_ge(weighted, n * NG + g - SB + 1)
                        for j in groups[g]:
                            w = C - j
                            run = S[:, g % SB, place[j]:place[j] + H * w].rearrange("p (h w) -> p h w", h=H)
                            ins = nc.vector.tensor_tensor(run, Qh[:, :, j:C],
                                                          Kh[:, :, j:j + 1].broadcast_to([P, H, w]), ALU.mult)
                        ins.then_inc(scores, 1)

                    def weigh(g):
                        dve.wait_ge(probs, n * NG + g + 1)
                        if g >= TB:
                            dve.wait_ge(num_used, n * NG + g - TB + 1)
                        for j in groups[g]:
                            w = C - j
                            run = S[:, g % SB, place[j]:place[j] + H * w].rearrange("p (h w) -> p h w", h=H)
                            o = PV[:, g % TB, place[j]:place[j] + H * w].rearrange("p (h w) -> p h w", h=H)
                            ins = nc.vector.tensor_tensor(o, run, Vh[:, :, j:j + 1].broadcast_to([P, H, w]),
                                                          ALU.mult)
                        ins.then_inc(weighted, 1)

                    for g in range(NG + 2):
                        if g < NG:
                            make_scores(g)
                        if g >= 2:
                            weigh(g - 2)
                    dve.wait_ge(den_used, (n + 1) * NG)
                    own.done(nc.vector.reciprocal(rden[:], den[:]))
                    dve.wait_ge(num_used, (n + 1) * NG)
                    nc.vector.tensor_tensor(att[:], num[:], rden[:], ALU.mult).then_inc(att_ready, 1)
                    dve.wait_ge(y_mm, n + 1)
                    own.done(nc.vector.tensor_copy(res[:], pa[:, 512:512 + D]))
                    own.done(nc.vector.tensor_tensor(y[:], res[:], pa[:, 0:D], ALU.add))
                    ins = nc.vector.tensor_tensor(y[:], y[:], bo_sb[:], ALU.add)
                    ins.then_inc(y_ready, 1)
                    dve.wait_ge(y_ready, n + 1)
                    own.done(nc.vector.bn_stats(stats[:], y[:]))
                    nc.vector.memset(spare[:], 0.0)
                    nc.vector.bn_aggr(mv[:], stats[:]).then_inc(var_ready, 1)
                    dve.wait_ge(var_ready, n + 1)
                    dve.wait_ge(std_ready, n + 1)
                    own.done(nc.vector.reciprocal(rstd[:], std[:]))
                    dve.wait_ge(stored[u], 16 * i)
                    nc.vector.tensor_scalar(yn[:, u], y[:], mv[:, 0:1], rstd[:, 0:1], ALU.subtract, ALU.mult)\
                        .then_inc(yn_ready, 1)
                own.close()

        @block.tensor
        def _(pe):
            pe.wait_ge(weights_in, 16 * 8)
            pe.wait_ge(consts, 2)
            with pe.Fori(0, NI) as i:
                for u in range(U):
                    n = i * U + u
                    pe.wait_ge(x_in[u], 16 * (i + 1))
                    pe.wait_ge(attT_out, 2 * n)
                    pe.wait_ge(y_ready, n)

                    def project(w_sb, dst, done):
                        for half in range(2):
                            for c in range(DC):
                                ins = nc.tensor.matmul(dst[:, 512 * half:512 * half + 512], xT[:, u, c],
                                                       w_sb[:, c, 512 * half:512 * half + 512],
                                                       start=(c == 0), stop=(c == DC - 1))
                            ins.then_inc(done, 1)

                    project(wk_sb, pb, k_mm)
                    project(wq_sb, pa, q_mm)
                    pe.wait_ge(q_out, n + 1)
                    project(wv_sb, pa, v_mm)
                    for g, js in enumerate(groups):
                        for acc, buf, ready, used, gate in ((den, S, probs, den_used, g % SB),
                                                            (num, PV, weighted, num_used, g % TB)):
                            pe.wait_ge(ready, n * NG + g + 1)
                            if g == 0:
                                pe.wait_ge(att_ready, n)
                            for j in js:
                                w = C - j
                                for half in range(2):
                                    h0 = 8 * half
                                    o = acc[:].rearrange("p (h c) -> p h c", h=H)[:, h0:h0 + 8, j:C]
                                    r = buf[:, gate, place[j] + h0 * w:place[j] + (h0 + 8) * w]\
                                        .rearrange("p (h w) -> p h w", h=8)
                                    ins = nc.tensor.matmul(o, ident[:], r, start=(j == 0), stop=(j == C - 1),
                                                           skip_group_check=True)
                            ins.then_inc(used, 1)
                    pe.wait_ge(v_out, n + 1)
                    pe.wait_ge(att_ready, n + 1)
                    for c in range(HC):
                        ins = nc.tensor.transpose(pb[:, c * P:(c + 1) * P], att[:, c * P:(c + 1) * P], ident[:])
                        if c % 4 == 3:
                            ins.then_inc(attT_mm, 1)
                    for c in range(DC):
                        ins = nc.tensor.transpose(pa[:, 512 + c * P:512 + (c + 1) * P], xT[:, u, c], ident[:])
                    ins.then_inc(x_used, 1)
                    for c in range(HC):
                        if c % 4 == 0:
                            pe.wait_ge(attT_out, 2 * n + c // 4 + 1)
                        ins = nc.tensor.matmul(pa[:, 0:D], attT[:, c], wo_sb[:, c], start=(c == 0),
                                               stop=(c == HC - 1))
                    ins.then_inc(y_mm, 1)


RWKV_COLUMNS = ["ln1_w", "ln2_w", "x_maa", "w_maa", "k_maa", "v_maa", "r_maa", "g_maa", "time_decay",
                "time_first", "gn_w", "gn_b", "ck_maa", "cr_maa"]


class FeatureNorm:

    def __init__(self, sem, name, ones, eps, groups):
        self.ones, self.eps, self.groups = ones, eps, groups
        self.mean_mm = sem(f"{name}_mean_mm")
        self.centered = sem(f"{name}_centered")
        self.squared = sem(f"{name}_squared")
        self.var_mm = sem(f"{name}_var_mm")
        self.std_out = sem(f"{name}_std_out")
        self.inverted = sem(f"{name}_inverted")
        self.normed = sem(f"{name}_normed")

    def sums(self, nc, src, stat):
        for g in range(self.groups):
            cs = [g] if self.groups > 1 else list(range(DC))
            for half in range(stat.shape[2]):
                for k, c in enumerate(cs):
                    ins = nc.tensor.matmul(stat[:, g, half], self.ones, src[:, c, 512 * half:512 * half + 512],
                                           start=(k == 0), stop=(k == len(cs) - 1))
        return ins

    def pe_mean(self, nc, pe, n, src, stat):
        self.sums(nc, src, stat).then_inc(self.mean_mm, 1)

    def pe_var(self, nc, pe, n, sq, stat):
        pe.wait_ge(self.squared, n + 1)
        self.sums(nc, sq, stat).then_inc(self.var_mm, 1)

    def spread(self, stat):
        s = stat.rearrange("p g h t -> p g (h t)")
        return s if self.groups == DC else s.broadcast_to([P, DC, s.shape[2]])

    def dve_center(self, nc, dve, n, src, out, stat):
        dve.wait_ge(self.mean_mm, n + 1)
        nc.vector.tensor_tensor(out, src, self.spread(stat), ALU.subtract).then_inc(self.centered, 1)

    def act_square(self, nc, act, n, src, sq):
        act.wait_ge(self.centered, n + 1)
        nc.scalar.activation(sq, src, ACT.Square).then_inc(self.squared, 1)

    def act_std(self, nc, act, n, stat, std):
        act.wait_ge(self.var_mm, n + 1)
        nc.scalar.activation(std, stat.rearrange("p g h t -> p g (h t)"), ACT.Sqrt,
                             bias=self.eps).then_inc(self.std_out, 1)

    def dve_scale(self, nc, dve, n, buf, std, weight):
        dve.wait_ge(self.std_out, n + 1)
        nc.vector.reciprocal(std, std).then_inc(self.inverted, 1)
        dve.wait_ge(self.inverted, n + 1)
        if weight is None:
            s = std if self.groups == DC else std.broadcast_to([P, DC, std.shape[2]])
            ins = nc.vector.tensor_tensor(buf, buf, s, ALU.mult)
        else:
            for c in range(DC):
                ins = nc.vector.scalar_tensor_tensor(buf[:, c], buf[:, c], weight[:, c:c + 1],
                                                     std[:, c if self.groups == DC else 0], ALU.mult, ALU.mult)
        ins.then_inc(self.normed, 1)
        dve.wait_ge(self.normed, n + 1)


def rwkv(nc, x_fm, masks, p, work_fm):
    L = 2
    H, HS = 4, 64
    E, NMIX, ED = 32, 5, 64
    FK = 6
    CH = T // P
    LEVELS = [1, 2, 4, 8, 16, 32, 64]
    NL = len(LEVELS)
    CONSTS = 8
    PAIRS = CH // 2
    VEC_STEPS = 1 + 2 + NL + (CH - 1) + 1 + 1 + 2
    with ExitStack() as ctx:
        sb, psum, sem = allocators(nc, ctx, "tm")
        X = sb("X", [P, DC, T])
        XL = sb("XL", [P, DC, T + 1])
        SX = sb("SX", [P, DC, T])
        ZX = sb("ZX", [P, 2, DC, T])
        MX = sb("MX", [P, T])
        MX4 = sb("MX4", [E, T])
        TD = sb("TD", [ED, T])
        W = sb("W", [P, DC, 2 * T])
        RKO = sb("RKO", [P, 3, DC, T])
        R, K, OUT = RKO[:, 0], RKO[:, 1], RKO[:, 2]
        K2 = RKO[:].rearrange("p a c t -> p (a c) t")
        Vt = sb("Vt", [P, CH, D])
        G = sb("G", [P, DC, T])
        T1 = sb("T1", [P, DC, T])
        T2 = sb("T2", [P, DC, T])
        A = sb("A", [P, CH * DC, 2, P])
        ST = sb("ST", [P, CH, DC, P])
        ident = sb("ident", [P, P])
        ones = sb("ones", [P, P])
        gones = sb("gones", [P, P])
        eps = sb("eps", [P, 1])
        spare = sb("spare", [P, 64])
        mask_f = sb("masks", [P, NL + 1, P])
        mask_sb = mask_f[:].bitcast(mybir.dt.uint32)
        w = {k: sb(k, s) for k, s in dict(
            tm_w1=[P, DC, NMIX * E], tm_w2=[P, D], tm_w24=[E, D], td_w1=[P, DC, ED], td_w2=[ED, D],
            Wr=[P, DC, D], Wk=[P, DC, D], Wv=[P, DC, D], Wo=[P, DC, D], Wg=[P, DC, D],
            cWk=[P, DC, FK * P], cWv=[P, FK, D], cWr=[P, DC, D]).items()}
        cols = sb("cols", [P, len(RWKV_COLUMNS), DC])
        col = {k: cols[:, i] for i, k in enumerate(RWKV_COLUMNS)}
        ps = psum("ps", [P, 8, 512])

        weights_in = sem("weights_in")
        x_in = sem("x_in")
        start_copy = sem("start_copy")
        consts = sem("consts")
        consts_p = sem("consts_p")
        ln1 = FeatureNorm(sem, "ln1", ones[:], eps[:, 0:1], 1)
        ln2 = FeatureNorm(sem, "ln2", ones[:], eps[:, 0:1], 1)
        gn = FeatureNorm(sem, "gn", gones[:], eps[:, 0:1], DC)
        mixin_ready = sem("mixin_ready")
        mix_mm = sem("mix_mm")
        tanh_mix = sem("tanh_mix")
        delta_mm = sem("delta_mm")
        delta_used = sem("delta_used")
        zx_ready = sem("zx_ready")
        proj_mm = sem("proj_mm")
        proj_out = sem("proj_out")
        td_mm = sem("td_mm")
        td_out = sem("td_out")
        uk_ready = sem("uk_ready")
        lvl_ready = sem("lvl_ready")
        lvl_mm = sem("lvl_mm")
        lvl_kept = sem("lvl_kept")
        kT_mm = sem("kT_mm")
        kT_out = sem("kT_out")
        kv_mm = sem("kv_mm")
        state_ready = sem("state_ready")
        out_mm = sem("out_mm")
        out_copied = sem("out_copied")
        gated = sem("gated")
        wo_mm = sem("wo_mm")
        mid_ready = sem("mid_ready")
        ck_ready = sem("ck_ready")
        ck_mm = sem("ck_mm")
        ck_out = sem("ck_out")
        ck_sq = sem("ck_sq")
        cr_mm = sem("cr_mm")
        cr_out = sem("cr_out")
        cv_mm = sem("cv_mm")
        x_ready = sem("x_ready")
        stored = sem("stored")
        vec = sem("vec")
        act_s = sem("act_s")
        block = ctx.enter_context(nc.Block())

        x_v = work_fm.rearrange("(c p) (b t) -> b p c t", p=P, t=T)
        MAAS = ["w_maa", "k_maa", "v_maa", "r_maa", "g_maa"]
        stat0 = ps[:, 0:2].rearrange("p (g h) t -> p g h t", g=1)
        stat1 = ps[:, 2:4].rearrange("p (g h) t -> p g h t", g=1)
        low4 = ps[:, 0:4].rearrange("p (g h) t -> p g h t", g=DC)
        high4 = ps[:, 4:8].rearrange("p (g h) t -> p g h t", g=DC)
        flat = lambda a: a.rearrange("p g h t -> p g (h t)")
        base = [0]
        for m in LEVELS:
            base.append(base[-1] + T // m)

        @block.sync
        def _(sp):
            sp.dma_start(work_fm, x_fm).then_inc(start_copy, 16)
            sp.dma_start(mask_f[:], masks.rearrange("l p i -> p l i")).then_inc(start_copy, 16)
            sp.wait_ge(start_copy, 32)
            with sp.Fori(0, L) as l:
                sp.wait_ge(x_ready, l * B)
                for k in ("tm_w1", "td_w1", "Wr", "Wk", "Wv", "Wo", "Wg", "cWk", "cWv", "cWr"):
                    sp.dma_start(w[k][:], p[k][bass.ds(l, 1)].rearrange("o (c p) n -> p (o c) n", p=P))\
                        .then_inc(weights_in, 16)
                sp.dma_start(w["tm_w2"][:], p["tm_w2"][bass.ds(l, 1), 0:4].rearrange("o f e d -> (o f e) d"))\
                    .then_inc(weights_in, 16)
                sp.dma_start(w["tm_w24"][:], p["tm_w2"][bass.ds(l, 1), 4:5].rearrange("o f e d -> (o f e) d"))\
                    .then_inc(weights_in, 16)
                sp.dma_start(w["td_w2"][:], p["td_w2"][bass.ds(l, 1)].rearrange("o e d -> (o e) d"))\
                    .then_inc(weights_in, 16)
                sp.dma_start(cols[:], p["columns"][bass.ds(l, 1)].rearrange("o p k c -> (o p) k c"))\
                    .then_inc(weights_in, 16)
                with sp.Fori(0, B) as b:
                    n = l * B + b
                    sp.wait_ge(stored, n * 16)
                    sp.dma_start(X[:], x_v[bass.ds(b, 1)].rearrange("o p c t -> p (o c) t")).then_inc(x_in, 16)

        NW = 16 * 14

        @block.gpsimd
        def _(pool):
            pool.memset(ident[:], 0.0).then_inc(consts_p, 1)
            pool.wait_ge(consts_p, 1)
            pool.affine_select(out=ident[:], in_=ident[:], compare_op=ALU.not_equal, fill=1.0, base=0,
                               pattern=[[-1, P]], channel_multiplier=1).then_inc(consts_p, 1)

        @block.scalar
        def _(act):
            act.wait_ge(consts, CONSTS)
            with act.Fori(0, L) as l, act.Fori(0, B) as b:
                n = l * B + b
                own = Steps(act, act_s, DC, n)
                ln1.act_square(nc, act, n, XL[:, :, 1:T + 1], T1[:])
                ln1.act_std(nc, act, n, stat1, T2[:, 0:1])
                act.wait_ge(mix_mm, n + 1)
                nc.scalar.activation(MX[:], ps[:, 4:6].rearrange("p h t -> p (h t)"), ACT.Tanh)
                nc.scalar.activation(MX4[:], ps[0:E, 6:8].rearrange("p h t -> p (h t)"), ACT.Tanh)\
                    .then_inc(tanh_mix, 1)
                act.wait_ge(proj_mm, n * 5 + 1)
                nc.scalar.activation(TD[:], ps[0:ED, 0:2].rearrange("p h t -> p (h t)"), ACT.Tanh)\
                    .then_inc(proj_out, 1)
                act.wait_ge(td_mm, n + 1)
                for c in range(DC):
                    own.done(nc.scalar.activation(W[:, c, 0:T], flat(low4)[:, c], ACT.Exp,
                                                  bias=col["time_decay"][:, c:c + 1]))
                nc.scalar.activation(W[:, :, 0:T], W[:, :, 0:T], ACT.Exp, scale=-1.0).then_inc(td_out, 1)
                act.wait_ge(proj_mm, n * 5 + 2)
                nc.scalar.activation(K, flat(low4), ACT.Copy).then_inc(proj_out, 1)
                act.wait_ge(proj_mm, n * 5 + 3)
                nc.scalar.activation(Vt[:].rearrange("p j d -> p (j d)"), ps[:, 0:4].rearrange("p a b -> p (a b)"),
                                     ACT.Copy).then_inc(proj_out, 1)
                act.wait_ge(proj_mm, n * 5 + 4)
                nc.scalar.activation(R, flat(low4), ACT.Tanh, scale=0.5).then_inc(proj_out, 1)
                act.wait_ge(proj_mm, n * 5 + 5)
                nc.scalar.activation(T2[:], flat(low4), ACT.Tanh, scale=0.5)
                nc.scalar.activation(G[:], flat(low4), ACT.Copy).then_inc(proj_out, 1)
                act.wait_ge(kT_mm, n + 1)
                nc.scalar.activation(ZX[:, 0].rearrange("p c t -> p (c t)"), ps[:, 4:8].rearrange("p a b -> p (a b)"),
                                     ACT.Copy).then_inc(kT_out, 1)
                act.wait_ge(out_mm, n + 1)
                nc.scalar.activation(OUT, flat(low4), ACT.Copy).then_inc(out_copied, 1)
                gn.act_square(nc, act, n, OUT, T1[:])
                gn.act_std(nc, act, n, low4, T2[:])
                ln2.act_square(nc, act, n, XL[:, :, 1:T + 1], T1[:])
                ln2.act_std(nc, act, n, stat1, T2[:, 0:1])
                for k in range(2 * FK):
                    act.wait_ge(ck_mm, n * 2 * FK + k + 1)
                    nc.scalar.activation(K2[:, k // 2, 512 * (k % 2):512 * (k % 2) + 512], ps[:, 4 + k % 4], ACT.Relu)\
                        .then_inc(ck_out, 1)
                act.wait_ge(cr_mm, n + 1)
                nc.scalar.activation(T1[:], flat(low4), ACT.Tanh, scale=0.5).then_inc(cr_out, 1)
                act.wait_ge(x_ready, n + 1)
                act.dma_start(x_v[bass.ds(b, 1)].rearrange("o p c t -> p (o c) t"), X[:]).then_inc(stored, 16)
            act.wait_ge(stored, L * B * 16)

        @block.vector
        def _(dve):
            for k, ins in enumerate([
                    nc.vector.memset(eps[:], EPS), nc.vector.memset(ones[:], 1.0 / D),
                    nc.vector.memset(XL[:, :, 0:1], 0.0), nc.vector.memset(gones[:], 0.0),
                    nc.vector.memset(A[:], 0.0), nc.vector.memset(ST[:], 0.0)]):
                ins.then_inc(consts, 1)
            dve.wait_ge(consts, 6)
            nc.vector.memset(gones[0:HS, 0:HS], 1.0 / HS).then_inc(consts, 1)
            nc.vector.memset(gones[HS:P, HS:P], 1.0 / HS).then_inc(consts, 1)
            with dve.Fori(0, L) as l:
                with dve.Fori(0, B) as b:
                    n = l * B + b
                    dve.wait_ge(weights_in, (l + 1) * NW)
                    dve.wait_ge(x_in, (n + 1) * 16)
                    own = Steps(dve, vec, VEC_STEPS, n)
                    free_columns = iter(range(64))

                    def beat():
                        k = next(free_columns)
                        return nc.vector.memset(spare[:, k:k + 1], 0.0)

                    xl, prev = XL[:, :, 1:T + 1], XL[:, :, 0:T]

                    def mix_in(out, maa):
                        for c in range(DC):
                            ins = nc.vector.scalar_tensor_tensor(out[:, c], SX[:, c], col[maa][:, c:c + 1],
                                                                 xl[:, c], ALU.mult, ALU.add)
                        return ins

                    ln1.dve_center(nc, dve, n, X[:], xl, stat0)
                    ln1.dve_scale(nc, dve, n, xl, T2[:, 0:1], col["ln1_w"])
                    own.done(nc.vector.tensor_tensor(SX[:], prev, xl, ALU.subtract))
                    mix_in(ZX[:, 1], "x_maa").then_inc(mixin_ready, 1)
                    for f, maa in enumerate(MAAS):
                        z = ZX[:, f % 2]
                        dve.wait_ge(delta_mm, n * 5 + f + 1)
                        if f == 1:
                            dve.wait_ge(mix_mm, n + 1)
                        if f >= 2:
                            dve.wait_ge(proj_mm, n * 5 + f - 1)
                        for c in range(DC):
                            ins = nc.vector.scalar_tensor_tensor(z[:, c], flat(high4)[:, c], col[maa][:, c:c + 1],
                                                                 SX[:, c], ALU.add, ALU.mult)
                        ins.then_inc(delta_used, 1)
                        dve.wait_ge(delta_used, n * 5 + f + 1)
                        nc.vector.tensor_tensor(z, z, xl, ALU.add).then_inc(zx_ready, 1)
                    dve.wait_ge(proj_out, n * 5 + 5)
                    own.done(nc.vector.tensor_scalar(R, R, 0.5, 0.5, ALU.mult, ALU.add))
                    own.done(nc.vector.scalar_tensor_tensor(G[:], T2[:], 1.0, G[:], ALU.add, ALU.mult))
                    for c in range(DC):
                        ins = nc.vector.tensor_scalar(T1[:, c], K[:, c], col["time_first"][:, c:c + 1], None, ALU.mult)
                    ins.then_inc(uk_ready, 1)
                    dve.wait_ge(uk_ready, n + 1)

                    def keep(lv):
                        for j in range(CH):
                            g, a = j // 2, j % 2
                            if a == 0:
                                dve.wait_ge(lvl_mm, n * (NL + 1) * PAIRS + lv * PAIRS + g + 1)
                                beat()
                            nc.vector.copy_predicated(A[:, 4 * g:4 * g + 4, a],
                                                      mask_sb[:, lv:lv + 1].broadcast_to([P, 4, P]),
                                                      ps[:, j].rearrange("p (h i) -> p h i", h=4))\
                                .then_inc(lvl_kept, 1)

                    dve.wait_ge(td_out, n + 1)
                    for lv, m in enumerate(LEVELS):
                        keep(lv)
                        nb = T // (2 * m)
                        tw = W[:, :, base[lv]:base[lv + 1]].rearrange("p c (b s) -> p c b s", s=2)
                        dve.wait_ge(lvl_mm, n * (NL + 1) * PAIRS + (lv + 2) * PAIRS)
                        for c in range(DC):
                            second = R[:, c].rearrange("p (b s m) -> p b s m", s=2, m=m)[:, :, 1]
                            first = K[:, c].rearrange("p (b s m) -> p b s m", s=2, m=m)[:, :, 0]
                            nc.vector.tensor_tensor(second, second, tw[:, c, :, 0:1].broadcast_to([P, nb, m]), ALU.mult)
                            nc.vector.tensor_tensor(first, first, tw[:, c, :, 1:2].broadcast_to([P, nb, m]), ALU.mult)
                        own.done(nc.vector.tensor_tensor(W[:, :, base[lv + 1]:base[lv + 1] + nb], tw[:, :, :, 0],
                                                         tw[:, :, :, 1], ALU.mult))
                        beat().then_inc(lvl_ready, 1)
                    keep(NL)
                    dve.wait_ge(kv_mm, n + 1)
                    for j in range(CH - 1):
                        for c in range(DC):
                            for a in range(2):
                                r0, r1 = HS * a, HS * a + HS
                                ins = nc.vector.scalar_tensor_tensor(
                                    ST[r0:r1, j + 1, c, r0:r1], ST[r0:r1, j, c, r0:r1],
                                    W[r0:r1, c, base[NL] + j:base[NL] + j + 1],
                                    ps[r0:r1, (2 * j + c) // 4, P * ((2 * j + c) % 4) + r0:P * ((2 * j + c) % 4) + r1],
                                    ALU.mult, ALU.add)
                        own.done(ins)
                    beat().then_inc(state_ready, 1)
                    dve.wait_ge(out_copied, n + 1)
                    gn.dve_center(nc, dve, n, OUT, OUT, high4)
                    gn.dve_scale(nc, dve, n, OUT, T2[:], col["gn_w"])
                    own.done(nc.vector.tensor_scalar(G[:], G[:], 0.5, None, ALU.mult))
                    for c in range(DC):
                        ins = nc.vector.scalar_tensor_tensor(OUT[:, c], OUT[:, c], col["gn_b"][:, c:c + 1], G[:, c],
                                                             ALU.add, ALU.mult)
                    ins.then_inc(gated, 1)
                    dve.wait_ge(wo_mm, n + 1)
                    nc.vector.tensor_tensor(X[:], X[:], flat(high4), ALU.add).then_inc(mid_ready, 1)
                    dve.wait_ge(mid_ready, n + 1)
                    ln2.dve_center(nc, dve, n, X[:], xl, stat0)
                    ln2.dve_scale(nc, dve, n, xl, T2[:, 0:1], col["ln2_w"])
                    own.done(nc.vector.tensor_tensor(SX[:], prev, xl, ALU.subtract))
                    mix_in(ZX[:, 0], "ck_maa")
                    mix_in(ZX[:, 1], "cr_maa").then_inc(ck_ready, 1)
                    for k in range(2 * FK):
                        dve.wait_ge(ck_out, n * 2 * FK + k + 1)
                        kk = K2[:, k // 2, 512 * (k % 2):512 * (k % 2) + 512]
                        nc.vector.tensor_tensor(kk, kk, kk, ALU.mult).then_inc(ck_sq, 1)
                    dve.wait_ge(cr_out, n + 1)
                    own.done(nc.vector.tensor_scalar(T1[:], T1[:], 0.5, 0.5, ALU.mult, ALU.add))
                    dve.wait_ge(cv_mm, n + 1)
                    own.done(nc.vector.tensor_tensor(T1[:], T1[:], flat(high4), ALU.mult))
                    nc.vector.tensor_tensor(X[:], X[:], T1[:], ALU.add).then_inc(x_ready, 1)
                    own.close()

        @block.tensor
        def _(pe):
            pe.wait_ge(consts, CONSTS)
            pe.wait_ge(consts_p, 2)
            with pe.Fori(0, L) as l:
                with pe.Fori(0, B) as b:
                    n = l * B + b
                    pe.wait_ge(weights_in, (l + 1) * NW)

                    def linear(dst, wt, src, rows=P, kc=DC):
                        for m in range((wt.shape[2] + P - 1) // P):
                            for half in range(2):
                                for c in range(kc):
                                    ins = nc.tensor.matmul(dst[0:rows, m, half], wt[:, c, m * P:m * P + rows],
                                                           src[:, c, 512 * half:512 * half + 512],
                                                           start=(c == 0), stop=(c == kc - 1))
                        return ins

                    pe.wait_ge(x_in, (n + 1) * 16)
                    ln1.pe_mean(nc, pe, n, X, stat0)
                    ln1.pe_var(nc, pe, n, T1, stat1)
                    pe.wait_ge(mixin_ready, n + 1)
                    pe.wait_ge(x_ready, n)
                    for half in range(2):
                        for c in range(DC):
                            nc.tensor.matmul(ps[:, 4 + half], w["tm_w1"][:, c, 0:P],
                                             ZX[:, 1, c, 512 * half:512 * half + 512], start=(c == 0), stop=(c == DC - 1))
                        for c in range(DC):
                            ins = nc.tensor.matmul(ps[0:E, 6 + half], w["tm_w1"][:, c, P:P + E],
                                                   ZX[:, 1, c, 512 * half:512 * half + 512],
                                                   start=(c == 0), stop=(c == DC - 1))
                    ins.then_inc(mix_mm, 1)

                    def delta(f):
                        if f == 0:
                            pe.wait_ge(tanh_mix, n + 1)
                        else:
                            pe.wait_ge(delta_used, n * 5 + f)
                        for c in range(DC):
                            for half in range(2):
                                t0, t1 = 512 * half, 512 * half + 512
                                if f < 4:
                                    lt, rt = w["tm_w2"][E * f:E * f + E, c * P:(c + 1) * P], MX[E * f:E * f + E, t0:t1]
                                    tp = (E * f, 0)
                                else:
                                    lt, rt = w["tm_w24"][:, c * P:(c + 1) * P], MX4[:, t0:t1]
                                    tp = (0, 0)
                                ins = nc.tensor.matmul(ps[:, 4 + 2 * c + half], lt, rt, start=True, stop=True,
                                                       tile_position=tp)
                        ins.then_inc(delta_mm, 1)

                    def project(f):
                        pe.wait_ge(zx_ready, n * 5 + f + 1)
                        z = ZX[:, f % 2]
                        if f == 0:
                            linear(low4, w["td_w1"], z, rows=ED).then_inc(proj_mm, 1)
                            pe.wait_ge(proj_out, n * 5 + 1)
                            for m in range(DC):
                                for half in range(2):
                                    ins = nc.tensor.matmul(low4[:, m, half], w["td_w2"][:, m * P:(m + 1) * P],
                                                           TD[:, 512 * half:512 * half + 512], start=True, stop=True)
                            ins.then_inc(td_mm, 1)
                            return
                        if f == 1:
                            pe.wait_ge(td_out, n + 1)
                        else:
                            pe.wait_ge(proj_out, n * 5 + f)
                        if f == 2:
                            for j in range(CH):
                                for c in range(DC):
                                    ins = nc.tensor.matmul(ps[:, j // 2, D * (j % 2):D * (j % 2) + D],
                                                           z[:, c, j * P:(j + 1) * P], w["Wv"][:, c],
                                                           start=(c == 0), stop=(c == DC - 1))
                            ins.then_inc(proj_mm, 1)
                            return
                        linear(low4, w[[None, "Wk", None, "Wr", "Wg"][f]], z).then_inc(proj_mm, 1)

                    delta(0)
                    delta(1)
                    project(0)
                    for f in range(2, 5):
                        delta(f)
                        project(f - 1)
                    project(4)
                    pe.wait_ge(proj_out, n * 5 + 5)
                    pe.wait_ge(uk_ready, n + 1)
                    pe.wait_ge(delta_used, n * 5 + 5)
                    for lv in range(NL + 1):
                        keys = T1 if lv == 0 else K
                        if lv >= 2:
                            pe.wait_ge(lvl_ready, n * NL + lv - 1)
                        for g in range(PAIRS):
                            if lv >= 1:
                                pe.wait_ge(lvl_kept, n * (NL + 1) * CH + (lv - 1) * CH + 2 * g + 2)
                            for k in range(4):
                                j, c = 2 * g + k // 2, k % 2
                                for a in range(2):
                                    ins = nc.tensor.matmul(ps[:, 2 * g + a, k * P:(k + 1) * P],
                                                           keys[HS * a:HS * a + HS, c, j * P:(j + 1) * P],
                                                           R[HS * a:HS * a + HS, c, j * P:(j + 1) * P],
                                                           start=True, stop=True)
                            ins.then_inc(lvl_mm, 1)
                    pe.wait_ge(lvl_ready, n * NL + NL)
                    pe.wait_ge(lvl_kept, (n + 1) * (NL + 1) * CH)
                    for j in range(CH):
                        for c in range(DC):
                            k = 2 * j + c
                            ins = nc.tensor.transpose(ps[:, 4 + k // 4, P * (k % 4):P * (k % 4) + P],
                                                      K[:, c, j * P:(j + 1) * P], ident[:])
                    ins.then_inc(kT_mm, 1)
                    pe.wait_ge(kT_out, n + 1)
                    kt = ZX[:, 0].rearrange("p c t -> p (c t)").rearrange("p (j d) -> p j d", j=CH)
                    for j in range(CH):
                        for c in range(DC):
                            k = 2 * j + c
                            ins = nc.tensor.matmul(ps[:, k // 4, P * (k % 4):P * (k % 4) + P],
                                                   kt[:, j, c * P:(c + 1) * P], Vt[:, j, c * P:(c + 1) * P],
                                                   start=True, stop=True)
                    ins.then_inc(kv_mm, 1)
                    pe.wait_ge(state_ready, n + 1)
                    for c in range(DC):
                        for j in range(CH):
                            o = low4[:, c, j // 4, P * (j % 4):P * (j % 4) + P]
                            nc.tensor.matmul(o, ST[:, j, c], R[:, c, j * P:(j + 1) * P], start=True, stop=False,
                                             skip_group_check=True)
                            for a in range(2):
                                ins = nc.tensor.matmul(o[HS * a:HS * a + HS], Vt[:, j, c * P + HS * a:c * P + HS * a + HS],
                                                       A[:, 2 * j + c, a], start=False, stop=True,
                                                       tile_position=(0, HS * a), skip_group_check=True)
                    ins.then_inc(out_mm, 1)
                    pe.wait_ge(out_copied, n + 1)
                    gn.pe_mean(nc, pe, n, OUT, high4)
                    gn.pe_var(nc, pe, n, T1, low4)
                    pe.wait_ge(gated, n + 1)
                    linear(high4, w["Wo"], OUT).then_inc(wo_mm, 1)
                    pe.wait_ge(mid_ready, n + 1)
                    ln2.pe_mean(nc, pe, n, X, stat0)
                    ln2.pe_var(nc, pe, n, T1, stat1)
                    pe.wait_ge(ck_ready, n + 1)
                    for k in range(2 * FK):
                        if k >= 4:
                            pe.wait_ge(ck_out, n * 2 * FK + k - 3)
                        for c in range(DC):
                            ins = nc.tensor.matmul(ps[:, 4 + k % 4], w["cWk"][:, c, P * (k // 2):P * (k // 2) + P],
                                                   ZX[:, 0, c, 512 * (k % 2):512 * (k % 2) + 512],
                                                   start=(c == 0), stop=(c == DC - 1))
                        ins.then_inc(ck_mm, 1)
                    linear(low4, w["cWr"], ZX[:, 1]).then_inc(cr_mm, 1)
                    pe.wait_ge(ck_sq, (n + 1) * 2 * FK)
                    linear(high4, w["cWv"], K2, kc=FK).then_inc(cv_mm, 1)


MOE_COLUMNS = ["ln_out_w", "ln1_g", "ln1_b", "ln2_g", "ln2_b", "bo"]


def attention_moe(nc, x_fm, rwkv_fm, p, out_fm):
    NH, SLOT = 16, 32
    HD = D // NH
    G4 = NH // 4
    QT = T // P
    NE, FE = 8, 1024
    FM = FE // P
    SCALE = HD ** -0.5
    UNITS = FM * 2
    MIDS = 8
    CONSTS = 2 + NE
    VEC_STEPS = 1 + 2 * G4 + 6
    with ExitStack() as ctx:
        sb, psum, sem = allocators(nc, ctx, "mo")
        XA = sb("XA", [P, DC, T])
        XB = sb("XB", [P, DC, T])
        HN = sb("HN", [P, DC, T])
        T1 = sb("T1", [P, DC, T])
        std = sb("std", [P, 1, T])
        QP = sb("QP", [P, G4, T])
        KP = sb("KP", [P, G4, T])
        VP = sb("VP", [P, QT, NH * SLOT])
        PT = sb("PT", [P, 3, 2, 512])
        mx = sb("mx", [P, QT, 2, NH])
        MB = sb("MB", [P, QT, NH * SLOT])
        MK = MB[:].rearrange("p a b -> p (a b)").bitcast(BF16).rearrange("p (e t) -> p e t", e=NE)
        OP = sb("OP", [P, G4, T])
        MID = QP[:].rearrange("p g (a t) -> p (g a) t", t=512)
        wq = sb("wq", [P, DC, NH * SLOT])
        wk = sb("wk", [P, DC, NH * SLOT])
        wv = sb("wv", [P, DC, NH * SLOT])
        wo = sb("wo", [P, G4, D])
        gw = sb("gw", [P, DC, NE])
        gb = sb("gb", [P, NE])
        bq = sb("bq", [P, G4])
        bk = sb("bk", [P, G4])
        bv = sb("bv", [P, NH * SLOT])
        mark_col = sb("mark_col", [P, G4])
        mark_row = sb("mark_row", [P, NH * SLOT])
        cols = sb("cols", [P, len(MOE_COLUMNS), DC])
        col = {k: cols[:, i] for i, k in enumerate(MOE_COLUMNS)}
        b2 = sb("b2", [NE, D])
        w1 = sb("w1", [P, 2, DC, FE])
        w2 = sb("w2", [P, 2, FM, D])
        b1 = sb("b1", [P, 2, FM])
        LG = sb("LG", [P, QT, NE])
        OH = sb("OH", [P, QT, NE])
        OHB = sb("OHB", [P, QT, NE], BF16)
        OHT = sb("OHT", [NE, T])
        top = sb("top", [P, QT])
        order = sb("order", [P, NE])
        ident = sb("ident", [P, P])
        identb = sb("identb", [P, P], BF16)
        sel = sb("sel", [P, P])
        ones = sb("ones", [P, P])
        eps = sb("eps", [P, 1])
        ps = psum("ps", [P, 8, 512])

        const_in = sem("const_in")
        consts = sem("consts")
        consts_p = sem("consts_p")
        bias_set = sem("bias_set")
        x_in = sem("x_in")
        N_ = lambda k: FeatureNorm(sem, k, ones[:], eps[:, 0:1], 1)
        ln_out, ln_join, ln1, ln2, ln_end = N_("out"), N_("join"), N_("ln1"), N_("ln2"), N_("end")
        summed = sem("summed")
        hn_ready = sem("hn_ready")
        qk_mm = sem("qk_mm")
        qk_out = sem("qk_out")
        v_mm = sem("v_mm")
        v_out = sem("v_out")
        s_mm = sem("s_mm")
        s_max = sem("s_max")
        mb_ready = sem("mb_ready")
        mt_mm = sem("mt_mm")
        q_ready = sem("q_ready")
        st_mm = sem("st_mm")
        probs = sem("probs")
        pv_mm = sem("pv_mm")
        o_out = sem("o_out")
        den_mm = sem("den_mm")
        o_normed = sem("o_normed")
        wo_mm = sem("wo_mm")
        xb_ready = sem("xb_ready")
        hn2_ready = sem("hn2_ready")
        lg_mm = sem("lg_mm")
        oh_ready = sem("oh_ready")
        oht_mm = sem("oht_mm")
        oht_out = sem("oht_out")
        mk_mm = sem("mk_mm")
        mk_out = sem("mk_out")
        w_in = [sem("w_in0"), sem("w_in1")]
        mid_mm = sem("mid_mm")
        relu_out = sem("relu_out")
        mid_ready = sem("mid_ready")
        exp_u = [sem("exp_u0"), sem("exp_u1")]
        total_ready = sem("total_ready")
        stored = sem("stored")
        vec = sem("vec")
        block = ctx.enter_context(nc.Block())

        fm = lambda a: a.rearrange("(c p) (b t) -> b p c t", p=P, t=T)
        x_v, r_v, o_v = fm(x_fm), fm(rwkv_fm), fm(out_fm)
        seq = lambda v, b: v[bass.ds(b, 1)].rearrange("o p c t -> p (o c) t")
        stat0 = ps[:, 0:2].rearrange("p (g h) t -> p g h t", g=1)
        stat1 = ps[:, 2:4].rearrange("p (g h) t -> p g h t", g=1)
        low4 = ps[:, 0:4].rearrange("p (g h) t -> p g h t", g=DC)
        flat = lambda a: a.rearrange("p g h t -> p g (h t)")
        AU = [(g, qh, kt, hp) for g in range(G4) for qh in range(2) for kt in range(QT) for hp in range(2)]
        NAU = len(AU)
        NCONST = 16 * 13

        @block.sync
        def _(sp):
            rows = lambda a: a.rearrange("(c p) n -> p c n", p=P)
            wide = lambda a: a.rearrange("(a n) -> a n", a=1).broadcast_to([P, a.shape[0]])
            for dst, src in ((wq, rows(p["wq"])), (wk, rows(p["wk"])), (wv, rows(p["wv"])), (wo, rows(p["wo"])),
                             (gw, rows(p["gate_w"])), (gb, wide(p["gate_b"])), (bq, p["bq_col"]), (bk, p["bk_col"]),
                             (bv, wide(p["bv"])), (mark_col, p["mark_col"]), (mark_row, wide(p["mark_row"])),
                             (cols, p["moe_columns"]), (b2, p["b2"])):
                sp.dma_start(dst[:], src).then_inc(const_in, 16)
            with sp.Fori(0, B) as b:
                sp.wait_ge(stored, b * 16)
                sp.dma_start(XA[:], seq(x_v, b)).then_inc(x_in, 16)
                sp.dma_start(XB[:], seq(r_v, b)).then_inc(x_in, 16)
                with sp.Fori(0, NE // 2) as e2:
                    for u in range(2):
                        ne = b * NE + e2 * 2 + u
                        sp.wait_ge(exp_u[u], (b * (NE // 2) + e2) * UNITS)
                        e = e2 * 2 + u
                        sp.dma_start(w1[:, u], p["w1"][bass.ds(e, 1)].rearrange("o (c p) f -> p (o c) f", p=P))\
                            .then_inc(w_in[u], 16)
                        sp.dma_start(w2[:, u], p["w2"][bass.ds(e, 1)].rearrange("o (c p) f -> p (o c) f", p=P))\
                            .then_inc(w_in[u], 16)
                        sp.dma_start(b1[:, u], p["b1_col"][bass.ds(e, 1)].rearrange("o p f -> (o p) f"))\
                            .then_inc(w_in[u], 16)

        @block.gpsimd
        def _(pool):
            pool.memset(ident[:], 0.0).then_inc(consts_p, 1)
            pool.memset(sel[:], 0.0).then_inc(consts_p, 1)
            pool.wait_ge(consts_p, 2)
            pool.affine_select(out=ident[:], in_=ident[:], compare_op=ALU.not_equal, fill=1.0, base=0,
                               pattern=[[-1, P]], channel_multiplier=1).then_inc(consts_p, 1)
            pool.affine_select(out=sel[:].rearrange("p (j r) -> p j r", r=SLOT),
                               in_=sel[:].rearrange("p (j r) -> p j r", r=SLOT), compare_op=ALU.not_equal,
                               fill=1.0, base=-HD, pattern=[[-SLOT, 4], [0, SLOT]], channel_multiplier=1)\
                .then_inc(consts_p, 1)
            pool.wait_ge(consts_p, 4)
            pool.tensor_copy(identb[:], ident[:]).then_inc(consts_p, 1)

        @block.scalar
        def _(act):
            act.wait_ge(consts, CONSTS)
            act.wait_ge(bias_set, 3)
            with act.Fori(0, B) as b:
                ln_out.act_square(nc, act, b, HN[:], T1[:])
                ln_out.act_std(nc, act, b, stat1, std[:])
                ln_join.act_square(nc, act, b, XA[:], T1[:])
                ln_join.act_std(nc, act, b, stat1, std[:])
                ln1.act_square(nc, act, b, HN[:], T1[:])
                ln1.act_std(nc, act, b, stat1, std[:])
                for k in range(4 * G4):
                    dst, bias = (QP, bq) if k < 2 * G4 else (KP, bk)
                    g, half = (k // 2) % G4, k % 2
                    act.wait_ge(qk_mm, b * 4 * G4 + k + 1)
                    nc.scalar.activation(dst[:, g, 512 * half:512 * half + 512], ps[:, k % 4], ACT.Identity,
                                         bias=bias[:, g:g + 1]).then_inc(qk_out, 1)
                for k, (g, qh, kt, hp) in enumerate(AU):
                    act.wait_ge(st_mm, b * NAU + k + 1)
                    if k >= 3:
                        act.wait_ge(pv_mm, b * NAU + k - 2)
                    nc.scalar.activation(PT[:, k % 3], ps[:, 2 * (k % 3):2 * (k % 3) + 2], ACT.Exp, scale=SCALE)\
                        .then_inc(probs, 1)
                ln2.act_square(nc, act, b, HN[:], T1[:])
                ln2.act_std(nc, act, b, stat1, std[:])
                act.wait_ge(oht_mm, b + 1)
                nc.scalar.activation(OHT[:], ps[0:NE, 0:2].rearrange("p h t -> p (h t)"), ACT.Copy).then_inc(oht_out, 1)
                for e in range(NE):
                    act.wait_ge(mk_mm, b * NE + e + 1)
                    k = 2 * (e % 2) + 4
                    nc.scalar.activation(MK[:, e], ps[:, k:k + 2].rearrange("p h t -> p (h t)"), ACT.Copy)\
                        .then_inc(mk_out, 1)
                with act.Fori(0, NE // 2) as e2:
                    for u in range(2):
                        ne = b * NE + e2 * 2 + u
                        act.wait_ge(w_in[u], (b * (NE // 2) + e2 + 1) * 48)
                        for k in range(UNITS):
                            act.wait_ge(mid_mm, ne * UNITS + k + 1)
                            nb = b * (NE // 2) + e2
                            if k >= MIDS:
                                act.wait_ge(exp_u[u], nb * UNITS + k - MIDS + 1)
                            elif u == 1:
                                act.wait_ge(exp_u[0], nb * UNITS + k + UNITS - MIDS + 1)
                            else:
                                act.wait_ge(exp_u[1], nb * UNITS)
                            nc.scalar.activation(MID[:, k % MIDS], ps[:, 4 + k % 4], ACT.Relu,
                                                 bias=b1[:, u, k // 2:k // 2 + 1]).then_inc(relu_out, 1)
                ln_end.act_square(nc, act, b, HN[:], T1[:])
                ln_end.act_std(nc, act, b, stat1, std[:])
                act.wait_ge(ln_end.normed, b + 1)
                act.dma_start(seq(o_v, b), HN[:]).then_inc(stored, 16)
            act.wait_ge(stored, B * 16)

        @block.vector
        def _(dve):
            for ins in (nc.vector.memset(eps[:], EPS), nc.vector.memset(ones[:], 1.0 / D)):
                ins.then_inc(consts, 1)
            for e in range(NE):
                nc.vector.memset(order[:, e:e + 1], float(NE - e)).then_inc(consts, 1)
            dve.wait_ge(const_in, NCONST)
            nc.vector.tensor_tensor(bk[:], bk[:], mark_col[:], ALU.add).then_inc(bias_set, 1)
            nc.vector.tensor_tensor(bv[:], bv[:], mark_row[:], ALU.add).then_inc(bias_set, 1)
            nc.vector.tensor_copy(bq[:], bq[:]).then_inc(bias_set, 1)
            dve.wait_ge(bias_set, 3)
            with dve.Fori(0, B) as b:
                own = Steps(dve, vec, VEC_STEPS, b)
                dve.wait_ge(x_in, (b + 1) * 32)
                ln_out.dve_center(nc, dve, b, XB[:], HN[:], stat0)
                ln_out.dve_scale(nc, dve, b, HN[:], std[:], col["ln_out_w"])
                nc.vector.tensor_tensor(XA[:], XA[:], HN[:], ALU.add).then_inc(summed, 1)
                dve.wait_ge(summed, 3 * b + 1)
                ln_join.dve_center(nc, dve, b, XA[:], XA[:], stat0)
                ln_join.dve_scale(nc, dve, b, XA[:], std[:], None)
                ln1.dve_center(nc, dve, b, XA[:], HN[:], stat0)
                ln1.dve_scale(nc, dve, b, HN[:], std[:], col["ln1_g"])
                for c in range(DC):
                    ins = nc.vector.tensor_scalar(HN[:, c], HN[:, c], col["ln1_b"][:, c:c + 1], None, ALU.add)
                ins.then_inc(hn_ready, 1)
                dve.wait_ge(mid_ready, b * NE * UNITS)
                own.done(nc.vector.memset(MB[:], 0.0))
                for j in range(QT):
                    dve.wait_ge(v_mm, b * QT + j + 1)
                    nc.vector.tensor_tensor(VP[:, j], ps[:, 4 + j % 4], bv[:], ALU.add).then_inc(v_out, 1)
                for k in range(G4 * QT * 2):
                    g, qt, kh = k // (2 * QT), (k // 2) % QT, k % 2
                    dve.wait_ge(s_mm, b * G4 * QT * 2 + k + 1)
                    k0 = 4 * (k % 2)
                    nc.vector.tensor_reduce(mx[:, qt, kh, 4 * g:4 * g + 4], ps[:, k0:k0 + 4], AX.X, ALU.max)\
                        .then_inc(s_max, 1)
                dve.wait_ge(s_max, (b + 1) * G4 * QT * 2)
                marked = MB[:].rearrange("p q (h r) -> p q h r", r=SLOT)[:, :, :, HD]
                nc.vector.tensor_tensor(marked, mx[:, :, 0], mx[:, :, 1], ALU.max).then_inc(mb_ready, 1)
                for g in range(G4):
                    dve.wait_ge(mt_mm, b * G4 + g + 1)
                    q0 = 2 * (g % 2)
                    nc.vector.tensor_tensor(QP[:, g], QP[:, g], ps[:, q0:q0 + 2].rearrange("p a t -> p (a t)"),
                                            ALU.subtract).then_inc(q_ready, 1)
                for k in range(G4 * 2):
                    dve.wait_ge(pv_mm, b * NAU + (k + 1) * NAU // (2 * G4))
                    nc.vector.tensor_copy(OP[:, k // 2, 512 * (k % 2):512 * (k % 2) + 512], ps[:, 6 + k % 2])\
                        .then_inc(o_out, 1)
                for k in range(G4 * 2):
                    dve.wait_ge(den_mm, b * G4 * 2 + k + 1)
                    inv = T1[:, 0, 512 * (k % 2):512 * (k % 2) + 512]
                    own.done(nc.vector.reciprocal(inv, ps[:, k % 4]))
                    o = OP[:, k // 2, 512 * (k % 2):512 * (k % 2) + 512]
                    nc.vector.tensor_tensor(o, o, inv, ALU.mult).then_inc(o_normed, 1)
                dve.wait_ge(wo_mm, b + 1)
                for c in range(DC):
                    ins = nc.vector.scalar_tensor_tensor(XB[:, c], flat(low4)[:, c], col["bo"][:, c:c + 1], XA[:, c],
                                                         ALU.add, ALU.add)
                ins.then_inc(xb_ready, 1)
                dve.wait_ge(xb_ready, b + 1)
                ln2.dve_center(nc, dve, b, XB[:], HN[:], stat0)
                ln2.dve_scale(nc, dve, b, HN[:], std[:], col["ln2_g"])
                for c in range(DC):
                    ins = nc.vector.tensor_scalar(HN[:, c], HN[:, c], col["ln2_b"][:, c:c + 1], None, ALU.add)
                ins.then_inc(hn2_ready, 1)
                nc.vector.tensor_tensor(XB[:], XB[:], XA[:], ALU.add).then_inc(summed, 1)
                dve.wait_ge(lg_mm, b + 1)
                lg = ps[:, 0, 0:QT * NE].rearrange("p (q e) -> p q e", e=NE)
                own.done(nc.vector.tensor_tensor(LG[:], lg, gb[:].rearrange("p (o e) -> p o e", o=1)
                                                 .broadcast_to([P, QT, NE]), ALU.add))
                wide = lambda t: t[:].rearrange("p (q o) -> p q o", o=1).broadcast_to([P, QT, NE])
                own.done(nc.vector.tensor_reduce(top[:], LG[:], AX.X, ALU.max))
                own.done(nc.vector.tensor_tensor(OH[:], LG[:], wide(top), ALU.is_ge))
                own.done(nc.vector.tensor_tensor(LG[:], OH[:], order[:].rearrange("p (o e) -> p o e", o=1)
                                                 .broadcast_to([P, QT, NE]), ALU.mult))
                own.done(nc.vector.tensor_reduce(top[:], LG[:], AX.X, ALU.max))
                own.done(nc.vector.tensor_tensor(OH[:], LG[:], wide(top), ALU.is_equal))
                nc.vector.tensor_copy(OHB[:], OH[:]).then_inc(oh_ready, 1)
                with dve.Fori(0, NE // 2) as e2:
                    for u in range(2):
                        ne = b * NE + e2 * 2 + u
                        dve.wait_ge(mk_out, (b + 1) * NE)
                        for k in range(UNITS):
                            dve.wait_ge(relu_out, ne * UNITS + k + 1)
                            m = MID[:, k % MIDS]
                            mask = MK[:, bass.ds(e2 * 2 + u, 1), 512 * (k % 2):512 * (k % 2) + 512]\
                                .rearrange("p o t -> p (o t)")
                            nc.vector.tensor_tensor(m, m, mask, ALU.mult).then_inc(mid_ready, 1)
                dve.wait_ge(exp_u[1], (b + 1) * (NE // 2) * UNITS)
                dve.wait_ge(summed, 3 * b + 2)
                nc.vector.tensor_tensor(XB[:], XB[:], flat(low4), ALU.add).then_inc(summed, 1)
                dve.wait_ge(summed, 3 * b + 3)
                ln_end.dve_center(nc, dve, b, XB[:], HN[:], stat0)
                ln_end.dve_scale(nc, dve, b, HN[:], std[:], None)
                own.close()

        @block.tensor
        def _(pe):
            pe.wait_ge(consts, CONSTS)
            pe.wait_ge(consts_p, 5)
            pe.wait_ge(bias_set, 3)
            with pe.Fori(0, B) as b:
                pe.wait_ge(x_in, (b + 1) * 32)
                ln_out.pe_mean(nc, pe, b, XB, stat0)
                ln_out.pe_var(nc, pe, b, T1, stat1)
                pe.wait_ge(summed, 3 * b + 1)
                ln_join.pe_mean(nc, pe, b, XA, stat0)
                ln_join.pe_var(nc, pe, b, T1, stat1)
                pe.wait_ge(ln_join.normed, b + 1)
                ln1.pe_mean(nc, pe, b, XA, stat0)
                ln1.pe_var(nc, pe, b, T1, stat1)
                pe.wait_ge(hn_ready, b + 1)
                for k in range(4 * G4):
                    w = wq if k < 2 * G4 else wk
                    g, half = (k // 2) % G4, k % 2
                    if k >= 4:
                        pe.wait_ge(qk_out, b * 4 * G4 + k - 3)
                    for c in range(DC):
                        ins = nc.tensor.matmul(ps[:, k % 4], w[:, c, g * P:(g + 1) * P],
                                               HN[:, c, 512 * half:512 * half + 512],
                                               start=(c == 0), stop=(c == DC - 1))
                    ins.then_inc(qk_mm, 1)
                for j in range(QT):
                    if j >= 4:
                        pe.wait_ge(v_out, b * QT + j - 3)
                    for c in range(DC):
                        ins = nc.tensor.matmul(ps[:, 4 + j % 4], HN[:, c, j * P:(j + 1) * P], wv[:, c],
                                               start=(c == 0), stop=(c == DC - 1))
                    ins.then_inc(v_mm, 1)
                pe.wait_ge(qk_out, (b + 1) * 4 * G4)
                pe.wait_ge(v_out, (b + 1) * QT)
                for k in range(G4 * QT * 2):
                    g, qt, kh = k // (2 * QT), (k // 2) % QT, k % 2
                    if k >= 2:
                        pe.wait_ge(s_max, b * G4 * QT * 2 + k - 1)
                    for j in range(4):
                        r0 = SLOT * j
                        ins = nc.tensor.matmul(ps[:, 4 * (k % 2) + j], QP[r0:r0 + SLOT, g, qt * P:(qt + 1) * P],
                                               KP[r0:r0 + SLOT, g, 512 * kh:512 * kh + 512], start=True, stop=True,
                                               tile_position=(r0, 0))
                    ins.then_inc(s_mm, 1)
                pe.wait_ge(mb_ready, b + 1)
                for g in range(G4):
                    if g >= 2:
                        pe.wait_ge(q_ready, b * G4 + g - 1)
                    for qt in range(QT):
                        ins = nc.tensor.transpose(ps[:, 2 * (g % 2) + qt // 4, P * (qt % 4):P * (qt % 4) + P],
                                                  MB[:, qt, g * P:(g + 1) * P], ident[:])
                    ins.then_inc(mt_mm, 1)
                pe.wait_ge(q_ready, (b + 1) * G4)

                def transposed_scores(k):
                    g, qh, kt, hp = AU[k]
                    if k >= 3:
                        pe.wait_ge(probs, b * NAU + k - 2)
                    for a in range(2):
                        r0 = SLOT * (2 * hp + a)
                        ins = nc.tensor.matmul(ps[:, 2 * (k % 3) + a], KP[r0:r0 + SLOT, g, kt * P:(kt + 1) * P],
                                               QP[r0:r0 + SLOT, g, 512 * qh:512 * qh + 512], start=True, stop=True,
                                               tile_position=(r0, 0))
                    ins.then_inc(st_mm, 1)

                def values(k):
                    g, qh, kt, hp = AU[k]
                    o = 2 * g + qh
                    if kt == 0 and hp == 0 and o >= 2:
                        pe.wait_ge(o_out, b * 2 * G4 + o - 1)
                    pe.wait_ge(probs, b * NAU + k + 1)
                    for a in range(2):
                        r0 = SLOT * (2 * hp + a)
                        ins = nc.tensor.matmul(ps[r0:r0 + SLOT, 6 + o % 2], VP[:, kt, g * P + r0:g * P + r0 + SLOT],
                                               PT[:, k % 3, a], start=(kt == 0), stop=(kt == QT - 1),
                                               tile_position=(0, r0), skip_group_check=True)
                    ins.then_inc(pv_mm, 1)

                for k in range(NAU + 2):
                    if k < NAU:
                        transposed_scores(k)
                    if k >= 2:
                        values(k - 2)
                for k in range(G4 * 2):
                    pe.wait_ge(o_out, b * 2 * G4 + k + 1)
                    if k >= 4:
                        pe.wait_ge(o_normed, b * 2 * G4 + k - 3)
                    nc.tensor.matmul(ps[:, k % 4], sel[:], OP[:, k // 2, 512 * (k % 2):512 * (k % 2) + 512],
                                     start=True, stop=True).then_inc(den_mm, 1)
                pe.wait_ge(o_normed, (b + 1) * 2 * G4)
                for m in range(DC):
                    for half in range(2):
                        for g in range(G4):
                            ins = nc.tensor.matmul(low4[:, m, half], wo[:, g, m * P:(m + 1) * P],
                                                   OP[:, g, 512 * half:512 * half + 512],
                                                   start=(g == 0), stop=(g == G4 - 1))
                ins.then_inc(wo_mm, 1)
                pe.wait_ge(xb_ready, b + 1)
                ln2.pe_mean(nc, pe, b, XB, stat0)
                ln2.pe_var(nc, pe, b, T1, stat1)
                pe.wait_ge(hn2_ready, b + 1)
                for qt in range(QT):
                    for c in range(DC):
                        ins = nc.tensor.matmul(ps[:, 0, NE * qt:NE * qt + NE], HN[:, c, qt * P:(qt + 1) * P], gw[:, c],
                                               start=(c == 0), stop=(c == DC - 1))
                ins.then_inc(lg_mm, 1)
                pe.wait_ge(oh_ready, b + 1)
                for qt in range(QT):
                    ins = nc.tensor.transpose(ps[0:NE, qt // 4, P * (qt % 4):P * (qt % 4) + P], OH[:, qt], ident[:])
                ins.then_inc(oht_mm, 1)
                for e in range(NE):
                    if e >= 2:
                        pe.wait_ge(mk_out, b * NE + e - 1)
                    for qt in range(QT):
                        ins = nc.tensor.matmul(ps[:, 4 + 2 * (e % 2) + qt // 4, P * (qt % 4):P * (qt % 4) + P],
                                               OHB[:, qt, e:e + 1].broadcast_to([P, P]), identb[:],
                                               start=True, stop=True)
                    ins.then_inc(mk_mm, 1)
                pe.wait_ge(oht_out, b + 1)
                for m in range(DC):
                    for half in range(2):
                        nc.tensor.matmul(low4[:, m, half], b2[:, m * P:(m + 1) * P],
                                         OHT[:, 512 * half:512 * half + 512], start=True, stop=False,
                                         skip_group_check=True)
                with pe.Fori(0, NE // 2) as e2:
                    for u in range(2):
                        ne = b * NE + e2 * 2 + u
                        pe.wait_ge(mk_out, (b + 1) * NE)
                        pe.wait_ge(w_in[u], (b * (NE // 2) + e2 + 1) * 48)

                        def hidden(k):
                            f, half = k // 2, k % 2
                            if k >= 4:
                                pe.wait_ge(relu_out, ne * UNITS + k - 3)
                            else:
                                pe.wait_ge(relu_out, ne * UNITS)
                            for c in range(DC):
                                ins = nc.tensor.matmul(ps[:, 4 + k % 4], w1[:, u, c, f * P:(f + 1) * P],
                                                       HN[:, c, 512 * half:512 * half + 512],
                                                       start=(c == 0), stop=(c == DC - 1))
                            ins.then_inc(mid_mm, 1)

                        def back(k):
                            f, half = k // 2, k % 2
                            pe.wait_ge(mid_ready, ne * UNITS + k + 1)
                            for m in range(DC):
                                ins = nc.tensor.matmul(low4[:, m, half], w2[:, u, f, m * P:(m + 1) * P],
                                                       MID[:, k % MIDS], start=False, stop=True,
                                                       skip_group_check=True)
                            ins.then_inc(exp_u[u], 1)
                            return ins

                        for k in range(UNITS + 3):
                            if k < UNITS:
                                hidden(k)
                            if k >= 3:
                                back(k - 3)
                pe.wait_ge(summed, 3 * b + 3)
                ln_end.pe_mean(nc, pe, b, XB, stat0)
                ln_end.pe_var(nc, pe, b, T1, stat1)


def slots(a, axis=-1):
    heads = np.reshape(a, a.shape[:-1] + (16, 16))
    out = np.zeros(a.shape[:-1] + (16, 32), a.dtype)
    out[..., 0:16] = heads
    return out.reshape(a.shape[:-1] + (512,))


def moe_inputs(i):
    f = lambda k: i["L0_ffn_" + k]
    mark = np.zeros((16, 32), np.float32)
    mark[:, 16] = 1.0
    column = lambda a: a.reshape(-1, P).T
    out = {k: slots(f(k)) for k in ("wq", "wk", "wv")}
    out["wo"] = slots(f("wo").T).T
    out.update(gate_w=f("gate_w"), gate_b=f("gate_b"), bq_col=column(slots(f("bq"))), bk_col=column(slots(f("bk"))),
               bv=slots(f("bv")), mark_col=column(mark.reshape(-1)), mark_row=mark.reshape(-1),
               moe_columns=np.stack([column(a) for a in (i["L0_attn_ln_out_w"], f("ln1_g"), f("ln1_b"), f("ln2_g"),
                                                         f("ln2_b"), f("bo"))], 1),
               b2=f("b2"), w1=f("w1"), w2=f("w2"), b1_col=f("b1").reshape(8, 8, P).transpose(0, 2, 1))
    return {k: np.ascontiguousarray(v) for k, v in out.items()}


def quantized_mlp(nc, x_tm, w_gate, w_up, w_down, out_tm):
    F = w_gate.shape[0]
    BLK = 16
    WR = 8
    WP = F // WR
    FULL = F // P
    FK = [P] * FULL + ([F - FULL * P] if F % P else [])
    NK = len(FK)
    U = 2
    NI = N // P // U
    MID_HIGH = (5.0, 3.5, 2.5)
    MID_LOW = (1.75, 1.25, 0.75, 0.25)
    QUANT_STEPS = 9

    with ExitStack() as ctx:
        sb, psum, sem = allocators(nc, ctx, "qm")
        wg_r = sb("wg_r", [WP, WR, D])
        wu_r = sb("wu_r", [WP, WR, D])
        wd_r = sb("wd_r", [P, DC, F])
        wT = sb("wT", [P, 2, DC, F])
        wdT = sb("wdT", [P, NK, D])
        ident = sb("ident", [P, P])
        eps = sb("eps", [P, 1])
        x = sb("x", [P, U, D])
        xq = sb("xq", [P, U, D])
        xqT = sb("xqT", [P, U, D])
        th = sb("th", [P, U, F])
        h = sb("h", [P, U, F])
        hqT = sb("hqT", [P, U, NK, P])
        FMAX = WR * D
        qn = sb("qn", [P, FMAX])
        qa = sb("qa", [P, FMAX])
        qs = sb("qs", [P, FMAX])
        qt = sb("qt", [P, FMAX])
        amax = sb("amax", [P, FMAX // BLK])
        rsc = sb("rsc", [P, FMAX // BLK])
        y = sb("y", [P, U, D])
        stats = sb("stats", [P, 6])
        spare = sb("spare", [P, 1])
        mv = sb("mv", [P, U, 2])
        std = sb("std", [P, U])
        rstd = sb("rstd", [P, U])
        yn = sb("yn", [P, U, D])
        gate = psum("gate", [P, 1024])
        up = psum("up", [P, 1024])
        xt_ps = psum("xt_ps", [P, 512])
        ht_ps = psum("ht_ps", [P, 1024])
        y_ps = psum("y_ps", [P, 512])
        y_of = [y_ps[:, 0:D], xt_ps[:, D:2 * D]]
        turn_ps = [gate[:, 0:512], gate[:, 512:1024], up[:, 0:512], up[:, 512:1024]]

        weights_in = sem("weights_in")
        consts = sem("consts")
        eps_set = sem("eps_set")
        wvec = sem("wvec")
        w_scaled = sem("w_scaled")
        w_signed = sem("w_signed")
        w_quant = sem("w_quant")
        w_mm = sem("w_mm")
        w_out = sem("w_out")
        x_in = [sem(f"x_in{u}") for u in range(U)]
        q_scaled = sem("q_scaled")
        q_signed = sem("q_signed")
        xq_ready = sem("xq_ready")
        xT_mm = sem("xT_mm")
        xT_out = sem("xT_out")
        gate_mm = sem("gate_mm")
        tanh_out = sem("tanh_out")
        h_ready = sem("h_ready")
        hq_ready = sem("hq_ready")
        hT_mm = sem("hT_mm")
        hT_out = sem("hT_out")
        y_mm = sem("y_mm")
        y_ready = sem("y_ready")
        var_ready = sem("var_ready")
        std_ready = sem("std_ready")
        yn_ready = sem("yn_ready")
        stored = [sem(f"stored{u}") for u in range(U)]
        vec = sem("vec")
        block = ctx.enter_context(nc.Block())

        W_JOBS = [(wg_r, WP, FMAX), (wu_r, WP, FMAX), (wd_r, P, DC * F)]
        W_TURNS = []
        for k, w_r in enumerate((wg_r, wu_r)):
            for r in range(WR):
                for c in range(DC):
                    W_TURNS.append((w_r[:, r, c * P:(c + 1) * P], WP, P, wT[:, k, c, r:F:WR], k))
        for c in range(DC):
            for k in range(NK):
                W_TURNS.append((wd_r[:, c, k * P:k * P + FK[k]], P, FK[k], wdT[0:FK[k], k, c * P:(c + 1) * P], 2))

        @block.sync
        def _(sp):
            sp.dma_start(wg_r[:], w_gate.rearrange("(p r) k -> p r k", r=WR)).then_inc(weights_in, 16)
            sp.dma_start(wu_r[:], w_up.rearrange("(p r) k -> p r k", r=WR)).then_inc(weights_in, 16)
            sp.dma_start(wd_r[:], w_down.rearrange("(c p) k -> p c k", p=P)).then_inc(weights_in, 16)
            with sp.Fori(0, NI) as i:
                for u in range(U):
                    sp.wait_ge(y_ready, i * U)
                    sp.dma_start(x[:, u], x_tm[bass.ds((i * U + u) * P, P), :]).then_inc(x_in[u], 16)

        @block.gpsimd
        def _(pool):
            pool.memset(ident[:], 0.0).then_inc(consts, 1)
            pool.wait_ge(consts, 1)
            pool.affine_select(out=ident[:], in_=ident[:], compare_op=ALU.not_equal, fill=1.0, base=0,
                               pattern=[[-1, P]], channel_multiplier=1).then_inc(consts, 1)

        def round_fp4(own, src, dst, rows, n, scaled, signed, at):
            nb = n // BLK
            blocks = lambda t: t.rearrange("p (b k) -> p b k", k=BLK)
            wide = lambda t: t.rearrange("p (b o) -> p b o", o=1).broadcast_to([rows, nb, BLK])
            own.done(nc.vector.tensor_reduce(amax[0:rows, 0:nb], blocks(src), AX.X, ALU.max,
                                             apply_absolute_value=True))
            own.done(nc.vector.tensor_scalar(amax[0:rows, 0:nb], amax[0:rows, 0:nb], 1.0 / 6.0, 1e-12,
                                             ALU.mult, ALU.max))
            own.done(nc.vector.reciprocal(rsc[0:rows, 0:nb], amax[0:rows, 0:nb]))
            nc.vector.tensor_tensor(blocks(qn[0:rows, 0:n]), blocks(src), wide(rsc[0:rows, 0:nb]),
                                    ALU.mult).then_inc(scaled, 1)
            own.eng.wait_ge(signed, at + 1)
            a, t = qa[0:rows, 0:n], qt[0:rows, 0:n]
            own.done(nc.vector.tensor_scalar(t, a, MID_HIGH[0], 2.0, ALU.is_gt, ALU.mult))
            for m in MID_HIGH[1:]:
                own.done(nc.vector.scalar_tensor_tensor(t, a, m, t, ALU.is_gt, ALU.add))
            own.done(nc.vector.tensor_scalar(t, t, 2.0, None, ALU.mult))
            for m in MID_LOW:
                own.done(nc.vector.scalar_tensor_tensor(t, a, m, t, ALU.is_gt, ALU.add))
            own.done(nc.vector.scalar_tensor_tensor(blocks(qs[0:rows, 0:n]), blocks(qs[0:rows, 0:n]), 0.5,
                                                    wide(amax[0:rows, 0:nb]), ALU.mult, ALU.mult))
            return nc.vector.tensor_tensor(dst, t, qs[0:rows, 0:n], ALU.mult)

        def magnitude_and_sign(act, rows, n, scaled, signed, at):
            act.wait_ge(scaled, at + 1)
            nc.scalar.activation(qa[0:rows, 0:n], qn[0:rows, 0:n], ACT.Abs)
            nc.scalar.activation(qs[0:rows, 0:n], qn[0:rows, 0:n], ACT.Sign).then_inc(signed, 1)

        @block.scalar
        def _(act):
            for k, (w_r, rows, n) in enumerate(W_JOBS):
                magnitude_and_sign(act, rows, n, w_scaled, w_signed, k)
            with act.Fori(0, NI) as i:
                for u in range(U):
                    n = i * U + u
                    magnitude_and_sign(act, P, D, q_scaled, q_signed, i * 2 * U + u)
                    act.wait_ge(xT_mm, n + 1)
                    nc.scalar.activation(xqT[:, u], xt_ps[:, 0:D], ACT.Copy).then_inc(xT_out, 1)
                    act.wait_ge(gate_mm, n + 1)
                    nc.scalar.activation(th[:, u], gate[:, 0:F], ACT.Tanh, scale=0.5).then_inc(tanh_out, 1)
                for u in range(U):
                    n = i * U + u
                    magnitude_and_sign(act, P, F, q_scaled, q_signed, i * 2 * U + U + u)
                    act.wait_ge(hT_mm, n + 1)
                    nc.scalar.activation(hqT[:, u, 0:FULL].rearrange("p k t -> p (k t)"), ht_ps[:, 0:FULL * P],
                                         ACT.Copy)
                    nc.scalar.activation(hqT[0:FK[-1], u, NK - 1], ht_ps[0:FK[-1], FULL * P:NK * P],
                                         ACT.Copy).then_inc(hT_out, 1)
                act.wait_ge(var_ready, (i + 1) * U)
                nc.scalar.activation(std[:], mv[:, :, 1], ACT.Sqrt, bias=eps[:, 0:1]).then_inc(std_ready, 1)
                for u in range(U):
                    act.wait_ge(yn_ready, i * U + u + 1)
                    act.dma_start(out_tm[bass.ds((i * U + u) * P, P), :], yn[:, u]).then_inc(stored[u], 16)
            for u in range(U):
                act.wait_ge(stored[u], 16 * NI)

        @block.vector
        def _(dve):
            nc.vector.memset(eps[:], EPS).then_inc(eps_set, 1)
            dve.wait_ge(weights_in, 16 * 3)
            own = Steps(dve, wvec, 3 * (3 + QUANT_STEPS), 0)
            for k, (w_r, rows, n) in enumerate(W_JOBS):
                flat = w_r[:].rearrange("p r k -> p (r k)")
                round_fp4(own, flat, flat, rows, n, w_scaled, w_signed, k).then_inc(w_quant, 1)
                dve.wait_ge(w_quant, k + 1)
            for k, (src, kp, m, dst, job) in enumerate(W_TURNS):
                dve.wait_ge(w_mm, k + 1)
                nc.vector.tensor_copy(dst, turn_ps[k % 4][0:m, 0:kp]).then_inc(w_out, 1)
            with dve.Fori(0, NI) as i:
                own = Steps(dve, vec, U * (2 * (3 + QUANT_STEPS) + 2) + 1, i)
                for u in range(U):
                    dve.wait_ge(x_in[u], 16 * (i + 1))
                    round_fp4(own, x[:, u], xq[:, u], P, D, q_scaled, q_signed, i * 2 * U + u)\
                        .then_inc(xq_ready, 1)
                    dve.wait_ge(xq_ready, i * U + u + 1)
                    dve.wait_ge(tanh_out, i * U + u + 1)
                    own.done(nc.vector.scalar_tensor_tensor(h[:, u], th[:, u], 1.0, gate[:, 0:F], ALU.add,
                                                            ALU.mult))
                    nc.vector.scalar_tensor_tensor(h[:, u], h[:, u], 0.5, up[:, 0:F], ALU.mult, ALU.mult)\
                        .then_inc(h_ready, 1)
                dve.wait_ge(h_ready, (i + 1) * U)
                for u in range(U):
                    round_fp4(own, h[:, u], h[:, u], P, F, q_scaled, q_signed, i * 2 * U + U + u)\
                        .then_inc(hq_ready, 1)
                    dve.wait_ge(hq_ready, i * U + u + 1)
                for u in range(U):
                    dve.wait_ge(y_mm, i * U + u + 1)
                    nc.vector.tensor_tensor(y[:, u], x[:, u], y_of[u], ALU.add).then_inc(y_ready, 1)
                    dve.wait_ge(y_ready, i * U + u + 1)
                    own.done(nc.vector.bn_stats(stats[:], y[:, u]))
                    nc.vector.memset(spare[:], 0.0)
                    nc.vector.bn_aggr(mv[:, u], stats[:]).then_inc(var_ready, 1)
                    dve.wait_ge(var_ready, i * U + u + 1)
                dve.wait_ge(std_ready, i + 1)
                own.done(nc.vector.reciprocal(rstd[:], std[:]))
                for u in range(U):
                    dve.wait_ge(stored[u], 16 * i)
                    nc.vector.tensor_scalar(yn[:, u], y[:, u], mv[:, u, 0:1], rstd[:, u:u + 1], ALU.subtract,
                                            ALU.mult).then_inc(yn_ready, 1)
                own.close()

        @block.tensor
        def _(pe):
            pe.wait_ge(consts, 2)
            for k, (src, kp, m, dst, job) in enumerate(W_TURNS):
                pe.wait_ge(w_quant, job + 1)
                if k >= 4:
                    pe.wait_ge(w_out, k - 3)
                nc.tensor.transpose(turn_ps[k % 4][0:m, 0:kp], src, ident[0:kp, 0:kp])\
                    .then_inc(w_mm, 1)
            pe.wait_ge(w_out, len(W_TURNS))
            with pe.Fori(0, NI) as i:
                for u in range(U):
                    n = i * U + u
                    pe.wait_ge(xq_ready, n + 1)
                    pe.wait_ge(xT_out, n)
                    pe.wait_ge(y_ready, i * U)
                    for c in range(DC):
                        ins = nc.tensor.transpose(xt_ps[:, c * P:(c + 1) * P], xq[:, u, c * P:(c + 1) * P], ident[:])
                    ins.then_inc(xT_mm, 1)
                    pe.wait_ge(xT_out, n + 1)
                    pe.wait_ge(h_ready, n)
                    for k, dst in ((0, gate), (1, up)):
                        for lo, hi in ((0, 512), (512, F)):
                            for c in range(DC):
                                ins = nc.tensor.matmul(dst[:, lo:hi], xqT[:, u, c * P:(c + 1) * P],
                                                       wT[:, k, c, lo:hi], start=(c == 0), stop=(c == DC - 1))
                    ins.then_inc(gate_mm, 1)
                for u in range(U):
                    n = i * U + u
                    pe.wait_ge(hq_ready, n + 1)
                    pe.wait_ge(hT_out, n)
                    for k in range(NK):
                        ins = nc.tensor.transpose(ht_ps[0:FK[k], k * P:(k + 1) * P], h[:, u, k * P:k * P + FK[k]],
                                                  ident[:])
                    ins.then_inc(hT_mm, 1)
                    pe.wait_ge(hT_out, n + 1)
                    pe.wait_ge(y_ready, i * U)
                    for k in range(NK):
                        ins = nc.tensor.matmul(y_of[u], hqT[0:FK[k], u, k], wdT[0:FK[k], k],
                                               start=(k == 0), stop=(k == NK - 1))
                    ins.then_inc(y_mm, 1)


def rwkv_inputs(i):
    f = lambda k: i["L0_attn_" + k]
    names = ["tm_w1", "tm_w2", "td_w1", "td_w2", "Wr", "Wk", "Wv", "Wo", "Wg", "cWk", "cWv", "cWr"]
    out = {k: f(k) for k in names}
    out["columns"] = np.stack([f(k).reshape(2, DC, P).transpose(0, 2, 1) for k in RWKV_COLUMNS], 2)
    key, query = np.arange(P)[:, None], np.arange(P)[None]
    levels = [key == query]
    for m in (1, 2, 4, 8, 16, 32, 64):
        levels.append((key // (2 * m) == query // (2 * m)) & (key // m % 2 == 0) & (query // m % 2 == 1))
    out["masks"] = np.array(levels, np.float32)
    return {k: np.ascontiguousarray(v) for k, v in out.items()}


def program(nc, x_fm, rwkv_in, moe_in, fa_in, qm_in, work, out):
    rwkv(nc, x_fm, rwkv_in["masks"], rwkv_in, work[0])
    attention_moe(nc, x_fm, work[0], moe_in, work[1])
    feature_attention(nc, work[1], *fa_in, work[2])
    quantized_mlp(nc, work[2], *qm_in, out)


def kernel(**inputs):
    import concourse.bacc as _bacc
    from concourse.bass_utils import run_bass_kernel_spmd as _run

    nc = _bacc.Bacc("TRN2", target_bir_lowering=False, num_devices=1)
    i = {k: np.asarray(v) for k, v in inputs.items()}
    arrays = {}

    def inn(name, a):
        name = "in_" + name
        arrays[name] = np.ascontiguousarray(a)
        return nc.dram_tensor(name, a.shape, mybir.dt.from_np(a.dtype), kind="ExternalInput").ap()

    x_fm = inn("x_fm", i["L0_attn_x"].reshape(N, D).T)
    rwkv_in = {k: inn("rwkv_" + k, a) for k, a in rwkv_inputs(i).items()}
    moe_in = {k: inn("moe_" + k, a) for k, a in moe_inputs(i).items()}
    fa_in = [inn("fa_" + k, i["L1_attn_" + k]) for k in ("Wq", "bq", "Wk", "bk", "Wv", "bv", "Wo", "bo")]
    qm_in = [inn("qm_" + k, i["L1_ffn_" + k]) for k in ("w_gate", "w_up", "w_down")]
    work = [nc.dram_tensor(f"work{k}", (D, N) if k < 2 else (N, D), F32, kind="Internal").ap() for k in range(3)]
    out = nc.dram_tensor("out", (N, D), F32, kind="ExternalOutput").ap()
    program(nc, x_fm, rwkv_in, moe_in, fa_in, qm_in, work, out)
    r = _run(nc, [arrays], core_ids=[0])
    return r.results[0]["out"].reshape(B, T, D)
```

```python
from contextlib import ExitStack

import numpy as np
import concourse.bass as bass
from concourse import mybir

F32 = mybir.dt.float32
BF16 = mybir.dt.bfloat16
U8 = mybir.dt.uint8
ALU = mybir.AluOpType
ACT = mybir.ActivationFunctionType
AX = mybir.AxisListType

P = 128
B, T, D = 4, 1024, 256
DC = D // P
N = B * T
EPS = 1e-5
BIG = 3.0e38


class Steps:

    def __init__(self, eng, sem, per_pass, n):
        self.eng, self.sem, self.per, self.n, self.k = eng, sem, per_pass, n, 0

    def done(self, ins):
        self.k += 1
        ins.then_inc(self.sem, 1)
        self.eng.wait_ge(self.sem, self.n * self.per + self.k)

    def close(self):
        assert self.k == self.per, (self.k, self.per)


def allocators(nc, ctx, tag):
    def sb(name, shape, dt=F32):
        return ctx.enter_context(nc.sbuf_tensor(f"{tag}_{name}", shape, dt))

    def psum(name, shape, dt=F32):
        return ctx.enter_context(nc.psum_tensor(f"{tag}_{name}", shape, dt))

    held = []

    def clear():
        nc.clear_and_free_semaphores(held)
        nc.all_engine_barrier()

    ctx.callback(clear)

    def sem(name):
        held.append(nc.alloc_semaphore(f"{tag}_{name}"))
        return held[-1]

    return sb, psum, sem


def feature_attention(nc, x_fm, wq, bq, wk, bk, wv, bv, wo, bo, out_tm):
    H, C = 16, 64
    HID = H * C
    TILES = N // P
    HC = HID // P
    NG = 12
    ROWS = sum(C - j for j in range(0, C, 2)) // NG
    GROUP_COLS = ROWS * 2 * H
    groups, left = [], list(range(0, C, 2))
    while left:
        runs, used = [], 0
        for j in list(left):
            if used + C - j <= ROWS:
                runs.append((j, used * 2 * H, C - j))
                used += C - j
                left.remove(j)
        assert used == ROWS
        groups.append(runs)
    assert len(groups) == NG
    SB = TB = 4
    assert NG % SB == 0
    LAG = 3
    AT_TURN, AT_OUT, AT_K, AT_Q, AT_V = 3, 5, 6, 7, 8
    AT_SUMS, AT_STD, AT_NORM, AT_STORE = 1, 8, 10, 11

    with ExitStack() as ctx:
        sb, psum, sem = allocators(nc, ctx, "fa")
        wq_sb = sb("wq", [P, DC, HID])
        wk_sb = sb("wk", [P, DC, HID])
        wv_sb = sb("wv", [P, DC, HID])
        wo_sb = sb("wo", [P, HC, D])
        bq_sb = sb("bq", [P, HID])
        bk_sb = sb("bk", [P, HID])
        bv_sb = sb("bv", [P, HID])
        bo_sb = sb("bo", [P, D])
        ident = sb("ident", [P, P])
        lift = sb("lift", [P, 2, HID])
        eps = sb("eps", [P, 1])
        xT = sb("xT", [P, 2, DC, P])
        Q = sb("Q", [P, 2, HID])
        K = sb("K", [P, 2, HID])
        V = sb("V", [P, 2, HID])
        kmax = sb("kmax", [P, HID])
        kmin = sb("kmin", [P, HID])
        M = sb("M", [P, 2, HID])
        S = sb("S", [P, SB, GROUP_COLS])
        PV = sb("PV", [P, TB, GROUP_COLS])
        nums = sb("nums", [P, HID])
        dens = sb("dens", [P, HID])
        att = dens
        attT = sb("attT", [P, HC, P])
        y = sb("y", [P, D])
        stats = sb("stats", [P, 6])
        mv = sb("mv", [P, 2])
        spare = sb("spare", [P, 1])
        std = sb("std", [P, 1])
        rstd = sb("rstd", [P, 1])
        yn = sb("yn", [P, 2, D])

        num = psum("num", [P, HID])
        den = psum("den", [P, HID])
        pa = psum("pa", [P, HID])
        pb = psum("pb", [P, HID])

        weights_in = sem("weights_in")
        consts = sem("consts")
        consts_v = sem("consts_v")
        x_in = [sem("x_in0"), sem("x_in1")]
        x_used = sem("x_used")
        q_mm = sem("q_mm")
        k_mm = sem("k_mm")
        v_mm = sem("v_mm")
        q_out = sem("q_out")
        k_out = sem("k_out")
        v_out = sem("v_out")
        scanned = sem("scanned")
        q_added = sem("q_added")
        extremes = sem("extremes")
        max_ready = sem("max_ready")
        scores = sem("scores")
        shifted = sem("shifted")
        probs = sem("probs")
        products = sem("products")
        weighted = sem("weighted")
        den_used = sem("den_used")
        num_used = sem("num_used")
        sums_out = sem("sums_out")
        dens_inverted = sem("dens_inverted")
        att_ready = sem("att_ready")
        attT_mm = sem("attT_mm")
        attT_out = sem("attT_out")
        y_mm = sem("y_mm")
        y_taken = sem("y_taken")
        y_ready = sem("y_ready")
        stats_ready = sem("stats_ready")
        var_ready = sem("var_ready")
        std_ready = sem("std_ready")
        inverted = sem("inverted")
        yn_ready = sem("yn_ready")
        stored = [sem("stored0"), sem("stored1")]
        block = ctx.enter_context(nc.Block())

        def over_tiles(eng, tile):
            tile(0, 0, True, False)
            with eng.Fori(0, TILES // 2 - 1) as i:
                tile(i * 2 + 1, 1, False, False)
                tile(i * 2 + 2, 0, False, False)
            tile(TILES - 1, 1, False, True)

        def run_of(buf, slot, run):
            j, at, w = run
            return buf[:, slot, at:at + 2 * H * w].rearrange("p (a h w) -> p a h w", a=2, h=H)

        def by_head(t):
            return t.rearrange("p (h c) -> p h c", h=H)

        def over_rows(t, u, j):
            return by_head(t[:, u])[:, :, j:C].rearrange("p (a h) w -> p a h w", a=1).broadcast_to([P, 2, H, C - j])

        def key_column(t, u, j):
            return t[:, u].rearrange("p (h c o) -> p c h o", h=H, o=1)[:, j:j + 2].broadcast_to([P, 2, H, C - j])

        x_v = x_fm.rearrange("(c p) t -> p c t", p=P)

        @block.sync
        def _(sp):
            for w_sb, w in ((wk_sb, wk), (wq_sb, wq), (wv_sb, wv), (wo_sb, wo)):
                sp.dma_start(w_sb[:], w.rearrange("(c p) n -> p c n", p=P)).then_inc(weights_in, 16)
            for b_sb, b_ in ((bq_sb, bq), (bk_sb, bk), (bv_sb, bv), (bo_sb, bo)):
                sp.dma_start(b_sb[:], b_.rearrange("(a n) -> a n", a=1).broadcast_to([P, b_.shape[0]]))\
                    .then_inc(weights_in, 16)
            for n in range(2):
                sp.dma_start(xT[:, n], x_v[:, :, n * P:(n + 1) * P]).then_inc(x_in[n], 16)
            with sp.Fori(0, TILES // 2 - 1) as i:
                for u in range(2):
                    n = i * 2 + 2 + u
                    sp.wait_ge(x_used, n - 1)
                    sp.dma_start(xT[:, u], x_v[:, :, bass.ds(n * P, P)]).then_inc(x_in[u], 16)

        @block.gpsimd
        def _(pool):
            pool.memset(ident[:], 0.0).then_inc(consts, 1)
            pool.wait_ge(consts, 1)
            pool.affine_select(out=ident[:], in_=ident[:], compare_op=ALU.not_equal, fill=1.0, base=0,
                               pattern=[[-1, P]], channel_multiplier=1).then_inc(consts, 1)

            def normalise(n):
                pool.wait_ge(sums_out, 2 * n + 2)
                pool.wait_ge(dens_inverted, n + 1)
                pool.tensor_tensor(att[:], nums[:], dens[:], ALU.mult).then_inc(att_ready, 1)

            def tile(n, u, first, last):
                for g, runs in enumerate(groups):
                    pool.wait_ge(scores, n * NG + g + 1)
                    if g == 0:
                        pool.wait_ge(max_ready, n + 1)
                    for run in runs:
                        r = run_of(S, g % SB, run)
                        for a in range(2):
                            ins = pool.tensor_tensor(r[:, a], r[:, a], over_rows(M, u, run[0])[:, a], ALU.subtract)
                    ins.then_inc(shifted, 1)
                    if g == AT_SUMS + 2 and not first:
                        normalise(n - 1)

            over_tiles(pool, tile)
            normalise(TILES - 1)

        @block.scalar
        def _(act):
            def take_sums(n):
                act.wait_ge(den_used, (n + 1) * NG)
                nc.scalar.activation(dens[:], den[:], ACT.Copy).then_inc(sums_out, 1)
                act.wait_ge(num_used, (n + 1) * NG)
                nc.scalar.activation(nums[:], num[:], ACT.Copy).then_inc(sums_out, 1)

            def take_turned(n):
                for half in range(2):
                    act.wait_ge(attT_mm, 2 * n + half + 1)
                    nc.scalar.activation(attT[:, 4 * half:4 * half + 4].rearrange("p c t -> p (c t)"),
                                         pb[:, 512 * half:512 * half + 512], ACT.Copy).then_inc(attT_out, 1)

            def deviation(n):
                act.wait_ge(var_ready, n + 1)
                nc.scalar.activation(std[:], mv[:, 1:2], ACT.Sqrt, bias=eps[:, 0:1]).then_inc(std_ready, 1)

            def store(n, u):
                act.wait_ge(yn_ready, n + 1)
                act.dma_start(out_tm[bass.ds(n * P, P), :], yn[:, u]).then_inc(stored[u], 16)

            def tile(n, u, first, last):
                for g in range(NG):
                    act.wait_ge(shifted, n * NG + g + 1)
                    nc.scalar.activation(S[:, g % SB], S[:, g % SB], ACT.Exp)\
                        .then_inc(probs, 1)
                    if g == AT_SUMS and not first:
                        take_sums(n - 1)
                    if g == AT_TURN + 2 and not first:
                        take_turned(n - 1)
                    if g == AT_STD and not first:
                        deviation(n - 1)
                    if g == AT_STORE and not first:
                        store(n - 1, 1 - u)

            act.wait_ge(consts_v, 4)
            over_tiles(act, tile)
            take_sums(TILES - 1)
            take_turned(TILES - 1)
            deviation(TILES - 1)
            store(TILES - 1, 1)
            act.wait_ge(stored[0], 8 * TILES)
            act.wait_ge(stored[1], 8 * TILES)

        @block.vector
        def _(dve):
            nc.vector.memset(eps[:], EPS).then_inc(consts_v, 1)
            nc.vector.memset(lift[:], 0.0).then_inc(consts_v, 1)
            dve.wait_ge(consts_v, 2)
            lv = lift[:].rearrange("p a (h c) -> p a h c", h=H)
            nc.vector.memset(lv[:, 0, :, 0:1], -BIG).then_inc(consts_v, 1)
            nc.vector.memset(lv[:, 1, :, 0:1], BIG).then_inc(consts_v, 1)
            dve.wait_ge(consts_v, 4)
            dve.wait_ge(weights_in, 16 * 8)

            def take_k(n, u):
                dve.wait_ge(k_mm, n * 2 + 2)
                nc.vector.tensor_tensor(K[:, u], pb[:], bk_sb[:], ALU.add).then_inc(k_out, 1)
                dve.wait_ge(k_out, n + 1)
                nc.vector.tensor_tensor_scan(kmax[:], lift[:, 0], K[:, u], 0.0, ALU.add, ALU.max).then_inc(scanned, 1)
                nc.vector.tensor_tensor_scan(kmin[:], lift[:, 1], K[:, u], 0.0, ALU.add, ALU.min).then_inc(scanned, 1)

            def take_q(n, u):
                dve.wait_ge(q_mm, n * 2 + 2)
                nc.vector.tensor_tensor(Q[:, u], pa[:], bq_sb[:], ALU.add).then_inc(q_added, 1)
                dve.wait_ge(q_added, n + 1)
                nc.vector.tensor_scalar(Q[:, u], Q[:, u], C ** -0.5, None, ALU.mult).then_inc(q_out, 1)
                dve.wait_ge(q_out, n + 1)
                dve.wait_ge(scanned, 2 * n + 2)
                nc.vector.tensor_tensor(kmax[:], kmax[:], Q[:, u], ALU.mult).then_inc(extremes, 1)
                nc.vector.tensor_tensor(kmin[:], kmin[:], Q[:, u], ALU.mult).then_inc(extremes, 1)
                dve.wait_ge(extremes, 2 * n + 2)
                nc.vector.tensor_tensor(M[:, u], kmax[:], kmin[:], ALU.max).then_inc(max_ready, 1)

            def take_v(n, u):
                dve.wait_ge(v_mm, n * 2 + 2)
                nc.vector.tensor_tensor(V[:, u], pb[:], bv_sb[:], ALU.add).then_inc(v_out, 1)

            def make_scores(n, u, g, first):
                if g >= SB or not first:
                    dve.wait_ge(den_used, n * NG + g - SB + 1)
                    dve.wait_ge(weighted, n * NG + g - SB + 1)
                for run in groups[g]:
                    ins = nc.vector.tensor_tensor(run_of(S, g % SB, run), over_rows(Q, u, run[0]),
                                                  key_column(K, u, run[0]), ALU.mult)
                ins.then_inc(scores, 1)

            def weigh(n, u, g, first):
                dve.wait_ge(probs, n * NG + g + 1)
                if g >= TB or not first:
                    dve.wait_ge(num_used, n * NG + g - TB + 1)
                for run in groups[g]:
                    ins = nc.vector.tensor_tensor(run_of(PV, g % TB, run), run_of(S, g % SB, run),
                                                  key_column(V, u, run[0]), ALU.mult)
                ins.then_inc(products, 1)
                dve.wait_ge(products, n * NG + g + 1)
                for run in groups[g]:
                    r = run_of(PV, g % TB, run)
                    ins = nc.vector.tensor_tensor(r[:, 0, :, 1:], r[:, 0, :, 1:], r[:, 1, :, 1:], ALU.add)
                ins.then_inc(weighted, 1)

            def invert(n):
                dve.wait_ge(sums_out, 2 * n + 1)
                nc.vector.reciprocal(dens[:], dens[:]).then_inc(dens_inverted, 1)

            def join(n):
                dve.wait_ge(y_mm, n + 1)
                nc.vector.tensor_tensor(y[:], pa[:, 0:D], bo_sb[:], ALU.add).then_inc(y_taken, 1)
                dve.wait_ge(y_taken, n + 1)
                nc.vector.tensor_tensor(y[:], y[:], pa[:, 512:512 + D], ALU.add).then_inc(y_ready, 1)
                dve.wait_ge(y_ready, n + 1)
                nc.vector.bn_stats(stats[:], y[:]).then_inc(stats_ready, 1)
                dve.wait_ge(stats_ready, n + 1)
                nc.vector.memset(spare[:], 0.0)
                nc.vector.bn_aggr(mv[:], stats[:]).then_inc(var_ready, 1)

            def norm(n, u, stores):
                dve.wait_ge(std_ready, n + 1)
                nc.vector.reciprocal(rstd[:], std[:]).then_inc(inverted, 1)
                dve.wait_ge(inverted, n + 1)
                if stores is not None:
                    dve.wait_ge(stored[u], stores)
                nc.vector.tensor_scalar(yn[:, u], y[:], mv[:, 0:1], rstd[:, 0:1], ALU.subtract, ALU.mult)\
                    .then_inc(yn_ready, 1)

            def tile(n, u, first, last):
                for g in range(NG):
                    make_scores(n, u, g, first)
                    if g >= 2:
                        weigh(n, u, g - 2, first)
                    elif not first:
                        weigh(n - 1, 1 - u, NG + g - 2, False)
                    if g == AT_SUMS + 1 and not first:
                        invert(n - 1)
                    if g == AT_OUT + LAG and not first:
                        join(n - 1)
                    if g == AT_NORM and not first:
                        norm(n - 1, 1 - u, 8 * (n - 2 + u))
                    if not last:
                        if g == AT_K + LAG:
                            take_k(n + 1, 1 - u)
                        if g == AT_Q + LAG:
                            take_q(n + 1, 1 - u)
                        if g == AT_V + LAG:
                            take_v(n + 1, 1 - u)

            take_k(0, 0)
            take_q(0, 0)
            take_v(0, 0)
            over_tiles(dve, tile)
            weigh(TILES - 1, 1, NG - 2, False)
            weigh(TILES - 1, 1, NG - 1, False)
            invert(TILES - 1)
            join(TILES - 1)
            norm(TILES - 1, 1, 16 * (TILES // 2 - 1))

        @block.tensor
        def _(pe):
            def project(n, u, w_sb, dst, done):
                for half in range(2):
                    for c in range(DC):
                        ins = nc.tensor.matmul(dst[:, 512 * half:512 * half + 512], xT[:, u, c],
                                               w_sb[:, c, 512 * half:512 * half + 512],
                                               start=(c == 0), stop=(c == DC - 1))
                    ins.then_inc(done, 1)

            def make_k(n, u, x_count):
                pe.wait_ge(x_in[u], x_count)
                project(n, u, wk_sb, pb, k_mm)

            def make_q(n, u):
                project(n, u, wq_sb, pa, q_mm)

            def make_v(n, u):
                pe.wait_ge(k_out, n + 1)
                project(n, u, wv_sb, pb, v_mm)

            def add_up(n, g, acc, buf, ready, used, added):
                pe.wait_ge(ready, n * NG + g + 1)
                for j, at, w in groups[g]:
                    for a in range(1 if added else 2):
                        for half in range(2):
                            h0 = 8 * half
                            r = run_of(buf, g % SB, (j, at, w))[:, a, h0:h0 + 8, a:w]
                            ins = nc.tensor.matmul(by_head(acc)[:, h0:h0 + 8, j + a:C], ident[:], r,
                                                   start=(j == 0 and a == 0), stop=True, skip_group_check=True)
                ins.then_inc(used, 1)

            def turn(n, u):
                pe.wait_ge(att_ready, n + 1)
                for c in range(HC):
                    ins = nc.tensor.transpose(pb[:, c * P:(c + 1) * P], att[:, c * P:(c + 1) * P], ident[:])
                    if c % 4 == 3:
                        ins.then_inc(attT_mm, 1)
                for c in range(DC):
                    ins = nc.tensor.transpose(pa[:, 512 + c * P:512 + (c + 1) * P], xT[:, u, c], ident[:])
                ins.then_inc(x_used, 1)

            def project_out(n):
                pe.wait_ge(attT_out, 2 * n + 2)
                for c in range(HC):
                    ins = nc.tensor.matmul(pa[:, 0:D], attT[:, c], wo_sb[:, c], start=(c == 0), stop=(c == HC - 1))
                ins.then_inc(y_mm, 1)

            def tile(n, u, first, last):
                for g in range(NG):
                    if g == 0 and not first:
                        pe.wait_ge(sums_out, 2 * n)
                    add_up(n, g, den, S, probs, den_used, False)
                    add_up(n, g, num, PV, weighted, num_used, True)
                    if not first:
                        if g == AT_TURN:
                            pe.wait_ge(v_out, n + 1)
                            pe.wait_ge(q_added, n + 1)
                            turn(n - 1, 1 - u)
                        if g == AT_OUT:
                            project_out(n - 1)
                    if not last:
                        if g == AT_K:
                            if not first:
                                pe.wait_ge(attT_out, 2 * n)
                            make_k(n + 1, 1 - u, 16 if first else 8 * (n + 2 + u))
                        if g == AT_Q:
                            if not first:
                                pe.wait_ge(y_ready, n)
                            make_q(n + 1, 1 - u)
                        if g == AT_V:
                            make_v(n + 1, 1 - u)

            pe.wait_ge(weights_in, 16 * 8)
            pe.wait_ge(consts, 2)
            make_k(0, 0, 16)
            make_q(0, 0)
            make_v(0, 0)
            over_tiles(pe, tile)
            turn(TILES - 1, 1)
            project_out(TILES - 1)


RWKV_COLUMNS = ["ln1_w", "ln2_w", "x_maa", "w_maa", "k_maa", "v_maa", "r_maa", "g_maa", "time_decay",
                "time_first", "gn_w", "gn_b", "ck_maa", "cr_maa"]


class FeatureNorm:

    def __init__(self, sem, name, ones, eps, groups):
        self.ones, self.eps, self.groups = ones, eps, groups
        self.mean_mm = sem(f"{name}_mean_mm")
        self.centered = sem(f"{name}_centered")
        self.squared = sem(f"{name}_squared")
        self.var_mm = sem(f"{name}_var_mm")
        self.std_out = sem(f"{name}_std_out")
        self.inverted = sem(f"{name}_inverted")
        self.normed = sem(f"{name}_normed")

    def sums(self, nc, src, stat):
        for g in range(self.groups):
            cs = [g] if self.groups > 1 else list(range(DC))
            for half in range(stat.shape[2]):
                for k, c in enumerate(cs):
                    ins = nc.tensor.matmul(stat[:, g, half], self.ones, src[:, c, 512 * half:512 * half + 512],
                                           start=(k == 0), stop=(k == len(cs) - 1))
        return ins

    def pe_mean(self, nc, pe, n, src, stat):
        self.sums(nc, src, stat).then_inc(self.mean_mm, 1)

    def pe_var(self, nc, pe, n, sq, stat):
        pe.wait_ge(self.squared, n + 1)
        self.sums(nc, sq, stat).then_inc(self.var_mm, 1)

    def spread(self, stat):
        s = stat.rearrange("p g h t -> p g (h t)")
        return s if self.groups == DC else s.broadcast_to([P, DC, s.shape[2]])

    def dve_center(self, nc, dve, n, src, out, stat):
        dve.wait_ge(self.mean_mm, n + 1)
        nc.vector.tensor_tensor(out, src, self.spread(stat), ALU.subtract).then_inc(self.centered, 1)

    def act_square(self, nc, act, n, src, sq):
        act.wait_ge(self.centered, n + 1)
        nc.scalar.activation(sq, src, ACT.Square).then_inc(self.squared, 1)

    def act_std(self, nc, act, n, stat, std):
        act.wait_ge(self.var_mm, n + 1)
        nc.scalar.activation(std, stat.rearrange("p g h t -> p g (h t)"), ACT.Sqrt,
                             bias=self.eps).then_inc(self.std_out, 1)

    def dve_scale(self, nc, dve, n, buf, std, weight):
        dve.wait_ge(self.std_out, n + 1)
        nc.vector.reciprocal(std, std).then_inc(self.inverted, 1)
        dve.wait_ge(self.inverted, n + 1)
        if weight is None:
            s = std if self.groups == DC else std.broadcast_to([P, DC, std.shape[2]])
            ins = nc.vector.tensor_tensor(buf, buf, s, ALU.mult)
        else:
            for c in range(DC):
                ins = nc.vector.scalar_tensor_tensor(buf[:, c], buf[:, c], weight[:, c:c + 1],
                                                     std[:, c if self.groups == DC else 0], ALU.mult, ALU.mult)
        ins.then_inc(self.normed, 1)
        dve.wait_ge(self.normed, n + 1)


def rwkv(nc, x_fm, masks, p, work_fm):
    L = 2
    H, HS = 4, 64
    E, NMIX, ED = 32, 5, 64
    FK = 6
    CH = T // P
    LEVELS = [1, 2, 4, 8, 16, 32, 64]
    NL = len(LEVELS)
    CONSTS = 8
    PAIRS = CH // 2
    VEC_STEPS = 1 + 2 + NL + (CH - 1) + 1 + 1 + 2
    with ExitStack() as ctx:
        sb, psum, sem = allocators(nc, ctx, "tm")
        X = sb("X", [P, DC, T])
        XL = sb("XL", [P, DC, T + 1])
        SX = sb("SX", [P, DC, T])
        ZX = sb("ZX", [P, 2, DC, T])
        MX = sb("MX", [P, T])
        MX4 = sb("MX4", [E, T])
        TD = sb("TD", [ED, T])
        W = sb("W", [P, DC, 2 * T])
        RKO = sb("RKO", [P, 3, DC, T])
        R, K, OUT = RKO[:, 0], RKO[:, 1], RKO[:, 2]
        K2 = RKO[:].rearrange("p a c t -> p (a c) t")
        Vt = sb("Vt", [P, CH, D])
        G = sb("G", [P, DC, T])
        T1 = sb("T1", [P, DC, T])
        T2 = sb("T2", [P, DC, T])
        A = sb("A", [P, CH * DC, 2, P])
        ST = sb("ST", [P, CH, DC, P])
        ident = sb("ident", [P, P])
        ones = sb("ones", [P, P])
        gones = sb("gones", [P, P])
        eps = sb("eps", [P, 1])
        spare = sb("spare", [P, 64])
        mask_f = sb("masks", [P, NL + 1, P])
        mask_sb = mask_f[:].bitcast(mybir.dt.uint32)
        w = {k: sb(k, s) for k, s in dict(
            tm_w1=[P, DC, NMIX * E], tm_w2=[P, D], tm_w24=[E, D], td_w1=[P, DC, ED], td_w2=[ED, D],
            Wr=[P, DC, D], Wk=[P, DC, D], Wv=[P, DC, D], Wo=[P, DC, D], Wg=[P, DC, D],
            cWk=[P, DC, FK * P], cWv=[P, FK, D], cWr=[P, DC, D]).items()}
        cols = sb("cols", [P, len(RWKV_COLUMNS), DC])
        col = {k: cols[:, i] for i, k in enumerate(RWKV_COLUMNS)}
        ps = psum("ps", [P, 8, 512])

        weights_in = sem("weights_in")
        x_in = sem("x_in")
        start_copy = sem("start_copy")
        consts = sem("consts")
        consts_p = sem("consts_p")
        ln1 = FeatureNorm(sem, "ln1", ones[:], eps[:, 0:1], 1)
        ln2 = FeatureNorm(sem, "ln2", ones[:], eps[:, 0:1], 1)
        gn = FeatureNorm(sem, "gn", gones[:], eps[:, 0:1], DC)
        mixin_ready = sem("mixin_ready")
        mix_mm = sem("mix_mm")
        tanh_mix = sem("tanh_mix")
        delta_mm = sem("delta_mm")
        delta_used = sem("delta_used")
        zx_ready = sem("zx_ready")
        proj_mm = sem("proj_mm")
        proj_out = sem("proj_out")
        td_mm = sem("td_mm")
        td_out = sem("td_out")
        uk_ready = sem("uk_ready")
        lvl_ready = sem("lvl_ready")
        lvl_mm = sem("lvl_mm")
        lvl_kept = sem("lvl_kept")
        kT_mm = sem("kT_mm")
        kT_out = sem("kT_out")
        kv_mm = sem("kv_mm")
        state_ready = sem("state_ready")
        out_mm = sem("out_mm")
        out_copied = sem("out_copied")
        gated = sem("gated")
        wo_mm = sem("wo_mm")
        mid_ready = sem("mid_ready")
        ck_ready = sem("ck_ready")
        ck_mm = sem("ck_mm")
        ck_out = sem("ck_out")
        ck_sq = sem("ck_sq")
        cr_mm = sem("cr_mm")
        cr_out = sem("cr_out")
        cv_mm = sem("cv_mm")
        x_ready = sem("x_ready")
        stored = sem("stored")
        vec = sem("vec")
        act_s = sem("act_s")
        block = ctx.enter_context(nc.Block())

        x_v = work_fm.rearrange("(c p) (b t) -> b p c t", p=P, t=T)
        MAAS = ["w_maa", "k_maa", "v_maa", "r_maa", "g_maa"]
        stat0 = ps[:, 0:2].rearrange("p (g h) t -> p g h t", g=1)
        stat1 = ps[:, 2:4].rearrange("p (g h) t -> p g h t", g=1)
        low4 = ps[:, 0:4].rearrange("p (g h) t -> p g h t", g=DC)
        high4 = ps[:, 4:8].rearrange("p (g h) t -> p g h t", g=DC)
        flat = lambda a: a.rearrange("p g h t -> p g (h t)")
        base = [0]
        for m in LEVELS:
            base.append(base[-1] + T // m)

        @block.sync
        def _(sp):
            sp.dma_start(work_fm, x_fm).then_inc(start_copy, 16)
            sp.dma_start(mask_f[:], masks.rearrange("l p i -> p l i")).then_inc(start_copy, 16)
            sp.wait_ge(start_copy, 32)
            with sp.Fori(0, L) as l:
                sp.wait_ge(x_ready, l * B)
                for k in ("tm_w1", "td_w1", "Wr", "Wk", "Wv", "Wo", "Wg", "cWk", "cWv", "cWr"):
                    sp.dma_start(w[k][:], p[k][bass.ds(l, 1)].rearrange("o (c p) n -> p (o c) n", p=P))\
                        .then_inc(weights_in, 16)
                sp.dma_start(w["tm_w2"][:], p["tm_w2"][bass.ds(l, 1), 0:4].rearrange("o f e d -> (o f e) d"))\
                    .then_inc(weights_in, 16)
                sp.dma_start(w["tm_w24"][:], p["tm_w2"][bass.ds(l, 1), 4:5].rearrange("o f e d -> (o f e) d"))\
                    .then_inc(weights_in, 16)
                sp.dma_start(w["td_w2"][:], p["td_w2"][bass.ds(l, 1)].rearrange("o e d -> (o e) d"))\
                    .then_inc(weights_in, 16)
                sp.dma_start(cols[:], p["columns"][bass.ds(l, 1)].rearrange("o p k c -> (o p) k c"))\
                    .then_inc(weights_in, 16)
                with sp.Fori(0, B) as b:
                    n = l * B + b
                    sp.wait_ge(stored, n * 16)
                    sp.dma_start(X[:], x_v[bass.ds(b, 1)].rearrange("o p c t -> p (o c) t")).then_inc(x_in, 16)

        NW = 16 * 14

        @block.gpsimd
        def _(pool):
            pool.memset(ident[:], 0.0).then_inc(consts_p, 1)
            pool.wait_ge(consts_p, 1)
            pool.affine_select(out=ident[:], in_=ident[:], compare_op=ALU.not_equal, fill=1.0, base=0,
                               pattern=[[-1, P]], channel_multiplier=1).then_inc(consts_p, 1)

        @block.scalar
        def _(act):
            act.wait_ge(consts, CONSTS)
            with act.Fori(0, L) as l, act.Fori(0, B) as b:
                n = l * B + b
                own = Steps(act, act_s, DC, n)
                ln1.act_square(nc, act, n, XL[:, :, 1:T + 1], T1[:])
                ln1.act_std(nc, act, n, stat1, T2[:, 0:1])
                act.wait_ge(mix_mm, n + 1)
                nc.scalar.activation(MX[:], ps[:, 4:6].rearrange("p h t -> p (h t)"), ACT.Tanh)
                nc.scalar.activation(MX4[:], ps[0:E, 6:8].rearrange("p h t -> p (h t)"), ACT.Tanh)\
                    .then_inc(tanh_mix, 1)
                act.wait_ge(proj_mm, n * 5 + 1)
                nc.scalar.activation(TD[:], ps[0:ED, 0:2].rearrange("p h t -> p (h t)"), ACT.Tanh)\
                    .then_inc(proj_out, 1)
                act.wait_ge(td_mm, n + 1)
                for c in range(DC):
                    own.done(nc.scalar.activation(W[:, c, 0:T], flat(low4)[:, c], ACT.Exp,
                                                  bias=col["time_decay"][:, c:c + 1]))
                nc.scalar.activation(W[:, :, 0:T], W[:, :, 0:T], ACT.Exp, scale=-1.0).then_inc(td_out, 1)
                act.wait_ge(proj_mm, n * 5 + 2)
                nc.scalar.activation(K, flat(low4), ACT.Copy).then_inc(proj_out, 1)
                act.wait_ge(proj_mm, n * 5 + 3)
                nc.scalar.activation(Vt[:].rearrange("p j d -> p (j d)"), ps[:, 0:4].rearrange("p a b -> p (a b)"),
                                     ACT.Copy).then_inc(proj_out, 1)
                act.wait_ge(proj_mm, n * 5 + 4)
                nc.scalar.activation(R, flat(low4), ACT.Tanh, scale=0.5).then_inc(proj_out, 1)
                act.wait_ge(proj_mm, n * 5 + 5)
                nc.scalar.activation(T2[:], flat(low4), ACT.Tanh, scale=0.5)
                nc.scalar.activation(G[:], flat(low4), ACT.Copy).then_inc(proj_out, 1)
                act.wait_ge(kT_mm, n + 1)
                nc.scalar.activation(ZX[:, 0].rearrange("p c t -> p (c t)"), ps[:, 4:8].rearrange("p a b -> p (a b)"),
                                     ACT.Copy).then_inc(kT_out, 1)
                act.wait_ge(out_mm, n + 1)
                nc.scalar.activation(OUT, flat(low4), ACT.Copy).then_inc(out_copied, 1)
                gn.act_square(nc, act, n, OUT, T1[:])
                gn.act_std(nc, act, n, low4, T2[:])
                ln2.act_square(nc, act, n, XL[:, :, 1:T + 1], T1[:])
                ln2.act_std(nc, act, n, stat1, T2[:, 0:1])
                for k in range(2 * FK):
                    act.wait_ge(ck_mm, n * 2 * FK + k + 1)
                    nc.scalar.activation(K2[:, k // 2, 512 * (k % 2):512 * (k % 2) + 512], ps[:, 4 + k % 4], ACT.Relu)\
                        .then_inc(ck_out, 1)
                act.wait_ge(cr_mm, n + 1)
                nc.scalar.activation(T1[:], flat(low4), ACT.Tanh, scale=0.5).then_inc(cr_out, 1)
                act.wait_ge(x_ready, n + 1)
                act.dma_start(x_v[bass.ds(b, 1)].rearrange("o p c t -> p (o c) t"), X[:]).then_inc(stored, 16)
            act.wait_ge(stored, L * B * 16)

        @block.vector
        def _(dve):
            for k, ins in enumerate([
                    nc.vector.memset(eps[:], EPS), nc.vector.memset(ones[:], 1.0 / D),
                    nc.vector.memset(XL[:, :, 0:1], 0.0), nc.vector.memset(gones[:], 0.0),
                    nc.vector.memset(A[:], 0.0), nc.vector.memset(ST[:], 0.0)]):
                ins.then_inc(consts, 1)
            dve.wait_ge(consts, 6)
            nc.vector.memset(gones[0:HS, 0:HS], 1.0 / HS).then_inc(consts, 1)
            nc.vector.memset(gones[HS:P, HS:P], 1.0 / HS).then_inc(consts, 1)
            with dve.Fori(0, L) as l:
                with dve.Fori(0, B) as b:
                    n = l * B + b
                    dve.wait_ge(weights_in, (l + 1) * NW)
                    dve.wait_ge(x_in, (n + 1) * 16)
                    own = Steps(dve, vec, VEC_STEPS, n)
                    free_columns = iter(range(64))

                    def beat():
                        k = next(free_columns)
                        return nc.vector.memset(spare[:, k:k + 1], 0.0)

                    xl, prev = XL[:, :, 1:T + 1], XL[:, :, 0:T]

                    def mix_in(out, maa):
                        for c in range(DC):
                            ins = nc.vector.scalar_tensor_tensor(out[:, c], SX[:, c], col[maa][:, c:c + 1],
                                                                 xl[:, c], ALU.mult, ALU.add)
                        return ins

                    ln1.dve_center(nc, dve, n, X[:], xl, stat0)
                    ln1.dve_scale(nc, dve, n, xl, T2[:, 0:1], col["ln1_w"])
                    own.done(nc.vector.tensor_tensor(SX[:], prev, xl, ALU.subtract))
                    mix_in(ZX[:, 1], "x_maa").then_inc(mixin_ready, 1)
                    for f, maa in enumerate(MAAS):
                        z = ZX[:, f % 2]
                        dve.wait_ge(delta_mm, n * 5 + f + 1)
                        if f == 1:
                            dve.wait_ge(mix_mm, n + 1)
                        if f >= 2:
                            dve.wait_ge(proj_mm, n * 5 + f - 1)
                        for c in range(DC):
                            ins = nc.vector.scalar_tensor_tensor(z[:, c], flat(high4)[:, c], col[maa][:, c:c + 1],
                                                                 SX[:, c], ALU.add, ALU.mult)
                        ins.then_inc(delta_used, 1)
                        dve.wait_ge(delta_used, n * 5 + f + 1)
                        nc.vector.tensor_tensor(z, z, xl, ALU.add).then_inc(zx_ready, 1)
                    dve.wait_ge(proj_out, n * 5 + 5)
                    own.done(nc.vector.tensor_scalar(R, R, 0.5, 0.5, ALU.mult, ALU.add))
                    own.done(nc.vector.scalar_tensor_tensor(G[:], T2[:], 1.0, G[:], ALU.add, ALU.mult))
                    for c in range(DC):
                        ins = nc.vector.tensor_scalar(T1[:, c], K[:, c], col["time_first"][:, c:c + 1], None, ALU.mult)
                    ins.then_inc(uk_ready, 1)
                    dve.wait_ge(uk_ready, n + 1)

                    def keep(lv):
                        for j in range(CH):
                            g, a = j // 2, j % 2
                            if a == 0:
                                dve.wait_ge(lvl_mm, n * (NL + 1) * PAIRS + lv * PAIRS + g + 1)
                                beat()
                            nc.vector.copy_predicated(A[:, 4 * g:4 * g + 4, a],
                                                      mask_sb[:, lv:lv + 1].broadcast_to([P, 4, P]),
                                                      ps[:, j].rearrange("p (h i) -> p h i", h=4))\
                                .then_inc(lvl_kept, 1)

                    dve.wait_ge(td_out, n + 1)
                    for lv, m in enumerate(LEVELS):
                        keep(lv)
                        nb = T // (2 * m)
                        tw = W[:, :, base[lv]:base[lv + 1]].rearrange("p c (b s) -> p c b s", s=2)
                        dve.wait_ge(lvl_mm, n * (NL + 1) * PAIRS + (lv + 2) * PAIRS)
                        for c in range(DC):
                            second = R[:, c].rearrange("p (b s m) -> p b s m", s=2, m=m)[:, :, 1]
                            first = K[:, c].rearrange("p (b s m) -> p b s m", s=2, m=m)[:, :, 0]
                            nc.vector.tensor_tensor(second, second, tw[:, c, :, 0:1].broadcast_to([P, nb, m]), ALU.mult)
                            nc.vector.tensor_tensor(first, first, tw[:, c, :, 1:2].broadcast_to([P, nb, m]), ALU.mult)
                        own.done(nc.vector.tensor_tensor(W[:, :, base[lv + 1]:base[lv + 1] + nb], tw[:, :, :, 0],
                                                         tw[:, :, :, 1], ALU.mult))
                        beat().then_inc(lvl_ready, 1)
                    keep(NL)
                    dve.wait_ge(kv_mm, n + 1)
                    for j in range(CH - 1):
                        for c in range(DC):
                            for a in range(2):
                                r0, r1 = HS * a, HS * a + HS
                                ins = nc.vector.scalar_tensor_tensor(
                                    ST[r0:r1, j + 1, c, r0:r1], ST[r0:r1, j, c, r0:r1],
                                    W[r0:r1, c, base[NL] + j:base[NL] + j + 1],
                                    ps[r0:r1, (2 * j + c) // 4, P * ((2 * j + c) % 4) + r0:P * ((2 * j + c) % 4) + r1],
                                    ALU.mult, ALU.add)
                        own.done(ins)
                    beat().then_inc(state_ready, 1)
                    dve.wait_ge(out_copied, n + 1)
                    gn.dve_center(nc, dve, n, OUT, OUT, high4)
                    gn.dve_scale(nc, dve, n, OUT, T2[:], col["gn_w"])
                    own.done(nc.vector.tensor_scalar(G[:], G[:], 0.5, None, ALU.mult))
                    for c in range(DC):
                        ins = nc.vector.scalar_tensor_tensor(OUT[:, c], OUT[:, c], col["gn_b"][:, c:c + 1], G[:, c],
                                                             ALU.add, ALU.mult)
                    ins.then_inc(gated, 1)
                    dve.wait_ge(wo_mm, n + 1)
                    nc.vector.tensor_tensor(X[:], X[:], flat(high4), ALU.add).then_inc(mid_ready, 1)
                    dve.wait_ge(mid_ready, n + 1)
                    ln2.dve_center(nc, dve, n, X[:], xl, stat0)
                    ln2.dve_scale(nc, dve, n, xl, T2[:, 0:1], col["ln2_w"])
                    own.done(nc.vector.tensor_tensor(SX[:], prev, xl, ALU.subtract))
                    mix_in(ZX[:, 0], "ck_maa")
                    mix_in(ZX[:, 1], "cr_maa").then_inc(ck_ready, 1)
                    for k in range(2 * FK):
                        dve.wait_ge(ck_out, n * 2 * FK + k + 1)
                        kk = K2[:, k // 2, 512 * (k % 2):512 * (k % 2) + 512]
                        nc.vector.tensor_tensor(kk, kk, kk, ALU.mult).then_inc(ck_sq, 1)
                    dve.wait_ge(cr_out, n + 1)
                    own.done(nc.vector.tensor_scalar(T1[:], T1[:], 0.5, 0.5, ALU.mult, ALU.add))
                    dve.wait_ge(cv_mm, n + 1)
                    own.done(nc.vector.tensor_tensor(T1[:], T1[:], flat(high4), ALU.mult))
                    nc.vector.tensor_tensor(X[:], X[:], T1[:], ALU.add).then_inc(x_ready, 1)
                    own.close()

        @block.tensor
        def _(pe):
            pe.wait_ge(consts, CONSTS)
            pe.wait_ge(consts_p, 2)
            with pe.Fori(0, L) as l:
                with pe.Fori(0, B) as b:
                    n = l * B + b
                    pe.wait_ge(weights_in, (l + 1) * NW)

                    def linear(dst, wt, src, rows=P, kc=DC):
                        for m in range((wt.shape[2] + P - 1) // P):
                            for half in range(2):
                                for c in range(kc):
                                    ins = nc.tensor.matmul(dst[0:rows, m, half], wt[:, c, m * P:m * P + rows],
                                                           src[:, c, 512 * half:512 * half + 512],
                                                           start=(c == 0), stop=(c == kc - 1))
                        return ins

                    pe.wait_ge(x_in, (n + 1) * 16)
                    ln1.pe_mean(nc, pe, n, X, stat0)
                    ln1.pe_var(nc, pe, n, T1, stat1)
                    pe.wait_ge(mixin_ready, n + 1)
                    pe.wait_ge(x_ready, n)
                    for half in range(2):
                        for c in range(DC):
                            nc.tensor.matmul(ps[:, 4 + half], w["tm_w1"][:, c, 0:P],
                                             ZX[:, 1, c, 512 * half:512 * half + 512], start=(c == 0), stop=(c == DC - 1))
                        for c in range(DC):
                            ins = nc.tensor.matmul(ps[0:E, 6 + half], w["tm_w1"][:, c, P:P + E],
                                                   ZX[:, 1, c, 512 * half:512 * half + 512],
                                                   start=(c == 0), stop=(c == DC - 1))
                    ins.then_inc(mix_mm, 1)

                    def delta(f):
                        if f == 0:
                            pe.wait_ge(tanh_mix, n + 1)
                        else:
                            pe.wait_ge(delta_used, n * 5 + f)
                        for c in range(DC):
                            for half in range(2):
                                t0, t1 = 512 * half, 512 * half + 512
                                if f < 4:
                                    lt, rt = w["tm_w2"][E * f:E * f + E, c * P:(c + 1) * P], MX[E * f:E * f + E, t0:t1]
                                    tp = (E * f, 0)
                                else:
                                    lt, rt = w["tm_w24"][:, c * P:(c + 1) * P], MX4[:, t0:t1]
                                    tp = (0, 0)
                                ins = nc.tensor.matmul(ps[:, 4 + 2 * c + half], lt, rt, start=True, stop=True,
                                                       tile_position=tp)
                        ins.then_inc(delta_mm, 1)

                    def project(f):
                        pe.wait_ge(zx_ready, n * 5 + f + 1)
                        z = ZX[:, f % 2]
                        if f == 0:
                            linear(low4, w["td_w1"], z, rows=ED).then_inc(proj_mm, 1)
                            pe.wait_ge(proj_out, n * 5 + 1)
                            for m in range(DC):
                                for half in range(2):
                                    ins = nc.tensor.matmul(low4[:, m, half], w["td_w2"][:, m * P:(m + 1) * P],
                                                           TD[:, 512 * half:512 * half + 512], start=True, stop=True)
                            ins.then_inc(td_mm, 1)
                            return
                        if f == 1:
                            pe.wait_ge(td_out, n + 1)
                        else:
                            pe.wait_ge(proj_out, n * 5 + f)
                        if f == 2:
                            for j in range(CH):
                                for c in range(DC):
                                    ins = nc.tensor.matmul(ps[:, j // 2, D * (j % 2):D * (j % 2) + D],
                                                           z[:, c, j * P:(j + 1) * P], w["Wv"][:, c],
                                                           start=(c == 0), stop=(c == DC - 1))
                            ins.then_inc(proj_mm, 1)
                            return
                        linear(low4, w[[None, "Wk", None, "Wr", "Wg"][f]], z).then_inc(proj_mm, 1)

                    delta(0)
                    delta(1)
                    project(0)
                    for f in range(2, 5):
                        delta(f)
                        project(f - 1)
                    project(4)
                    pe.wait_ge(proj_out, n * 5 + 5)
                    pe.wait_ge(uk_ready, n + 1)
                    pe.wait_ge(delta_used, n * 5 + 5)
                    for lv in range(NL + 1):
                        keys = T1 if lv == 0 else K
                        if lv >= 2:
                            pe.wait_ge(lvl_ready, n * NL + lv - 1)
                        for g in range(PAIRS):
                            if lv >= 1:
                                pe.wait_ge(lvl_kept, n * (NL + 1) * CH + (lv - 1) * CH + 2 * g + 2)
                            for k in range(4):
                                j, c = 2 * g + k // 2, k % 2
                                for a in range(2):
                                    ins = nc.tensor.matmul(ps[:, 2 * g + a, k * P:(k + 1) * P],
                                                           keys[HS * a:HS * a + HS, c, j * P:(j + 1) * P],
                                                           R[HS * a:HS * a + HS, c, j * P:(j + 1) * P],
                                                           start=True, stop=True)
                            ins.then_inc(lvl_mm, 1)
                    pe.wait_ge(lvl_ready, n * NL + NL)
                    pe.wait_ge(lvl_kept, (n + 1) * (NL + 1) * CH)
                    for j in range(CH):
                        for c in range(DC):
                            k = 2 * j + c
                            ins = nc.tensor.transpose(ps[:, 4 + k // 4, P * (k % 4):P * (k % 4) + P],
                                                      K[:, c, j * P:(j + 1) * P], ident[:])
                    ins.then_inc(kT_mm, 1)
                    pe.wait_ge(kT_out, n + 1)
                    kt = ZX[:, 0].rearrange("p c t -> p (c t)").rearrange("p (j d) -> p j d", j=CH)
                    for j in range(CH):
                        for c in range(DC):
                            k = 2 * j + c
                            ins = nc.tensor.matmul(ps[:, k // 4, P * (k % 4):P * (k % 4) + P],
                                                   kt[:, j, c * P:(c + 1) * P], Vt[:, j, c * P:(c + 1) * P],
                                                   start=True, stop=True)
                    ins.then_inc(kv_mm, 1)
                    pe.wait_ge(state_ready, n + 1)
                    for c in range(DC):
                        for j in range(CH):
                            o = low4[:, c, j // 4, P * (j % 4):P * (j % 4) + P]
                            nc.tensor.matmul(o, ST[:, j, c], R[:, c, j * P:(j + 1) * P], start=True, stop=False,
                                             skip_group_check=True)
                            for a in range(2):
                                ins = nc.tensor.matmul(o[HS * a:HS * a + HS], Vt[:, j, c * P + HS * a:c * P + HS * a + HS],
                                                       A[:, 2 * j + c, a], start=False, stop=True,
                                                       tile_position=(0, HS * a), skip_group_check=True)
                    ins.then_inc(out_mm, 1)
                    pe.wait_ge(out_copied, n + 1)
                    gn.pe_mean(nc, pe, n, OUT, high4)
                    gn.pe_var(nc, pe, n, T1, low4)
                    pe.wait_ge(gated, n + 1)
                    linear(high4, w["Wo"], OUT).then_inc(wo_mm, 1)
                    pe.wait_ge(mid_ready, n + 1)
                    ln2.pe_mean(nc, pe, n, X, stat0)
                    ln2.pe_var(nc, pe, n, T1, stat1)
                    pe.wait_ge(ck_ready, n + 1)
                    for k in range(2 * FK):
                        if k >= 4:
                            pe.wait_ge(ck_out, n * 2 * FK + k - 3)
                        for c in range(DC):
                            ins = nc.tensor.matmul(ps[:, 4 + k % 4], w["cWk"][:, c, P * (k // 2):P * (k // 2) + P],
                                                   ZX[:, 0, c, 512 * (k % 2):512 * (k % 2) + 512],
                                                   start=(c == 0), stop=(c == DC - 1))
                        ins.then_inc(ck_mm, 1)
                    linear(low4, w["cWr"], ZX[:, 1]).then_inc(cr_mm, 1)
                    pe.wait_ge(ck_sq, (n + 1) * 2 * FK)
                    linear(high4, w["cWv"], K2, kc=FK).then_inc(cv_mm, 1)


MOE_COLUMNS = ["ln_out_w", "ln1_g", "ln1_b", "ln2_g", "ln2_b", "bo", "bq", "bk"]


def attention_moe(nc, x_fm, rwkv_fm, p, out_fm):
    NH, SLOT = 16, 32
    HD = D // NH
    G4 = NH // 4
    QT = T // P
    NE, FE = 8, 1024
    FM = FE // P
    SCALE = HD ** -0.5
    UNITS = FM * 2
    MIDS = 8
    CONSTS = 2 + NE
    VEC_STEPS = 5 * G4 + 2 * G4 + 6
    STACKS = 16 * 2 * 6
    with ExitStack() as ctx:
        sb, psum, sem = allocators(nc, ctx, "mo")
        XA = sb("XA", [P, DC, T])
        XB = sb("XB", [P, DC, T])
        HN = sb("HN", [P, DC, T])
        T1 = sb("T1", [P, DC, T])
        std = sb("std", [P, 1, T])
        QS = sb("QS", [P, NH, T], BF16)
        KS = sb("KS", [P, NH, T], BF16)
        VP = sb("VP", [P, QT, NH * SLOT])
        shared = sb("shared", [P, 6144])
        parts = shared[:].bitcast(BF16).rearrange("p (a s c t) -> p a s c t", a=2, s=3, c=DC)
        PT = shared[:, 0:4096].rearrange("p (k a t) -> p k a t", k=4, a=2)
        MID = shared[:, 0:4096].rearrange("p (k t) -> p k t", k=MIDS)
        mx = sb("mx", [P, QT, 2, NH])
        mg = sb("mg", [P, QT, 4])
        NM = sb("NM", [P, QT, 3, 4], BF16)
        NMT = std[0:12, 0, 0:T // 2].bitcast(BF16)
        MK = QS[:].rearrange("p h t -> p (h t)").rearrange("p (a e t) -> p a e t", a=2, e=NE)[:, 0]
        OP = sb("OP", [P, G4, T])
        QF, KF = T1, OP[:, 0:DC]
        wq = sb("wq", [P, DC, D])
        wk = sb("wk", [P, DC, D])
        wv = sb("wv", [P, DC, NH * SLOT])
        wo = sb("wo", [P, G4, D])
        gw = sb("gw", [P, DC, NE])
        gb = sb("gb", [P, NE])
        bv = sb("bv", [P, NH * SLOT])
        cols = sb("cols", [P, len(MOE_COLUMNS), DC])
        col = {k: cols[:, i] for i, k in enumerate(MOE_COLUMNS)}
        b2 = sb("b2", [NE, D])
        w1 = sb("w1", [P, 2, DC, FE])
        w2 = sb("w2", [P, 2, FM, D])
        b1 = sb("b1", [P, 2, FM])
        LG = sb("LG", [P, QT, NE])
        OH = sb("OH", [P, QT, NE])
        OHB = sb("OHB", [P, QT, NE], BF16)
        OHT = std[0:NE, 0]
        top = sb("top", [P, QT])
        order = sb("order", [P, NE])
        ident = sb("ident", [P, P])
        identb = sb("identb", [P, P], BF16)
        sel = sb("sel", [P, P])
        ones = sb("ones", [P, P])
        eps = sb("eps", [P, 1])
        ps = psum("ps", [P, 8, 512])

        const_in = sem("const_in")
        consts = sem("consts")
        consts_p = sem("consts_p")
        ones_set = sem("ones_set")
        split_h = sem("split_h")
        split_r = sem("split_r")
        split_m = sem("split_m")
        split_l = sem("split_l")
        parts_out = sem("parts_out")
        stacked = [sem(f"stacked{g}") for g in range(G4)]
        nm_ready = sem("nm_ready")
        nmt_mm = sem("nmt_mm")
        nmt_out = sem("nmt_out")
        nm_out = sem("nm_out")
        nm_in = sem("nm_in")
        x_in = sem("x_in")
        N_ = lambda k: FeatureNorm(sem, k, ones[:], eps[:, 0:1], 1)
        ln_out, ln_join, ln1, ln2, ln_end = N_("out"), N_("join"), N_("ln1"), N_("ln2"), N_("end")
        summed = sem("summed")
        hn_ready = sem("hn_ready")
        qk_mm = sem("qk_mm")
        qk_out = sem("qk_out")
        v_mm = sem("v_mm")
        v_out = sem("v_out")
        s_mm = sem("s_mm")
        s_max = sem("s_max")
        st_mm = sem("st_mm")
        probs = sem("probs")
        pv_mm = sem("pv_mm")
        o_out = sem("o_out")
        den_mm = sem("den_mm")
        o_normed = sem("o_normed")
        wo_mm = sem("wo_mm")
        xb_ready = sem("xb_ready")
        hn2_ready = sem("hn2_ready")
        lg_mm = sem("lg_mm")
        oh_ready = sem("oh_ready")
        oht_mm = sem("oht_mm")
        oht_out = sem("oht_out")
        mk_mm = sem("mk_mm")
        mk_out = sem("mk_out")
        w_in = [sem("w_in0"), sem("w_in1")]
        mid_mm = sem("mid_mm")
        relu_out = sem("relu_out")
        mid_ready = sem("mid_ready")
        exp_u = [sem("exp_u0"), sem("exp_u1")]
        total_ready = sem("total_ready")
        stored = sem("stored")
        vec = sem("vec")
        parts_dram = nc.dram_tensor("mo_parts", (2, 3, D, T), BF16, kind="Internal").ap()
        nm_dram = nc.dram_tensor("mo_maxima", (12, T), BF16, kind="Internal").ap()
        block = ctx.enter_context(nc.Block())

        fm = lambda a: a.rearrange("(c p) (b t) -> b p c t", p=P, t=T)
        x_v, r_v, o_v = fm(x_fm), fm(rwkv_fm), fm(out_fm)
        seq = lambda v, b: v[bass.ds(b, 1)].rearrange("o p c t -> p (o c) t")
        stat0 = ps[:, 0:2].rearrange("p (g h) t -> p g h t", g=1)
        stat1 = ps[:, 2:4].rearrange("p (g h) t -> p g h t", g=1)
        low4 = ps[:, 0:4].rearrange("p (g h) t -> p g h t", g=DC)
        flat = lambda a: a.rearrange("p g h t -> p g (h t)")
        STEPS = [(g, qh, kt) for g in range(G4) for qh in range(2) for kt in range(QT)]
        NS = len(STEPS)
        PER_G = NS // G4
        MAXU = 4 * QT * 2
        NCONST = 16 * 9
        PAIRS = [(0, 0), (0, 1), (1, 0), (1, 1), (0, 2), (2, 0)]
        ROWS = HD * len(PAIRS)

        def max_units(step):
            k = step % PER_G
            return range(min(5 * k, MAXU), min(5 * k + 5, MAXU)) if step // PER_G < G4 - 1 else range(0)

        MAX_DONE, MAX_TURN = 12, 13

        @block.sync
        def _(sp):
            rows = lambda a: a.rearrange("(c p) n -> p c n", p=P)
            wide = lambda a: a.rearrange("(a n) -> a n", a=1).broadcast_to([P, a.shape[0]])
            for dst, src in ((wq, rows(p["wq"])), (wk, rows(p["wk"])), (wv, rows(p["wv"])), (wo, rows(p["wo"])),
                             (gw, rows(p["gate_w"])), (gb, wide(p["gate_b"])), (bv, wide(p["bv"])), (cols, p["moe_columns"]), (b2, p["b2"])):
                sp.dma_start(dst[:], src).then_inc(const_in, 16)
            with sp.Fori(0, B) as b:
                sp.wait_ge(stored, b * 16)
                sp.dma_start(XA[:], seq(x_v, b)).then_inc(x_in, 16)
                sp.dma_start(XB[:], seq(r_v, b)).then_inc(x_in, 16)
                for part, ready in enumerate((split_h, split_m, split_l)):
                    for a in range(2):
                        sp.wait_ge(ready, b * 2 + a + 1)
                        sp.dma_start(parts_dram[a, part].rearrange("(c p) t -> p c t", p=P), parts[:, a, part])\
                            .then_inc(parts_out, 16)
                sp.wait_ge(parts_out, (b + 1) * 6 * 16)
                for g in range(G4):
                    for a, stack in enumerate((QS, KS)):
                        for k, pair in enumerate(PAIRS):
                            rows = parts_dram[a, pair[a], 4 * HD * g:4 * HD * (g + 1)]
                            sp.dma_start(stack[HD * k:HD * k + HD, 4 * g:4 * g + 4],
                                         rows.rearrange("(h r) t -> r h t", r=HD)).then_inc(stacked[g], 16)
                for g in range(G4):
                    sp.wait_ge(nmt_out, b * G4 + g + 1)
                    sp.dma_start(nm_dram, NMT).then_inc(nm_out, 16)
                    sp.wait_ge(nm_out, (b * G4 + g + 1) * 16)
                    sp.dma_start(QS[ROWS:ROWS + 3, 4 * g:4 * g + 4], nm_dram.rearrange("(k h) t -> k h t", k=3))\
                        .then_inc(nm_in, 16)

        @block.gpsimd
        def _(pool):
            pool.memset(ident[:], 0.0).then_inc(consts_p, 1)
            pool.memset(sel[:], 0.0).then_inc(consts_p, 1)
            pool.wait_ge(consts_p, 2)
            pool.affine_select(out=ident[:], in_=ident[:], compare_op=ALU.not_equal, fill=1.0, base=0,
                               pattern=[[-1, P]], channel_multiplier=1).then_inc(consts_p, 1)
            pool.affine_select(out=sel[:].rearrange("p (j r) -> p j r", r=SLOT),
                               in_=sel[:].rearrange("p (j r) -> p j r", r=SLOT), compare_op=ALU.not_equal,
                               fill=1.0, base=-HD, pattern=[[-SLOT, 4], [0, SLOT]], channel_multiplier=1)\
                .then_inc(consts_p, 1)
            pool.wait_ge(consts_p, 4)
            pool.tensor_copy(identb[:], ident[:]).then_inc(consts_p, 1)
            with pool.Fori(0, B) as b, pool.Fori(0, NE // 2) as e2:
                for u in range(2):
                    pool.wait_ge(exp_u[u], (b * (NE // 2) + e2) * UNITS)
                    e = e2 * 2 + u
                    pool.dma_start(w1[:, u], p["w1"][bass.ds(e, 1)].rearrange("o (c p) f -> p (o c) f", p=P))\
                        .then_inc(w_in[u], 16)
                    pool.dma_start(w2[:, u], p["w2"][bass.ds(e, 1)].rearrange("o (c p) f -> p (o c) f", p=P))\
                        .then_inc(w_in[u], 16)
                    pool.dma_start(b1[:, u], p["b1_col"][bass.ds(e, 1)].rearrange("o p f -> (o p) f"))\
                        .then_inc(w_in[u], 16)

        def take_output(act, b, o):
            act.wait_ge(pv_mm, b * NS + (o + 1) * QT)
            nc.scalar.activation(OP[:, o // 2, 512 * (o % 2):512 * (o % 2) + 512], ps[:, 7], ACT.Copy)\
                .then_inc(o_out, 1)

        @block.scalar
        def _(act):
            act.wait_ge(consts, CONSTS)
            act.wait_ge(const_in, NCONST)
            with act.Fori(0, B) as b:
                ln_out.act_square(nc, act, b, HN[:], T1[:])
                ln_out.act_std(nc, act, b, stat1, std[:])
                ln_join.act_square(nc, act, b, XA[:], T1[:])
                ln_join.act_std(nc, act, b, stat1, std[:])
                ln1.act_square(nc, act, b, HN[:], T1[:])
                ln1.act_std(nc, act, b, stat1, std[:])
                for a, (dst, bias) in enumerate(((QF, "bq"), (KF, "bk"))):
                    for c in range(DC):
                        act.wait_ge(qk_mm, b * 4 + 2 * a + c + 1)
                        nc.scalar.activation(dst[:, c], ps[:, 2 * c:2 * c + 2].rearrange("p h t -> p (h t)"),
                                             ACT.Identity, bias=col[bias][:, c:c + 1]).then_inc(qk_out, 1)
                    act.wait_ge(qk_out, b * 4 + 2 * a + 2)
                    nc.scalar.activation(parts[:, a, 0], dst[:], ACT.Copy).then_inc(split_h, 1)
                for a, dst in enumerate((QF, KF)):
                    act.wait_ge(split_r, b * 2 + a + 1)
                    nc.scalar.activation(parts[:, a, 1], dst[:], ACT.Copy).then_inc(split_m, 1)
                act.wait_ge(parts_out, (b + 1) * 6 * 16)
                for k, (g, qh, kt) in enumerate(STEPS):
                    for hp in range(2):
                        n = 2 * k + hp
                        act.wait_ge(st_mm, b * 2 * NS + n + 1)
                        if k >= 2:
                            act.wait_ge(pv_mm, b * NS + k - 1)
                        nc.scalar.activation(PT[:, n % 4], ps[:, 3 + 2 * hp:5 + 2 * hp], ACT.Exp, scale=SCALE)\
                            .then_inc(probs, 1)
                    if k % QT == 0 and k > 0:
                        take_output(act, b, k // QT - 1)
                take_output(act, b, 2 * G4 - 1)
                ln2.act_square(nc, act, b, HN[:], T1[:])
                ln2.act_std(nc, act, b, stat1, std[:])
                act.wait_ge(oht_mm, b + 1)
                nc.scalar.activation(OHT, ps[0:NE, 0:2].rearrange("p h t -> p (h t)"), ACT.Copy).then_inc(oht_out, 1)
                for e in range(NE):
                    act.wait_ge(mk_mm, b * NE + e + 1)
                    k = 2 * (e % 2) + 4
                    nc.scalar.activation(MK[:, e], ps[:, k:k + 2].rearrange("p h t -> p (h t)"), ACT.Copy)\
                        .then_inc(mk_out, 1)
                with act.Fori(0, NE // 2) as e2:
                    for u in range(2):
                        ne = b * NE + e2 * 2 + u
                        act.wait_ge(w_in[u], (b * (NE // 2) + e2 + 1) * 48)
                        for k in range(UNITS):
                            act.wait_ge(mid_mm, ne * UNITS + k + 1)
                            nb = b * (NE // 2) + e2
                            if k >= MIDS:
                                act.wait_ge(exp_u[u], nb * UNITS + k - MIDS + 1)
                            elif u == 1:
                                act.wait_ge(exp_u[0], nb * UNITS + k + UNITS - MIDS + 1)
                            else:
                                act.wait_ge(exp_u[1], nb * UNITS)
                            nc.scalar.activation(MID[:, k % MIDS], ps[:, 4 + k % 4], ACT.Relu,
                                                 bias=b1[:, u, k // 2:k // 2 + 1]).then_inc(relu_out, 1)
                ln_end.act_square(nc, act, b, HN[:], T1[:])
                ln_end.act_std(nc, act, b, stat1, std[:])
                act.wait_ge(ln_end.normed, b + 1)
                act.dma_start(seq(o_v, b), HN[:]).then_inc(stored, 16)
            act.wait_ge(stored, B * 16)

        @block.vector
        def _(dve):
            for ins in (nc.vector.memset(eps[:], EPS), nc.vector.memset(ones[:], 1.0 / D)):
                ins.then_inc(consts, 1)
            for e in range(NE):
                nc.vector.memset(order[:, e:e + 1], float(NE - e)).then_inc(consts, 1)
            dve.wait_ge(const_in, NCONST)
            nc.vector.memset(KS[ROWS:P], 1.0).then_inc(ones_set, 1)
            with dve.Fori(0, B) as b:
                own = Steps(dve, vec, VEC_STEPS, b)
                dve.wait_ge(x_in, (b + 1) * 32)
                ln_out.dve_center(nc, dve, b, XB[:], HN[:], stat0)
                ln_out.dve_scale(nc, dve, b, HN[:], std[:], col["ln_out_w"])
                nc.vector.tensor_tensor(XA[:], XA[:], HN[:], ALU.add).then_inc(summed, 1)
                dve.wait_ge(summed, 3 * b + 1)
                ln_join.dve_center(nc, dve, b, XA[:], XA[:], stat0)
                ln_join.dve_scale(nc, dve, b, XA[:], std[:], None)
                ln1.dve_center(nc, dve, b, XA[:], HN[:], stat0)
                ln1.dve_scale(nc, dve, b, HN[:], std[:], col["ln1_g"])
                for c in range(DC):
                    ins = nc.vector.tensor_scalar(HN[:, c], HN[:, c], col["ln1_b"][:, c:c + 1], None, ALU.add)
                ins.then_inc(hn_ready, 1)
                for j in range(QT):
                    dve.wait_ge(v_mm, b * QT + j + 1)
                    nc.vector.tensor_tensor(VP[:, j], ps[:, 4 + j % 4], bv[:], ALU.add).then_inc(v_out, 1)
                for a, src in enumerate((QF, KF)):
                    dve.wait_ge(split_h, b * 2 + a + 1)
                    nc.vector.tensor_tensor(src[:], src[:], parts[:, a, 0], ALU.subtract).then_inc(split_r, 1)
                for a, src in enumerate((QF, KF)):
                    dve.wait_ge(split_m, b * 2 + a + 1)
                    nc.vector.tensor_tensor(parts[:, a, 2], src[:], parts[:, a, 1], ALU.subtract).then_inc(split_l, 1)

                def take_max(g, v):
                    j, qt, kh = v // 16, (v // 2) % QT, v % 2
                    dve.wait_ge(s_mm, (b * G4 + g) * MAXU + v + 1)
                    nc.vector.tensor_reduce(mx[:, qt, kh, 4 * g + j:4 * g + j + 1], ps[:, v % 2], AX.X, ALU.max)\
                        .then_inc(s_max, 1)

                def split_max(g):
                    dve.wait_ge(s_max, (b * G4 + g + 1) * MAXU)
                    if g > 0:
                        dve.wait_ge(nmt_mm, b * G4 + g)
                    own.done(nc.vector.tensor_tensor(mg[:], mx[:, :, 0, 4 * g:4 * g + 4], mx[:, :, 1, 4 * g:4 * g + 4],
                                                     ALU.max))
                    own.done(nc.vector.tensor_scalar(mg[:], mg[:], -1.0, None, ALU.mult))
                    own.done(nc.vector.tensor_copy(NM[:, :, 0], mg[:]))
                    own.done(nc.vector.tensor_tensor(mg[:], mg[:], NM[:, :, 0], ALU.subtract))
                    own.done(nc.vector.tensor_copy(NM[:, :, 1], mg[:]))
                    nc.vector.tensor_tensor(NM[:, :, 2], mg[:], NM[:, :, 1], ALU.subtract).then_inc(nm_ready, 1)

                def take_turned_max(g):
                    dve.wait_ge(nmt_mm, b * G4 + g + 1)
                    if g > 0:
                        dve.wait_ge(nm_in, (b * G4 + g) * 16)
                    nc.vector.tensor_copy(NMT, ps[0:12, 2].bitcast(BF16)).then_inc(nmt_out, 1)

                for v in range(MAXU):
                    take_max(0, v)
                split_max(0)
                take_turned_max(0)
                for k in range(NS):
                    for v in max_units(k):
                        take_max(k // PER_G + 1, v)
                    if k // PER_G < G4 - 1 and k % PER_G == MAX_DONE:
                        split_max(k // PER_G + 1)
                    if k // PER_G < G4 - 1 and k % PER_G == MAX_TURN:
                        take_turned_max(k // PER_G + 1)
                for k in range(G4 * 2):
                    dve.wait_ge(den_mm, b * G4 * 2 + k + 1)
                    inv = T1[:, 0, 512 * (k % 2):512 * (k % 2) + 512]
                    own.done(nc.vector.reciprocal(inv, ps[:, k % 4]))
                    o = OP[:, k // 2, 512 * (k % 2):512 * (k % 2) + 512]
                    nc.vector.tensor_tensor(o, o, inv, ALU.mult).then_inc(o_normed, 1)
                dve.wait_ge(wo_mm, b + 1)
                for c in range(DC):
                    ins = nc.vector.scalar_tensor_tensor(XB[:, c], flat(low4)[:, c], col["bo"][:, c:c + 1], XA[:, c],
                                                         ALU.add, ALU.add)
                ins.then_inc(xb_ready, 1)
                dve.wait_ge(xb_ready, b + 1)
                ln2.dve_center(nc, dve, b, XB[:], HN[:], stat0)
                ln2.dve_scale(nc, dve, b, HN[:], std[:], col["ln2_g"])
                for c in range(DC):
                    ins = nc.vector.tensor_scalar(HN[:, c], HN[:, c], col["ln2_b"][:, c:c + 1], None, ALU.add)
                ins.then_inc(hn2_ready, 1)
                nc.vector.tensor_tensor(XB[:], XB[:], XA[:], ALU.add).then_inc(summed, 1)
                dve.wait_ge(lg_mm, b + 1)
                lg = ps[:, 0, 0:QT * NE].rearrange("p (q e) -> p q e", e=NE)
                own.done(nc.vector.tensor_tensor(LG[:], lg, gb[:].rearrange("p (o e) -> p o e", o=1)
                                                 .broadcast_to([P, QT, NE]), ALU.add))
                wide = lambda t: t[:].rearrange("p (q o) -> p q o", o=1).broadcast_to([P, QT, NE])
                own.done(nc.vector.tensor_reduce(top[:], LG[:], AX.X, ALU.max))
                own.done(nc.vector.tensor_tensor(OH[:], LG[:], wide(top), ALU.is_ge))
                own.done(nc.vector.tensor_tensor(LG[:], OH[:], order[:].rearrange("p (o e) -> p o e", o=1)
                                                 .broadcast_to([P, QT, NE]), ALU.mult))
                own.done(nc.vector.tensor_reduce(top[:], LG[:], AX.X, ALU.max))
                own.done(nc.vector.tensor_tensor(OH[:], LG[:], wide(top), ALU.is_equal))
                nc.vector.tensor_copy(OHB[:], OH[:]).then_inc(oh_ready, 1)
                with dve.Fori(0, NE // 2) as e2:
                    for u in range(2):
                        ne = b * NE + e2 * 2 + u
                        dve.wait_ge(mk_out, (b + 1) * NE)
                        for k in range(UNITS):
                            dve.wait_ge(relu_out, ne * UNITS + k + 1)
                            m = MID[:, k % MIDS]
                            mask = MK[:, bass.ds(e2 * 2 + u, 1), 512 * (k % 2):512 * (k % 2) + 512]\
                                .rearrange("p o t -> p (o t)")
                            nc.vector.tensor_tensor(m, m, mask, ALU.mult).then_inc(mid_ready, 1)
                dve.wait_ge(exp_u[1], (b + 1) * (NE // 2) * UNITS)
                dve.wait_ge(summed, 3 * b + 2)
                nc.vector.tensor_tensor(XB[:], XB[:], flat(low4), ALU.add).then_inc(summed, 1)
                dve.wait_ge(summed, 3 * b + 3)
                ln_end.dve_center(nc, dve, b, XB[:], HN[:], stat0)
                ln_end.dve_scale(nc, dve, b, HN[:], std[:], None)
                own.close()

        @block.tensor
        def _(pe):
            pe.wait_ge(consts, CONSTS)
            pe.wait_ge(consts_p, 5)
            pe.wait_ge(const_in, NCONST)
            pe.wait_ge(ones_set, 1)
            with pe.Fori(0, B) as b:
                pe.wait_ge(x_in, (b + 1) * 32)
                ln_out.pe_mean(nc, pe, b, XB, stat0)
                ln_out.pe_var(nc, pe, b, T1, stat1)
                pe.wait_ge(summed, 3 * b + 1)
                ln_join.pe_mean(nc, pe, b, XA, stat0)
                ln_join.pe_var(nc, pe, b, T1, stat1)
                pe.wait_ge(ln_join.normed, b + 1)
                ln1.pe_mean(nc, pe, b, XA, stat0)
                ln1.pe_var(nc, pe, b, T1, stat1)
                pe.wait_ge(hn_ready, b + 1)
                for a, w in enumerate((wq, wk)):
                    for c in range(DC):
                        if a == 1:
                            pe.wait_ge(qk_out, b * 4 + c + 1)
                        for half in range(2):
                            for k in range(DC):
                                ins = nc.tensor.matmul(ps[:, 2 * c + half], w[:, k, c * P:(c + 1) * P],
                                                       HN[:, k, 512 * half:512 * half + 512],
                                                       start=(k == 0), stop=(k == DC - 1))
                        ins.then_inc(qk_mm, 1)
                for j in range(QT):
                    if j >= 4:
                        pe.wait_ge(v_out, b * QT + j - 3)
                    for c in range(DC):
                        ins = nc.tensor.matmul(ps[:, 4 + j % 4], HN[:, c, j * P:(j + 1) * P], wv[:, c],
                                               start=(c == 0), stop=(c == DC - 1))
                    ins.then_inc(v_mm, 1)
                pe.wait_ge(qk_out, (b + 1) * 4)
                pe.wait_ge(v_out, (b + 1) * QT)

                def scores_for_max(g, v):
                    j, qt, kh = v // 16, (v // 2) % QT, v % 2
                    if v == 0:
                        pe.wait_ge(stacked[g], (b + 1) * STACKS)
                    if g > 0 or v >= 2:
                        pe.wait_ge(s_max, (b * G4 + g) * MAXU + v - 1)
                    nc.tensor.matmul(ps[:, v % 2], QS[0:ROWS, 4 * g + j, qt * P:(qt + 1) * P],
                                     KS[0:ROWS, 4 * g + j, 512 * kh:512 * kh + 512], start=True, stop=True)\
                        .then_inc(s_mm, 1)

                def turn_max(g):
                    pe.wait_ge(nm_ready, b * G4 + g + 1)
                    if g > 0:
                        pe.wait_ge(nmt_out, b * G4 + g)
                    for qt in range(QT):
                        ins = nc.tensor.transpose(ps[0:12, 2].bitcast(BF16)[:, qt * P:(qt + 1) * P],
                                                  NM[:, qt].rearrange("p a h -> p (a h)"), identb[:])
                    ins.then_inc(nmt_mm, 1)

                def transposed_scores(k):
                    g, qh, kt = STEPS[k]
                    if k % PER_G == 0:
                        pe.wait_ge(nm_in, (b * G4 + g + 1) * 16)
                    for hp in range(2):
                        if k >= 1:
                            pe.wait_ge(probs, b * 2 * NS + 2 * k + hp - 1)
                        for a in range(2):
                            h = 4 * g + 2 * hp + a
                            ins = nc.tensor.matmul(ps[:, 3 + 2 * hp + a], KS[0:ROWS + 3, h, kt * P:(kt + 1) * P],
                                                   QS[0:ROWS + 3, h, 512 * qh:512 * qh + 512], start=True, stop=True)
                        ins.then_inc(st_mm, 1)

                def values(k):
                    g, qh, kt = STEPS[k]
                    if kt == 0 and k > 0:
                        pe.wait_ge(o_out, b * 2 * G4 + k // QT)
                    pe.wait_ge(probs, b * 2 * NS + 2 * k + 2)
                    for j in range(4):
                        r0 = SLOT * j
                        ins = nc.tensor.matmul(ps[r0:r0 + SLOT, 7], VP[:, kt, g * P + r0:g * P + r0 + SLOT],
                                               PT[:, (2 * k + j // 2) % 4, j % 2], start=(kt == 0),
                                               stop=(kt == QT - 1), tile_position=(0, r0), skip_group_check=True)
                    ins.then_inc(pv_mm, 1)

                for v in range(MAXU):
                    scores_for_max(0, v)
                turn_max(0)
                for k in range(NS + 1):
                    if k < NS:
                        transposed_scores(k)
                        for v in max_units(k):
                            scores_for_max(k // PER_G + 1, v)
                        if k // PER_G < G4 - 1 and k % PER_G == MAX_TURN:
                            turn_max(k // PER_G + 1)
                    if k >= 1:
                        values(k - 1)
                for k in range(G4 * 2):
                    pe.wait_ge(o_out, b * 2 * G4 + k + 1)
                    if k >= 4:
                        pe.wait_ge(o_normed, b * 2 * G4 + k - 3)
                    nc.tensor.matmul(ps[:, k % 4], sel[:], OP[:, k // 2, 512 * (k % 2):512 * (k % 2) + 512],
                                     start=True, stop=True).then_inc(den_mm, 1)
                pe.wait_ge(o_normed, (b + 1) * 2 * G4)
                for m in range(DC):
                    for half in range(2):
                        for g in range(G4):
                            ins = nc.tensor.matmul(low4[:, m, half], wo[:, g, m * P:(m + 1) * P],
                                                   OP[:, g, 512 * half:512 * half + 512],
                                                   start=(g == 0), stop=(g == G4 - 1))
                ins.then_inc(wo_mm, 1)
                pe.wait_ge(xb_ready, b + 1)
                ln2.pe_mean(nc, pe, b, XB, stat0)
                ln2.pe_var(nc, pe, b, T1, stat1)
                pe.wait_ge(hn2_ready, b + 1)
                for qt in range(QT):
                    for c in range(DC):
                        ins = nc.tensor.matmul(ps[:, 0, NE * qt:NE * qt + NE], HN[:, c, qt * P:(qt + 1) * P], gw[:, c],
                                               start=(c == 0), stop=(c == DC - 1))
                ins.then_inc(lg_mm, 1)
                pe.wait_ge(oh_ready, b + 1)
                for qt in range(QT):
                    ins = nc.tensor.transpose(ps[0:NE, qt // 4, P * (qt % 4):P * (qt % 4) + P], OH[:, qt], ident[:])
                ins.then_inc(oht_mm, 1)
                for e in range(NE):
                    if e >= 2:
                        pe.wait_ge(mk_out, b * NE + e - 1)
                    for qt in range(QT):
                        ins = nc.tensor.matmul(ps[:, 4 + 2 * (e % 2) + qt // 4, P * (qt % 4):P * (qt % 4) + P],
                                               OHB[:, qt, e:e + 1].broadcast_to([P, P]), identb[:],
                                               start=True, stop=True)
                    ins.then_inc(mk_mm, 1)
                pe.wait_ge(oht_out, b + 1)
                for m in range(DC):
                    for half in range(2):
                        nc.tensor.matmul(low4[:, m, half], b2[:, m * P:(m + 1) * P],
                                         OHT[:, 512 * half:512 * half + 512], start=True, stop=False,
                                         skip_group_check=True)
                with pe.Fori(0, NE // 2) as e2:
                    for u in range(2):
                        ne = b * NE + e2 * 2 + u
                        pe.wait_ge(mk_out, (b + 1) * NE)
                        pe.wait_ge(w_in[u], (b * (NE // 2) + e2 + 1) * 48)

                        def hidden(k):
                            f, half = k // 2, k % 2
                            if k >= 4:
                                pe.wait_ge(relu_out, ne * UNITS + k - 3)
                            else:
                                pe.wait_ge(relu_out, ne * UNITS)
                            for c in range(DC):
                                ins = nc.tensor.matmul(ps[:, 4 + k % 4], w1[:, u, c, f * P:(f + 1) * P],
                                                       HN[:, c, 512 * half:512 * half + 512],
                                                       start=(c == 0), stop=(c == DC - 1))
                            ins.then_inc(mid_mm, 1)

                        def back(k):
                            f, half = k // 2, k % 2
                            pe.wait_ge(mid_ready, ne * UNITS + k + 1)
                            for m in range(DC):
                                ins = nc.tensor.matmul(low4[:, m, half], w2[:, u, f, m * P:(m + 1) * P],
                                                       MID[:, k % MIDS], start=False, stop=True,
                                                       skip_group_check=True)
                            ins.then_inc(exp_u[u], 1)
                            return ins

                        for k in range(UNITS + 3):
                            if k < UNITS:
                                hidden(k)
                            if k >= 3:
                                back(k - 3)
                pe.wait_ge(summed, 3 * b + 3)
                ln_end.pe_mean(nc, pe, b, XB, stat0)
                ln_end.pe_var(nc, pe, b, T1, stat1)


def slots(a, mark=0.0):
    out = np.zeros(a.shape[:-1] + (16, 32), a.dtype)
    out[..., 0:16] = np.reshape(a, a.shape[:-1] + (16, 16))
    out[..., 16] = mark
    return out.reshape(a.shape[:-1] + (512,))


def moe_inputs(i):
    f = lambda k: i["L0_ffn_" + k]
    out = {k: f(k) for k in ("wq", "wk", "gate_w", "gate_b", "b2", "w1", "w2")}
    out["wv"], out["bv"], out["wo"] = slots(f("wv")), slots(f("bv"), 1.0), slots(f("wo").T).T
    vectors = [i["L0_attn_ln_out_w"]] + [f(k) for k in MOE_COLUMNS[1:]]
    out["moe_columns"] = np.stack([a.reshape(DC, P).T for a in vectors], 1)
    out["b1_col"] = f("b1").reshape(8, 8, P).transpose(0, 2, 1)
    return {k: np.ascontiguousarray(v) for k, v in out.items()}


def quantized_mlp(nc, x_tm, w_gate, w_up, w_down, out_tm):
    F = w_gate.shape[0]
    BLK = 16
    WR = 8
    WP = F // WR
    FULL = F // P
    FK = [P] * FULL + ([F - FULL * P] if F % P else [])
    NK = len(FK)
    U = 2
    NI = N // P // U
    MID_HIGH = (5.0, 3.5, 2.5)
    MID_LOW = (1.75, 1.25, 0.75, 0.25)
    QUANT_STEPS = 9

    with ExitStack() as ctx:
        sb, psum, sem = allocators(nc, ctx, "qm")
        wg_r = sb("wg_r", [WP, WR, D])
        wu_r = sb("wu_r", [WP, WR, D])
        wd_r = sb("wd_r", [P, DC, F])
        wT = sb("wT", [P, 2, DC, F])
        wdT = sb("wdT", [P, NK, D])
        ident = sb("ident", [P, P])
        eps = sb("eps", [P, 1])
        x = sb("x", [P, U, D])
        xq = sb("xq", [P, U, D])
        xqT = sb("xqT", [P, U, D])
        th = sb("th", [P, U, F])
        h = sb("h", [P, U, F])
        hqT = sb("hqT", [P, U, NK, P])
        FMAX = WR * D
        qn = sb("qn", [P, FMAX])
        qa = sb("qa", [P, FMAX])
        qs = sb("qs", [P, FMAX])
        qt = sb("qt", [P, FMAX])
        amax = sb("amax", [P, FMAX // BLK])
        rsc = sb("rsc", [P, FMAX // BLK])
        y = sb("y", [P, U, D])
        stats = sb("stats", [P, 6])
        spare = sb("spare", [P, 1])
        mv = sb("mv", [P, U, 2])
        std = sb("std", [P, U])
        rstd = sb("rstd", [P, U])
        yn = sb("yn", [P, U, D])
        gate = psum("gate", [P, 1024])
        up = psum("up", [P, 1024])
        xt_ps = psum("xt_ps", [P, 512])
        ht_ps = psum("ht_ps", [P, 1024])
        y_ps = psum("y_ps", [P, 512])
        y_of = [y_ps[:, 0:D], xt_ps[:, D:2 * D]]
        turn_ps = [gate[:, 0:512], gate[:, 512:1024], up[:, 0:512], up[:, 512:1024]]

        weights_in = sem("weights_in")
        consts = sem("consts")
        eps_set = sem("eps_set")
        wvec = sem("wvec")
        w_scaled = sem("w_scaled")
        w_signed = sem("w_signed")
        w_quant = sem("w_quant")
        w_mm = sem("w_mm")
        w_out = sem("w_out")
        x_in = [sem(f"x_in{u}") for u in range(U)]
        q_scaled = sem("q_scaled")
        q_signed = sem("q_signed")
        xq_ready = sem("xq_ready")
        xT_mm = sem("xT_mm")
        xT_out = sem("xT_out")
        gate_mm = sem("gate_mm")
        tanh_out = sem("tanh_out")
        h_ready = sem("h_ready")
        hq_ready = sem("hq_ready")
        hT_mm = sem("hT_mm")
        hT_out = sem("hT_out")
        y_mm = sem("y_mm")
        y_ready = sem("y_ready")
        var_ready = sem("var_ready")
        std_ready = sem("std_ready")
        yn_ready = sem("yn_ready")
        stored = [sem(f"stored{u}") for u in range(U)]
        vec = sem("vec")
        block = ctx.enter_context(nc.Block())

        W_JOBS = [(wg_r, WP, FMAX), (wu_r, WP, FMAX), (wd_r, P, DC * F)]
        W_TURNS = []
        for k, w_r in enumerate((wg_r, wu_r)):
            for r in range(WR):
                for c in range(DC):
                    W_TURNS.append((w_r[:, r, c * P:(c + 1) * P], WP, P, wT[:, k, c, r:F:WR], k))
        for c in range(DC):
            for k in range(NK):
                W_TURNS.append((wd_r[:, c, k * P:k * P + FK[k]], P, FK[k], wdT[0:FK[k], k, c * P:(c + 1) * P], 2))

        @block.sync
        def _(sp):
            sp.dma_start(wg_r[:], w_gate.rearrange("(p r) k -> p r k", r=WR)).then_inc(weights_in, 16)
            sp.dma_start(wu_r[:], w_up.rearrange("(p r) k -> p r k", r=WR)).then_inc(weights_in, 16)
            sp.dma_start(wd_r[:], w_down.rearrange("(c p) k -> p c k", p=P)).then_inc(weights_in, 16)
            with sp.Fori(0, NI) as i:
                for u in range(U):
                    sp.wait_ge(y_ready, i * U)
                    sp.dma_start(x[:, u], x_tm[bass.ds((i * U + u) * P, P), :]).then_inc(x_in[u], 16)

        @block.gpsimd
        def _(pool):
            pool.memset(ident[:], 0.0).then_inc(consts, 1)
            pool.wait_ge(consts, 1)
            pool.affine_select(out=ident[:], in_=ident[:], compare_op=ALU.not_equal, fill=1.0, base=0,
                               pattern=[[-1, P]], channel_multiplier=1).then_inc(consts, 1)

        def round_fp4(own, src, dst, rows, n, scaled, signed, at):
            nb = n // BLK
            blocks = lambda t: t.rearrange("p (b k) -> p b k", k=BLK)
            wide = lambda t: t.rearrange("p (b o) -> p b o", o=1).broadcast_to([rows, nb, BLK])
            own.done(nc.vector.tensor_reduce(amax[0:rows, 0:nb], blocks(src), AX.X, ALU.max,
                                             apply_absolute_value=True))
            own.done(nc.vector.tensor_scalar(amax[0:rows, 0:nb], amax[0:rows, 0:nb], 1.0 / 6.0, 1e-12,
                                             ALU.mult, ALU.max))
            own.done(nc.vector.reciprocal(rsc[0:rows, 0:nb], amax[0:rows, 0:nb]))
            nc.vector.tensor_tensor(blocks(qn[0:rows, 0:n]), blocks(src), wide(rsc[0:rows, 0:nb]),
                                    ALU.mult).then_inc(scaled, 1)
            own.eng.wait_ge(signed, at + 1)
            a, t = qa[0:rows, 0:n], qt[0:rows, 0:n]
            own.done(nc.vector.tensor_scalar(t, a, MID_HIGH[0], 2.0, ALU.is_gt, ALU.mult))
            for m in MID_HIGH[1:]:
                own.done(nc.vector.scalar_tensor_tensor(t, a, m, t, ALU.is_gt, ALU.add))
            own.done(nc.vector.tensor_scalar(t, t, 2.0, None, ALU.mult))
            for m in MID_LOW:
                own.done(nc.vector.scalar_tensor_tensor(t, a, m, t, ALU.is_gt, ALU.add))
            own.done(nc.vector.scalar_tensor_tensor(blocks(qs[0:rows, 0:n]), blocks(qs[0:rows, 0:n]), 0.5,
                                                    wide(amax[0:rows, 0:nb]), ALU.mult, ALU.mult))
            return nc.vector.tensor_tensor(dst, t, qs[0:rows, 0:n], ALU.mult)

        def magnitude_and_sign(act, rows, n, scaled, signed, at):
            act.wait_ge(scaled, at + 1)
            nc.scalar.activation(qa[0:rows, 0:n], qn[0:rows, 0:n], ACT.Abs)
            nc.scalar.activation(qs[0:rows, 0:n], qn[0:rows, 0:n], ACT.Sign).then_inc(signed, 1)

        @block.scalar
        def _(act):
            for k, (w_r, rows, n) in enumerate(W_JOBS):
                magnitude_and_sign(act, rows, n, w_scaled, w_signed, k)
            with act.Fori(0, NI) as i:
                for u in range(U):
                    n = i * U + u
                    magnitude_and_sign(act, P, D, q_scaled, q_signed, i * 2 * U + u)
                    act.wait_ge(xT_mm, n + 1)
                    nc.scalar.activation(xqT[:, u], xt_ps[:, 0:D], ACT.Copy).then_inc(xT_out, 1)
                    act.wait_ge(gate_mm, n + 1)
                    nc.scalar.activation(th[:, u], gate[:, 0:F], ACT.Tanh, scale=0.5).then_inc(tanh_out, 1)
                for u in range(U):
                    n = i * U + u
                    magnitude_and_sign(act, P, F, q_scaled, q_signed, i * 2 * U + U + u)
                    act.wait_ge(hT_mm, n + 1)
                    nc.scalar.activation(hqT[:, u, 0:FULL].rearrange("p k t -> p (k t)"), ht_ps[:, 0:FULL * P],
                                         ACT.Copy)
                    nc.scalar.activation(hqT[0:FK[-1], u, NK - 1], ht_ps[0:FK[-1], FULL * P:NK * P],
                                         ACT.Copy).then_inc(hT_out, 1)
                act.wait_ge(var_ready, (i + 1) * U)
                nc.scalar.activation(std[:], mv[:, :, 1], ACT.Sqrt, bias=eps[:, 0:1]).then_inc(std_ready, 1)
                for u in range(U):
                    act.wait_ge(yn_ready, i * U + u + 1)
                    act.dma_start(out_tm[bass.ds((i * U + u) * P, P), :], yn[:, u]).then_inc(stored[u], 16)
            for u in range(U):
                act.wait_ge(stored[u], 16 * NI)

        @block.vector
        def _(dve):
            nc.vector.memset(eps[:], EPS).then_inc(eps_set, 1)
            dve.wait_ge(weights_in, 16 * 3)
            own = Steps(dve, wvec, 3 * (3 + QUANT_STEPS), 0)
            for k, (w_r, rows, n) in enumerate(W_JOBS):
                flat = w_r[:].rearrange("p r k -> p (r k)")
                round_fp4(own, flat, flat, rows, n, w_scaled, w_signed, k).then_inc(w_quant, 1)
                dve.wait_ge(w_quant, k + 1)
            for k, (src, kp, m, dst, job) in enumerate(W_TURNS):
                dve.wait_ge(w_mm, k + 1)
                nc.vector.tensor_copy(dst, turn_ps[k % 4][0:m, 0:kp]).then_inc(w_out, 1)
            with dve.Fori(0, NI) as i:
                own = Steps(dve, vec, U * (2 * (3 + QUANT_STEPS) + 2) + 1, i)
                for u in range(U):
                    dve.wait_ge(x_in[u], 16 * (i + 1))
                    round_fp4(own, x[:, u], xq[:, u], P, D, q_scaled, q_signed, i * 2 * U + u)\
                        .then_inc(xq_ready, 1)
                    dve.wait_ge(xq_ready, i * U + u + 1)
                    dve.wait_ge(tanh_out, i * U + u + 1)
                    own.done(nc.vector.scalar_tensor_tensor(h[:, u], th[:, u], 1.0, gate[:, 0:F], ALU.add,
                                                            ALU.mult))
                    nc.vector.scalar_tensor_tensor(h[:, u], h[:, u], 0.5, up[:, 0:F], ALU.mult, ALU.mult)\
                        .then_inc(h_ready, 1)
                dve.wait_ge(h_ready, (i + 1) * U)
                for u in range(U):
                    round_fp4(own, h[:, u], h[:, u], P, F, q_scaled, q_signed, i * 2 * U + U + u)\
                        .then_inc(hq_ready, 1)
                    dve.wait_ge(hq_ready, i * U + u + 1)
                for u in range(U):
                    dve.wait_ge(y_mm, i * U + u + 1)
                    nc.vector.tensor_tensor(y[:, u], x[:, u], y_of[u], ALU.add).then_inc(y_ready, 1)
                    dve.wait_ge(y_ready, i * U + u + 1)
                    own.done(nc.vector.bn_stats(stats[:], y[:, u]))
                    nc.vector.memset(spare[:], 0.0)
                    nc.vector.bn_aggr(mv[:, u], stats[:]).then_inc(var_ready, 1)
                    dve.wait_ge(var_ready, i * U + u + 1)
                dve.wait_ge(std_ready, i + 1)
                own.done(nc.vector.reciprocal(rstd[:], std[:]))
                for u in range(U):
                    dve.wait_ge(stored[u], 16 * i)
                    nc.vector.tensor_scalar(yn[:, u], y[:, u], mv[:, u, 0:1], rstd[:, u:u + 1], ALU.subtract,
                                            ALU.mult).then_inc(yn_ready, 1)
                own.close()

        @block.tensor
        def _(pe):
            pe.wait_ge(consts, 2)
            for k, (src, kp, m, dst, job) in enumerate(W_TURNS):
                pe.wait_ge(w_quant, job + 1)
                if k >= 4:
                    pe.wait_ge(w_out, k - 3)
                nc.tensor.transpose(turn_ps[k % 4][0:m, 0:kp], src, ident[0:kp, 0:kp])\
                    .then_inc(w_mm, 1)
            pe.wait_ge(w_out, len(W_TURNS))
            with pe.Fori(0, NI) as i:
                for u in range(U):
                    n = i * U + u
                    pe.wait_ge(xq_ready, n + 1)
                    pe.wait_ge(xT_out, n)
                    pe.wait_ge(y_ready, i * U)
                    for c in range(DC):
                        ins = nc.tensor.transpose(xt_ps[:, c * P:(c + 1) * P], xq[:, u, c * P:(c + 1) * P], ident[:])
                    ins.then_inc(xT_mm, 1)
                    pe.wait_ge(xT_out, n + 1)
                    pe.wait_ge(h_ready, n)
                    for k, dst in ((0, gate), (1, up)):
                        for lo, hi in ((0, 512), (512, F)):
                            for c in range(DC):
                                ins = nc.tensor.matmul(dst[:, lo:hi], xqT[:, u, c * P:(c + 1) * P],
                                                       wT[:, k, c, lo:hi], start=(c == 0), stop=(c == DC - 1))
                    ins.then_inc(gate_mm, 1)
                for u in range(U):
                    n = i * U + u
                    pe.wait_ge(hq_ready, n + 1)
                    pe.wait_ge(hT_out, n)
                    for k in range(NK):
                        ins = nc.tensor.transpose(ht_ps[0:FK[k], k * P:(k + 1) * P], h[:, u, k * P:k * P + FK[k]],
                                                  ident[:])
                    ins.then_inc(hT_mm, 1)
                    pe.wait_ge(hT_out, n + 1)
                    pe.wait_ge(y_ready, i * U)
                    for k in range(NK):
                        ins = nc.tensor.matmul(y_of[u], hqT[0:FK[k], u, k], wdT[0:FK[k], k],
                                               start=(k == 0), stop=(k == NK - 1))
                    ins.then_inc(y_mm, 1)


def rwkv_inputs(i):
    f = lambda k: i["L0_attn_" + k]
    names = ["tm_w1", "tm_w2", "td_w1", "td_w2", "Wr", "Wk", "Wv", "Wo", "Wg", "cWk", "cWv", "cWr"]
    out = {k: f(k) for k in names}
    out["columns"] = np.stack([f(k).reshape(2, DC, P).transpose(0, 2, 1) for k in RWKV_COLUMNS], 2)
    key, query = np.arange(P)[:, None], np.arange(P)[None]
    levels = [key == query]
    for m in (1, 2, 4, 8, 16, 32, 64):
        levels.append((key // (2 * m) == query // (2 * m)) & (key // m % 2 == 0) & (query // m % 2 == 1))
    out["masks"] = np.array(levels, np.float32)
    return {k: np.ascontiguousarray(v) for k, v in out.items()}


def program(nc, x_fm, rwkv_in, moe_in, fa_in, qm_in, work, out):
    rwkv(nc, x_fm, rwkv_in["masks"], rwkv_in, work[0])
    attention_moe(nc, x_fm, work[0], moe_in, work[1])
    feature_attention(nc, work[1], *fa_in, work[2])
    quantized_mlp(nc, work[2], *qm_in, out)


def kernel(**inputs):
    import concourse.bacc as _bacc
    from concourse.bass_utils import run_bass_kernel_spmd as _run

    nc = _bacc.Bacc("TRN2", target_bir_lowering=False, num_devices=1)
    i = {k: np.asarray(v) for k, v in inputs.items()}
    arrays = {}

    def inn(name, a):
        name = "in_" + name
        arrays[name] = np.ascontiguousarray(a)
        return nc.dram_tensor(name, a.shape, mybir.dt.from_np(a.dtype), kind="ExternalInput").ap()

    x_fm = inn("x_fm", i["L0_attn_x"].reshape(N, D).T)
    rwkv_in = {k: inn("rwkv_" + k, a) for k, a in rwkv_inputs(i).items()}
    moe_in = {k: inn("moe_" + k, a) for k, a in moe_inputs(i).items()}
    fa_in = [inn("fa_" + k, i["L1_attn_" + k]) for k in ("Wq", "bq", "Wk", "bk", "Wv", "bv", "Wo", "bo")]
    qm_in = [inn("qm_" + k, i["L1_ffn_" + k]) for k in ("w_gate", "w_up", "w_down")]
    work = [nc.dram_tensor(f"work{k}", (D, N) if k < 2 else (N, D), F32, kind="Internal").ap() for k in range(3)]
    out = nc.dram_tensor("out", (N, D), F32, kind="ExternalOutput").ap()
    program(nc, x_fm, rwkv_in, moe_in, fa_in, qm_in, work, out)
    r = _run(nc, [arrays], core_ids=[0])
    return r.results[0]["out"].reshape(B, T, D)
```

```python
from contextlib import ExitStack

import numpy as np
import concourse.bass as bass
from concourse import mybir

F32 = mybir.dt.float32
BF16 = mybir.dt.bfloat16
U8 = mybir.dt.uint8
ALU = mybir.AluOpType
ACT = mybir.ActivationFunctionType
AX = mybir.AxisListType

P = 128
B, T, D = 4, 1024, 256
DC = D // P
N = B * T
EPS = 1e-5
BIG = 3.0e38


class Steps:

    def __init__(self, eng, sem, per_pass, n):
        self.eng, self.sem, self.per, self.n, self.k = eng, sem, per_pass, n, 0

    def done(self, ins):
        self.k += 1
        ins.then_inc(self.sem, 1)
        self.eng.wait_ge(self.sem, self.n * self.per + self.k)

    def close(self):
        assert self.k == self.per, (self.k, self.per)


def allocators(nc, ctx, tag):
    def sb(name, shape, dt=F32):
        return ctx.enter_context(nc.sbuf_tensor(f"{tag}_{name}", shape, dt))

    def psum(name, shape, dt=F32):
        return ctx.enter_context(nc.psum_tensor(f"{tag}_{name}", shape, dt))

    held = []

    def clear():
        nc.clear_and_free_semaphores(held)
        nc.all_engine_barrier()

    ctx.callback(clear)

    def sem(name):
        held.append(nc.alloc_semaphore(f"{tag}_{name}"))
        return held[-1]

    return sb, psum, sem


def feature_attention(nc, x_fm, wq, bq, wk, bk, wv, bv, wo, bo, out_tm):
    H, C = 16, 64
    HID = H * C
    TILES = N // P
    HC = HID // P
    NG = 12
    ROWS = sum(C - j for j in range(0, C, 2)) // NG
    GROUP_COLS = ROWS * 2 * H
    groups, left = [], list(range(0, C, 2))
    while left:
        runs, used = [], 0
        for j in list(left):
            if used + C - j <= ROWS:
                runs.append((j, used * 2 * H, C - j))
                used += C - j
                left.remove(j)
        assert used == ROWS
        groups.append(runs)
    assert len(groups) == NG
    SB = TB = 4
    assert NG % SB == 0
    LAG = 3
    AT_TURN, AT_OUT, AT_K, AT_Q, AT_V = 2, 3, 5, 6, 8
    AT_SUMS, AT_STD, AT_NORM, AT_STORE = 1, 8, 10, 11

    with ExitStack() as ctx:
        sb, psum, sem = allocators(nc, ctx, "fa")
        wq_sb = sb("wq", [P, DC, HID])
        wk_sb = sb("wk", [P, DC, HID])
        wv_sb = sb("wv", [P, DC, HID])
        wo_sb = sb("wo", [P, HC, D])
        bq_sb = sb("bq", [P, HID])
        bk_sb = sb("bk", [P, HID])
        bv_sb = sb("bv", [P, HID])
        bo_sb = sb("bo", [P, D])
        ident = sb("ident", [P, P])
        lift = sb("lift", [P, 2, HID])
        eps = sb("eps", [P, 1])
        xT = sb("xT", [P, 2, DC, P])
        Q = sb("Q", [P, 2, HID])
        K = sb("K", [P, 2, HID])
        V = sb("V", [P, 2, HID])
        kmax = sb("kmax", [P, HID])
        kmin = sb("kmin", [P, HID])
        M = sb("M", [P, 2, HID])
        S = sb("S", [P, SB, GROUP_COLS])
        PV = sb("PV", [P, TB, GROUP_COLS])
        nums = sb("nums", [P, HID])
        dens = sb("dens", [P, HID])
        att = dens
        attT = sb("attT", [P, HC, P])
        y = sb("y", [P, D])
        stats = sb("stats", [P, 6])
        mv = sb("mv", [P, 2])
        spare = sb("spare", [P, 1])
        logv = sb("logv", [P, 1])
        rstd = sb("rstd", [P, 1])
        yn = sb("yn", [P, 2, D])

        num = psum("num", [P, HID])
        den = psum("den", [P, HID])
        pa = psum("pa", [P, HID])
        pb = psum("pb", [P, HID])

        weights_in = sem("weights_in")
        consts = sem("consts")
        consts_v = sem("consts_v")
        x_in = [sem("x_in0"), sem("x_in1")]
        x_used = sem("x_used")
        q_mm = sem("q_mm")
        k_mm = sem("k_mm")
        v_mm = sem("v_mm")
        q_out = sem("q_out")
        k_out = sem("k_out")
        v_out = sem("v_out")
        scanned = sem("scanned")
        extremes = sem("extremes")
        max_ready = sem("max_ready")
        scores = sem("scores")
        shifted = sem("shifted")
        probs = sem("probs")
        products = sem("products")
        weighted = sem("weighted")
        den_used = sem("den_used")
        num_used = sem("num_used")
        sums_out = sem("sums_out")
        dens_inverted = sem("dens_inverted")
        att_ready = sem("att_ready")
        attT_mm = sem("attT_mm")
        attT_out = sem("attT_out")
        y_mm = sem("y_mm")
        y_taken = sem("y_taken")
        y_ready = sem("y_ready")
        stats_ready = sem("stats_ready")
        var_ready = sem("var_ready")
        log_ready = sem("log_ready")
        inverted = sem("inverted")
        yn_ready = sem("yn_ready")
        stored = [sem("stored0"), sem("stored1")]
        block = ctx.enter_context(nc.Block())

        def over_tiles(eng, tile):
            tile(0, 0, True, False)
            with eng.Fori(0, TILES // 2 - 1) as i:
                tile(i * 2 + 1, 1, False, False)
                tile(i * 2 + 2, 0, False, False)
            tile(TILES - 1, 1, False, True)

        def run_of(buf, slot, run):
            j, at, w = run
            return buf[:, slot, at:at + 2 * H * w].rearrange("p (a h w) -> p a h w", a=2, h=H)

        def by_head(t):
            return t.rearrange("p (h c) -> p h c", h=H)

        def over_rows(t, u, j):
            return by_head(t[:, u])[:, :, j:C].rearrange("p (a h) w -> p a h w", a=1).broadcast_to([P, 2, H, C - j])

        def key_column(t, u, j):
            return t[:, u].rearrange("p (h c o) -> p c h o", h=H, o=1)[:, j:j + 2].broadcast_to([P, 2, H, C - j])

        x_v = x_fm.rearrange("(c p) t -> p c t", p=P)

        @block.sync
        def _(sp):
            for w_sb, w in ((wk_sb, wk), (wq_sb, wq), (wv_sb, wv), (wo_sb, wo)):
                sp.dma_start(w_sb[:], w.rearrange("(c p) n -> p c n", p=P)).then_inc(weights_in, 16)
            for b_sb, b_ in ((bq_sb, bq), (bk_sb, bk), (bv_sb, bv), (bo_sb, bo)):
                sp.dma_start(b_sb[:], b_.rearrange("(a n) -> a n", a=1).broadcast_to([P, b_.shape[0]]))\
                    .then_inc(weights_in, 16)
            for n in range(2):
                sp.dma_start(xT[:, n], x_v[:, :, n * P:(n + 1) * P]).then_inc(x_in[n], 16)
            with sp.Fori(0, TILES // 2 - 1) as i:
                for u in range(2):
                    n = i * 2 + 2 + u
                    sp.wait_ge(x_used, n - 1)
                    sp.dma_start(xT[:, u], x_v[:, :, bass.ds(n * P, P)]).then_inc(x_in[u], 16)

        @block.gpsimd
        def _(pool):
            pool.memset(ident[:], 0.0).then_inc(consts, 1)
            pool.wait_ge(consts, 1)
            pool.affine_select(out=ident[:], in_=ident[:], compare_op=ALU.not_equal, fill=1.0, base=0,
                               pattern=[[-1, P]], channel_multiplier=1).then_inc(consts, 1)

            def normalise(n):
                pool.wait_ge(sums_out, 2 * n + 2)
                pool.wait_ge(dens_inverted, n + 1)
                pool.tensor_tensor(att[:], nums[:], dens[:], ALU.mult).then_inc(att_ready, 1)

            def extreme_scores(n, u):
                pool.wait_ge(scanned, 2 * n + 2)
                pool.wait_ge(q_out, n + 1)
                pool.tensor_tensor(kmax[:], kmax[:], Q[:, u], ALU.mult).then_inc(extremes, 1)
                pool.tensor_tensor(kmin[:], kmin[:], Q[:, u], ALU.mult).then_inc(extremes, 1)

            def tile(n, u, first, last):
                for g, runs in enumerate(groups):
                    pool.wait_ge(scores, n * NG + g + 1)
                    if g == 0:
                        pool.wait_ge(max_ready, n + 1)
                    for run in runs:
                        r = run_of(S, g % SB, run)
                        for a in range(2):
                            ins = pool.tensor_tensor(r[:, a], r[:, a], over_rows(M, u, run[0])[:, a], ALU.subtract)
                    ins.then_inc(shifted, 1)
                    if g == AT_SUMS + 2 and not first:
                        normalise(n - 1)
                    if g == AT_Q + LAG and not last:
                        extreme_scores(n + 1, 1 - u)

            extreme_scores(0, 0)
            over_tiles(pool, tile)
            normalise(TILES - 1)

        @block.scalar
        def _(act):
            def take_dens(n):
                act.wait_ge(den_used, (n + 1) * NG)
                if not isinstance(n, int) or n > 0:
                    act.wait_ge(attT_mm, 2 * n)
                nc.scalar.activation(dens[:], den[:], ACT.Ln).then_inc(sums_out, 1)
                act.wait_ge(sums_out, 2 * n + 1)
                nc.scalar.activation(dens[:], dens[:], ACT.Exp, scale=-1.0).then_inc(dens_inverted, 1)

            def take_nums(n):
                act.wait_ge(num_used, (n + 1) * NG)
                nc.scalar.activation(nums[:], num[:], ACT.Copy).then_inc(sums_out, 1)

            def take_turned(n):
                for half in range(2):
                    act.wait_ge(attT_mm, 2 * n + half + 1)
                    nc.scalar.activation(attT[:, 4 * half:4 * half + 4].rearrange("p c t -> p (c t)"),
                                         pb[:, 512 * half:512 * half + 512], ACT.Copy).then_inc(attT_out, 1)

            def deviation(n):
                act.wait_ge(var_ready, n + 1)
                nc.scalar.activation(logv[:], mv[:, 1:2], ACT.Ln, bias=eps[:, 0:1]).then_inc(log_ready, 1)
                act.wait_ge(log_ready, n + 1)
                nc.scalar.activation(rstd[:], logv[:], ACT.Exp, scale=-0.5).then_inc(inverted, 1)

            def store(n, u):
                act.wait_ge(yn_ready, n + 1)
                act.dma_start(out_tm[bass.ds(n * P, P), :], yn[:, u]).then_inc(stored[u], 16)

            def tile(n, u, first, last):
                for g in range(NG):
                    act.wait_ge(shifted, n * NG + g + 1)
                    nc.scalar.activation(S[:, g % SB], S[:, g % SB], ACT.Exp, scale=C ** -0.5)\
                        .then_inc(probs, 1)
                    if g == AT_SUMS - 1 and not first:
                        take_dens(n - 1)
                    if g == AT_SUMS and not first:
                        take_nums(n - 1)
                    if g == AT_TURN + 2 and not first:
                        take_turned(n - 1)
                    if g == AT_STD and not first:
                        deviation(n - 1)
                    if g == AT_STORE and not first:
                        store(n - 1, 1 - u)

            act.wait_ge(consts_v, 4)
            over_tiles(act, tile)
            take_dens(TILES - 1)
            take_nums(TILES - 1)
            take_turned(TILES - 1)
            deviation(TILES - 1)
            store(TILES - 1, 1)
            act.wait_ge(stored[0], 8 * TILES)
            act.wait_ge(stored[1], 8 * TILES)

        @block.vector
        def _(dve):
            nc.vector.memset(eps[:], EPS).then_inc(consts_v, 1)
            nc.vector.memset(lift[:], 0.0).then_inc(consts_v, 1)
            dve.wait_ge(consts_v, 2)
            lv = lift[:].rearrange("p a (h c) -> p a h c", h=H)
            nc.vector.memset(lv[:, 0, :, 0:1], -BIG).then_inc(consts_v, 1)
            nc.vector.memset(lv[:, 1, :, 0:1], BIG).then_inc(consts_v, 1)
            dve.wait_ge(consts_v, 4)
            dve.wait_ge(weights_in, 16 * 8)

            def take_k(n, u, first=False):
                dve.wait_ge(k_mm, n * 2 + 2)
                nc.vector.tensor_tensor(K[:, u], pb[:], bk_sb[:], ALU.add).then_inc(k_out, 1)
                dve.wait_ge(k_out, n + 1)
                if not first:
                    dve.wait_ge(max_ready, n)
                nc.vector.tensor_tensor_scan(kmax[:], lift[:, 0], K[:, u], 0.0, ALU.add, ALU.max).then_inc(scanned, 1)
                nc.vector.tensor_tensor_scan(kmin[:], lift[:, 1], K[:, u], 0.0, ALU.add, ALU.min).then_inc(scanned, 1)

            def take_q(n, u):
                dve.wait_ge(q_mm, n * 2 + 2)
                nc.vector.tensor_tensor(Q[:, u], pa[:], bq_sb[:], ALU.add).then_inc(q_out, 1)
                dve.wait_ge(q_out, n + 1)

            def take_max(n, u):
                dve.wait_ge(extremes, 2 * n + 2)
                nc.vector.tensor_tensor(M[:, u], kmax[:], kmin[:], ALU.max).then_inc(max_ready, 1)

            def take_v(n, u):
                dve.wait_ge(v_mm, n * 2 + 2)
                nc.vector.tensor_tensor(V[:, u], pb[:], bv_sb[:], ALU.add).then_inc(v_out, 1)

            def make_scores(n, u, g, first):
                if g >= SB or not first:
                    dve.wait_ge(den_used, n * NG + g - SB + 1)
                    dve.wait_ge(products, n * NG + g - SB + 1)
                for run in groups[g]:
                    ins = nc.vector.tensor_tensor(run_of(S, g % SB, run), over_rows(Q, u, run[0]),
                                                  key_column(K, u, run[0]), ALU.mult)
                ins.then_inc(scores, 1)

            def weigh(n, u, g, first):
                dve.wait_ge(probs, n * NG + g + 1)
                if g >= TB or not first:
                    dve.wait_ge(num_used, n * NG + g - TB + 1)
                for run in groups[g]:
                    ins = nc.vector.tensor_tensor(run_of(PV, g % TB, run), run_of(S, g % SB, run),
                                                  key_column(V, u, run[0]), ALU.mult)
                ins.then_inc(products, 1)
                dve.wait_ge(products, n * NG + g + 1)
                for run in groups[g]:
                    r = run_of(PV, g % TB, run)
                    ins = nc.vector.tensor_tensor(r[:, 0, :, 1:], r[:, 0, :, 1:], r[:, 1, :, 1:], ALU.add)
                ins.then_inc(weighted, 1)

            def join(n):
                dve.wait_ge(y_mm, n + 1)
                nc.vector.tensor_tensor(y[:], pa[:, 0:D], bo_sb[:], ALU.add).then_inc(y_taken, 1)
                dve.wait_ge(y_taken, n + 1)
                nc.vector.tensor_tensor(y[:], y[:], pa[:, 512:512 + D], ALU.add).then_inc(y_ready, 1)
                dve.wait_ge(y_ready, n + 1)
                nc.vector.bn_stats(stats[:], y[:]).then_inc(stats_ready, 1)
                dve.wait_ge(stats_ready, n + 1)
                nc.vector.memset(spare[:], 0.0)
                nc.vector.bn_aggr(mv[:], stats[:]).then_inc(var_ready, 1)

            def norm(n, u, stores):
                dve.wait_ge(inverted, n + 1)
                if stores is not None:
                    dve.wait_ge(stored[u], stores)
                nc.vector.tensor_scalar(yn[:, u], y[:], mv[:, 0:1], rstd[:, 0:1], ALU.subtract, ALU.mult)\
                    .then_inc(yn_ready, 1)

            def tile(n, u, first, last):
                for g in range(NG):
                    make_scores(n, u, g, first)
                    if g == 0:
                        take_max(n, u)
                    if g >= 2:
                        weigh(n, u, g - 2, first)
                    elif not first:
                        weigh(n - 1, 1 - u, NG + g - 2, False)
                    if g == AT_OUT + LAG and not first:
                        join(n - 1)
                    if g == AT_NORM and not first:
                        norm(n - 1, 1 - u, 8 * (n - 2 + u))
                    if not last:
                        if g == AT_K + LAG:
                            take_k(n + 1, 1 - u)
                        if g == AT_Q + LAG:
                            take_q(n + 1, 1 - u)
                        if g == AT_V + LAG:
                            take_v(n + 1, 1 - u)

            take_k(0, 0, True)
            take_q(0, 0)
            take_v(0, 0)
            over_tiles(dve, tile)
            weigh(TILES - 1, 1, NG - 2, False)
            weigh(TILES - 1, 1, NG - 1, False)
            join(TILES - 1)
            norm(TILES - 1, 1, 16 * (TILES // 2 - 1))

        @block.tensor
        def _(pe):
            def project(n, u, w_sb, dst, done):
                for half in range(2):
                    for c in range(DC):
                        ins = nc.tensor.matmul(dst[:, 512 * half:512 * half + 512], xT[:, u, c],
                                               w_sb[:, c, 512 * half:512 * half + 512],
                                               start=(c == 0), stop=(c == DC - 1))
                    ins.then_inc(done, 1)

            def make_k(n, u, x_count):
                pe.wait_ge(x_in[u], x_count)
                project(n, u, wk_sb, pb, k_mm)

            def make_q(n, u):
                project(n, u, wq_sb, pa, q_mm)

            def make_v(n, u):
                pe.wait_ge(k_out, n + 1)
                project(n, u, wv_sb, pb, v_mm)

            def add_up(n, g, acc, buf, used, added):
                for j, at, w in groups[g]:
                    for a in range(1 if added else 2):
                        for half in range(2):
                            h0 = 8 * half
                            r = run_of(buf, g % SB, (j, at, w))[:, a, h0:h0 + 8, a:w]
                            ins = nc.tensor.matmul(by_head(acc)[:, h0:h0 + 8, j + a:C], ident[:], r,
                                                   start=(j == 0 and a == 0), stop=True, skip_group_check=True)
                ins.then_inc(used, 1)

            def turn(n, u):
                pe.wait_ge(att_ready, n + 1)
                for c in range(HC):
                    ins = nc.tensor.transpose(pb[:, c * P:(c + 1) * P], att[:, c * P:(c + 1) * P], ident[:])
                    if c % 4 == 3:
                        ins.then_inc(attT_mm, 1)
                for c in range(DC):
                    ins = nc.tensor.transpose(pa[:, 512 + c * P:512 + (c + 1) * P], xT[:, u, c], ident[:])
                ins.then_inc(x_used, 1)

            def project_out(n):
                pe.wait_ge(attT_out, 2 * n + 2)
                for c in range(HC):
                    ins = nc.tensor.matmul(pa[:, 0:D], attT[:, c], wo_sb[:, c], start=(c == 0), stop=(c == HC - 1))
                ins.then_inc(y_mm, 1)

            def add_numerators(n, g):
                pe.wait_ge(weighted, n * NG + g + 1)
                add_up(n, g, num, PV, num_used, True)

            def tile(n, u, first, last):
                for g in range(NG):
                    if g == 0 and not first:
                        pe.wait_ge(sums_out, 2 * n - 1)
                    pe.wait_ge(probs, n * NG + g + 1)
                    add_up(n, g, den, S, den_used, False)
                    if g == 0 and not first:
                        add_numerators(n - 1, NG - 1)
                    if g == 1 and not first:
                        pe.wait_ge(sums_out, 2 * n)
                    if g >= 1:
                        add_numerators(n, g - 1)
                    if not first:
                        if g == AT_TURN:
                            pe.wait_ge(v_out, n + 1)
                            pe.wait_ge(q_out, n + 1)
                            turn(n - 1, 1 - u)
                        if g == AT_OUT:
                            project_out(n - 1)
                    if not last:
                        if g == AT_K:
                            if not first:
                                pe.wait_ge(attT_out, 2 * n)
                            make_k(n + 1, 1 - u, 16 if first else 8 * (n + 2 + u))
                        if g == AT_Q:
                            if not first:
                                pe.wait_ge(y_ready, n)
                            make_q(n + 1, 1 - u)
                        if g == AT_V:
                            make_v(n + 1, 1 - u)

            pe.wait_ge(weights_in, 16 * 8)
            pe.wait_ge(consts, 2)
            make_k(0, 0, 16)
            make_q(0, 0)
            make_v(0, 0)
            over_tiles(pe, tile)
            add_numerators(TILES - 1, NG - 1)
            turn(TILES - 1, 1)
            project_out(TILES - 1)


RWKV_COLUMNS = ["ln1_w", "ln2_w", "x_maa", "w_maa", "k_maa", "v_maa", "r_maa", "g_maa", "time_decay",
                "time_first", "gn_w", "gn_b", "ck_maa", "cr_maa"]


class FeatureNorm:

    def __init__(self, sem, name, ones, eps, groups):
        self.ones, self.eps, self.groups = ones, eps, groups
        self.mean_mm = sem(f"{name}_mean_mm")
        self.centered = sem(f"{name}_centered")
        self.squared = sem(f"{name}_squared")
        self.var_mm = sem(f"{name}_var_mm")
        self.log_out = sem(f"{name}_log_out")
        self.rstd_out = sem(f"{name}_rstd_out")
        self.normed = sem(f"{name}_normed")

    def half(self, t, h):
        return t[:, :, 512 * h:512 * h + 512]

    def sums(self, nc, src, stat, h):
        for g in range(self.groups):
            cs = [g] if self.groups > 1 else list(range(DC))
            for k, c in enumerate(cs):
                ins = nc.tensor.matmul(stat[:, g, h], self.ones, src[:, c, 512 * h:512 * h + 512],
                                       start=(k == 0), stop=(k == len(cs) - 1))
        return ins

    def pe_mean(self, nc, pe, n, src, stat):
        for h in range(2):
            self.sums(nc, src, stat, h).then_inc(self.mean_mm, 1)

    def pe_var(self, nc, pe, n, sq, stat):
        for h in range(2):
            pe.wait_ge(self.squared, 2 * n + h + 1)
            self.sums(nc, sq, stat, h).then_inc(self.var_mm, 1)

    def dve_center(self, nc, dve, n, src, out, stat):
        for h in range(2):
            dve.wait_ge(self.mean_mm, 2 * n + h + 1)
            mean = stat[:, :, h] if self.groups == DC else stat[:, :, h].broadcast_to([P, DC, 512])
            nc.vector.tensor_tensor(self.half(out, h), self.half(src, h), mean, ALU.subtract)\
                .then_inc(self.centered, 1)

    def act_square(self, nc, act, n, src, sq):
        for h in range(2):
            act.wait_ge(self.centered, 2 * n + h + 1)
            nc.scalar.activation(self.half(sq, h), self.half(src, h), ACT.Square).then_inc(self.squared, 1)

    def act_rstd(self, nc, act, n, stat, rstd):
        for h in range(2):
            act.wait_ge(self.var_mm, 2 * n + h + 1)
            nc.scalar.activation(self.half(rstd, h), stat[:, :, h], ACT.Ln, bias=self.eps).then_inc(self.log_out, 1)
        for h in range(2):
            act.wait_ge(self.log_out, 2 * n + h + 1)
            nc.scalar.activation(self.half(rstd, h), self.half(rstd, h), ACT.Exp, scale=-0.5)\
                .then_inc(self.rstd_out, 1)

    def dve_scale(self, nc, dve, n, buf, rstd, weight):
        for h in range(2):
            dve.wait_ge(self.rstd_out, 2 * n + h + 1)
            b_, s = self.half(buf, h), self.half(rstd, h)
            if weight is None:
                ins = nc.vector.tensor_tensor(b_, b_, s if self.groups == DC else s.broadcast_to([P, DC, 512]), ALU.mult)
            else:
                for c in range(DC):
                    ins = nc.vector.scalar_tensor_tensor(b_[:, c], b_[:, c], weight[:, c:c + 1],
                                                         s[:, c if self.groups == DC else 0], ALU.mult, ALU.mult)
        ins.then_inc(self.normed, 1)
        dve.wait_ge(self.normed, n + 1)


def rwkv(nc, x_fm, masks, p, work_fm):
    L = 2
    H, HS = 4, 64
    E, NMIX, ED = 32, 5, 64
    FK = 6
    CH = T // P
    LEVELS = [1, 2, 4, 8, 16, 32, 64]
    NL = len(LEVELS)
    CONSTS = 13
    VEC_STEPS = 1 + 2 + (CH - 1) + 1 + 1 + 2
    PER = (NL + 1) * DC
    with ExitStack() as ctx:
        sb, psum, sem = allocators(nc, ctx, "tm")
        XIN = sb("XIN", [P, DC, T])
        X = sb("X", [P, DC, T])
        XL = sb("XL", [P, DC, T + 1])
        SX = sb("SX", [P, DC, T])
        ZX = sb("ZX", [P, 2, DC, T])
        MX = sb("MX", [P, T])
        MX4 = sb("MX4", [P, T])
        TD = sb("TD", [P, T])
        W = sb("W", [P, DC, 2 * T])
        RKO = sb("RKO", [P, 3, DC, T])
        R, K, OUT = RKO[:, 0], RKO[:, 1], RKO[:, 2]
        K2 = RKO[:].rearrange("p a c t -> p (a c) t")
        Vt = sb("Vt", [P, CH, D])
        G = sb("G", [P, DC, T])
        T1 = sb("T1", [P, DC, T])
        T2 = sb("T2", [P, DC, T])
        Rp = sb("Rp", [P, DC, 2, T])
        A = sb("A", [P, DC, CH, 2, P])
        ST = sb("ST", [P, CH, DC, P])
        ident = sb("ident", [P, P])
        ones = sb("ones", [P, P])
        gones = sb("gones", [P, P])
        eps = sb("eps", [P, 1])
        spare = sb("spare", [P, 20])
        mask_f = sb("masks", [P, P + NL * P // 2])
        mask_sb = mask_f[:].bitcast(mybir.dt.uint32)
        w = {k: sb(k, s) for k, s in dict(
            tm_w1=[P, DC, NMIX * E], tm_w2=[P, NMIX, D], td_w1=[P, DC, ED], td_w2=[P, D],
            Wr=[P, DC, D], Wk=[P, DC, D], Wv=[P, DC, D], Wo=[P, DC, D], Wg=[P, DC, D],
            cWk=[P, DC, FK * P], cWv=[P, FK, D], cWr=[P, DC, D]).items()}
        cols = sb("cols", [P, len(RWKV_COLUMNS), DC])
        col = {k: cols[:, i] for i, k in enumerate(RWKV_COLUMNS)}
        ps = psum("ps", [P, 8, 512])

        weights_in = sem("weights_in")
        x_in = sem("x_in")
        start_copy = sem("start_copy")
        consts = sem("consts")
        consts_p = sem("consts_p")
        ln1 = FeatureNorm(sem, "ln1", ones[:], eps[:, 0:1], 1)
        ln2 = FeatureNorm(sem, "ln2", ones[:], eps[:, 0:1], 1)
        gn = FeatureNorm(sem, "gn", gones[:], eps[:, 0:1], DC)
        mixin_ready = sem("mixin_ready")
        mix_mm = sem("mix_mm")
        tanh_mix = sem("tanh_mix")
        delta_mm = sem("delta_mm")
        delta_used = sem("delta_used")
        zx_ready = sem("zx_ready")
        proj_mm = sem("proj_mm")
        proj_out = sem("proj_out")
        td_mm = sem("td_mm")
        td_out = sem("td_out")
        uk_ready = sem("uk_ready")
        r_decayed = sem("r_decayed")
        k_decayed = sem("k_decayed")
        w_ready = sem("w_ready")
        lvl_mm = sem("lvl_mm")
        lvl_kept = sem("lvl_kept")
        kT_mm = sem("kT_mm")
        kT_out = sem("kT_out")
        kv_mm = sem("kv_mm")
        state_ready = sem("state_ready")
        out_mm = sem("out_mm")
        out_copied = sem("out_copied")
        gated = sem("gated")
        wo_mm = sem("wo_mm")
        mid_ready = sem("mid_ready")
        ck_ready = sem("ck_ready")
        ck_mm = sem("ck_mm")
        ck_out = sem("ck_out")
        ck_sq = sem("ck_sq")
        cr_mm = sem("cr_mm")
        cr_out = sem("cr_out")
        cv_mm = sem("cv_mm")
        x_ready = sem("x_ready")
        stored = sem("stored")
        vec = sem("vec")
        act_s = sem("act_s")
        block = ctx.enter_context(nc.Block())

        x_v = work_fm.rearrange("(c p) (b t) -> b p c t", p=P, t=T)
        MAAS = ["w_maa", "k_maa", "v_maa", "r_maa", "g_maa"]
        stat0 = ps[:, 0:2].rearrange("p (g h) t -> p g h t", g=1)
        stat1 = ps[:, 2:4].rearrange("p (g h) t -> p g h t", g=1)
        low4 = ps[:, 0:4].rearrange("p (g h) t -> p g h t", g=DC)
        high4 = ps[:, 4:8].rearrange("p (g h) t -> p g h t", g=DC)
        gn_mean = ps[:, 4:8].rearrange("p (h g) t -> p g h t", g=DC)
        gn_var = ps[:, 0:4].rearrange("p (h g) t -> p g h t", g=DC)
        flat = lambda a: a.rearrange("p g h t -> p g (h t)")
        base = [0]
        for m in LEVELS:
            base.append(base[-1] + T // m)

        def level_decays(lv):
            return W[:, :, base[lv]:base[lv + 1]].rearrange("p c (b s) -> p c b s", s=2)

        def level_bank(lv, c):
            return 4 * (lv % 2) + 2 * c

        @block.sync
        def _(sp):
            sp.dma_start(work_fm, x_fm).then_inc(start_copy, 16)
            sp.dma_start(mask_f[:], masks).then_inc(start_copy, 16)
            sp.wait_ge(start_copy, 32)
            sp.wait_ge(consts, CONSTS)
            with sp.Fori(0, L) as l:
                sp.wait_ge(x_ready, l * B)
                for k in ("tm_w1", "td_w1", "Wr", "Wk", "Wv", "Wo", "Wg", "cWk", "cWv", "cWr"):
                    sp.dma_start(w[k][:], p[k][bass.ds(l, 1)].rearrange("o (c p) n -> p (o c) n", p=P))\
                        .then_inc(weights_in, 16)
                for f in range(NMIX):
                    r0 = E * (f % 4)
                    sp.dma_start(w["tm_w2"][r0:r0 + E, f], p["tm_w2"][bass.ds(l, 1), f].rearrange("o e d -> (o e) d"))\
                        .then_inc(weights_in, 16)
                sp.dma_start(w["td_w2"][0:ED], p["td_w2"][bass.ds(l, 1)].rearrange("o e d -> (o e) d"))\
                    .then_inc(weights_in, 16)
                sp.dma_start(cols[:], p["columns"][bass.ds(l, 1)].rearrange("o p k c -> (o p) k c"))\
                    .then_inc(weights_in, 16)
                with sp.Fori(0, B) as b:
                    n = l * B + b
                    sp.wait_ge(mid_ready, n)
                    sp.dma_start(XIN[:], x_v[bass.ds(b, 1)].rearrange("o p c t -> p (o c) t")).then_inc(x_in, 16)

        NW = 16 * 17

        @block.gpsimd
        def _(pool):
            pool.memset(ident[:], 0.0).then_inc(consts_p, 1)
            pool.wait_ge(consts_p, 1)
            pool.affine_select(out=ident[:], in_=ident[:], compare_op=ALU.not_equal, fill=1.0, base=0,
                               pattern=[[-1, P]], channel_multiplier=1).then_inc(consts_p, 1)
            with pool.Fori(0, L) as l, pool.Fori(0, B) as b:
                n = l * B + b
                pool.wait_ge(td_out, n + 1)
                for lv, m in enumerate(LEVELS):
                    nb = T // (2 * m)
                    tw = level_decays(lv)
                    if lv >= 1:
                        pool.wait_ge(w_ready, n * NL + lv)
                    pool.tensor_tensor(W[:, :, base[lv + 1]:base[lv + 1] + nb], tw[:, :, :, 0], tw[:, :, :, 1],
                                       ALU.mult).then_inc(w_ready, 1)
                    for c in range(DC):
                        pool.wait_ge(lvl_mm, n * PER + (lv + 1) * DC + c + 1)
                        first = K[:, c].rearrange("p (b s m) -> p b s m", s=2, m=m)[:, :, 0]
                        pool.tensor_tensor(first, first, tw[:, c, :, 1:2].broadcast_to([P, nb, m]), ALU.mult)\
                            .then_inc(k_decayed, 1)

        @block.scalar
        def _(act):
            act.wait_ge(consts, CONSTS)
            with act.Fori(0, L) as l, act.Fori(0, B) as b:
                n = l * B + b
                own = Steps(act, act_s, DC, n)
                ln1.act_square(nc, act, n, XL[:, :, 1:T + 1], T1[:])
                ln1.act_rstd(nc, act, n, stat1, T2[:, 0:1])
                act.wait_ge(mix_mm, n + 1)
                nc.scalar.activation(MX[:], ps[:, 4:6].rearrange("p h t -> p (h t)"), ACT.Tanh)
                nc.scalar.activation(MX4[0:E], ps[0:E, 6:8].rearrange("p h t -> p (h t)"), ACT.Tanh)\
                    .then_inc(tanh_mix, 1)
                act.wait_ge(proj_mm, n * 5 + 1)
                nc.scalar.activation(TD[0:ED], ps[0:ED, 0:2].rearrange("p h t -> p (h t)"), ACT.Tanh)\
                    .then_inc(proj_out, 1)
                act.wait_ge(td_mm, n + 1)
                for c in range(DC):
                    own.done(nc.scalar.activation(W[:, c, 0:T], flat(low4)[:, c], ACT.Exp,
                                                  bias=col["time_decay"][:, c:c + 1]))
                nc.scalar.activation(W[:, :, 0:T], W[:, :, 0:T], ACT.Exp, scale=-1.0).then_inc(td_out, 1)
                act.wait_ge(proj_mm, n * 5 + 2)
                nc.scalar.activation(K, flat(low4), ACT.Copy).then_inc(proj_out, 1)
                act.wait_ge(proj_mm, n * 5 + 3)
                nc.scalar.activation(Vt[:].rearrange("p j d -> p (j d)"), ps[:, 0:4].rearrange("p a b -> p (a b)"),
                                     ACT.Copy).then_inc(proj_out, 1)
                act.wait_ge(proj_mm, n * 5 + 4)
                nc.scalar.activation(R, flat(low4), ACT.Tanh, scale=0.5).then_inc(proj_out, 1)
                act.wait_ge(proj_mm, n * 5 + 5)
                nc.scalar.activation(T2[:], flat(low4), ACT.Tanh, scale=0.5)
                nc.scalar.activation(G[:], flat(low4), ACT.Copy).then_inc(proj_out, 1)
                act.wait_ge(kT_mm, n + 1)
                nc.scalar.activation(ZX[:, 0].rearrange("p c t -> p (c t)"), ps[:, 4:8].rearrange("p a b -> p (a b)"),
                                     ACT.Copy).then_inc(kT_out, 1)
                act.wait_ge(out_mm, n + 1)
                nc.scalar.activation(OUT, flat(low4), ACT.Copy).then_inc(out_copied, 1)
                gn.act_square(nc, act, n, OUT, T1[:])
                gn.act_rstd(nc, act, n, gn_var, T2[:])
                ln2.act_square(nc, act, n, XL[:, :, 1:T + 1], T1[:])
                ln2.act_rstd(nc, act, n, stat1, T2[:, 0:1])
                for k in range(2 * FK):
                    act.wait_ge(ck_mm, n * 2 * FK + k + 1)
                    nc.scalar.activation(K2[:, k // 2, 512 * (k % 2):512 * (k % 2) + 512], ps[:, 4 + k % 4], ACT.Relu)\
                        .then_inc(ck_out, 1)
                act.wait_ge(cr_mm, n + 1)
                nc.scalar.activation(T1[:], flat(low4), ACT.Tanh, scale=0.5).then_inc(cr_out, 1)
                act.wait_ge(x_ready, n + 1)
                act.dma_start(x_v[bass.ds(b, 1)].rearrange("o p c t -> p (o c) t"), X[:]).then_inc(stored, 16)
            act.wait_ge(stored, L * B * 16)

        @block.vector
        def _(dve):
            for k, ins in enumerate([
                    nc.vector.memset(eps[:], EPS), nc.vector.memset(ones[:], 1.0 / D),
                    nc.vector.memset(XL[:, :, 0:1], 0.0), nc.vector.memset(gones[:], 0.0),
                    nc.vector.memset(A[:], 0.0), nc.vector.memset(ST[:], 0.0), nc.vector.memset(Rp[:], 0.0),
                    nc.vector.memset(w["tm_w2"][:], 0.0), nc.vector.memset(w["td_w2"][:], 0.0),
                    nc.vector.memset(MX4[:], 0.0), nc.vector.memset(TD[:], 0.0)]):
                ins.then_inc(consts, 1)
            dve.wait_ge(consts, 11)
            nc.vector.memset(gones[0:HS, 0:HS], 1.0 / HS).then_inc(consts, 1)
            nc.vector.memset(gones[HS:P, HS:P], 1.0 / HS).then_inc(consts, 1)
            with dve.Fori(0, L) as l:
                with dve.Fori(0, B) as b:
                    n = l * B + b
                    dve.wait_ge(weights_in, (l + 1) * NW)
                    dve.wait_ge(x_in, (n + 1) * 16)
                    own = Steps(dve, vec, VEC_STEPS, n)
                    free_columns = iter(range(20))

                    def beat():
                        k = next(free_columns)
                        return nc.vector.memset(spare[:, k:k + 1], 0.0)

                    xl, prev = XL[:, :, 1:T + 1], XL[:, :, 0:T]

                    def mix_in(out, maa):
                        for c in range(DC):
                            ins = nc.vector.scalar_tensor_tensor(out[:, c], SX[:, c], col[maa][:, c:c + 1],
                                                                 xl[:, c], ALU.mult, ALU.add)
                        return ins

                    ln1.dve_center(nc, dve, n, XIN[:], xl, stat0)
                    ln1.dve_scale(nc, dve, n, xl, T2[:, 0:1], col["ln1_w"])
                    own.done(nc.vector.tensor_tensor(SX[:], prev, xl, ALU.subtract))
                    mix_in(ZX[:, 1], "x_maa").then_inc(mixin_ready, 1)
                    for f, maa in enumerate(MAAS):
                        z = ZX[:, f % 2]
                        dve.wait_ge(delta_mm, n * 5 + f + 1)
                        if f == 1:
                            dve.wait_ge(mix_mm, n + 1)
                        if f >= 2:
                            dve.wait_ge(proj_mm, n * 5 + f - 1)
                        for c in range(DC):
                            ins = nc.vector.scalar_tensor_tensor(z[:, c], flat(high4)[:, c], col[maa][:, c:c + 1],
                                                                 SX[:, c], ALU.add, ALU.mult)
                        ins.then_inc(delta_used, 1)
                        dve.wait_ge(delta_used, n * 5 + f + 1)
                        nc.vector.tensor_tensor(z, z, xl, ALU.add).then_inc(zx_ready, 1)
                    dve.wait_ge(proj_out, n * 5 + 4)
                    for a in range(2):
                        r0, r1 = HS * a, HS * a + HS
                        ins = nc.vector.tensor_scalar(Rp[r0:r1, :, a], R[r0:r1], 0.5, 0.5, ALU.mult, ALU.add)
                    own.done(ins)
                    for c in range(DC):
                        ins = nc.vector.tensor_scalar(T1[:, c], K[:, c], col["time_first"][:, c:c + 1], None, ALU.mult)
                    ins.then_inc(uk_ready, 1)
                    dve.wait_ge(uk_ready, n + 1)

                    def keep(lv, c):
                        dve.wait_ge(lvl_mm, n * PER + lv * DC + c + 1)
                        if lv:
                            dve.wait_ge(lvl_kept, n * PER + (lv - 1) * DC + c + 1)
                        beat()
                        m = LEVELS[lv - 1] if lv else P
                        to = A[:, c].rearrange("p j a i -> p (j a) i")
                        if lv:
                            to = to.rearrange("p k (b s m) -> p k b s m", s=2, m=m)[:, :, :, 1]
                            mask = mask_sb[:, P + P // 2 * (lv - 1):P + P // 2 * lv]\
                                .rearrange("p (o b m) -> p o b m", o=1, m=m)
                            got = ps[:, level_bank(lv, c):level_bank(lv, c) + 2]\
                                .rearrange("p q (k b m) -> p (q k) b m", k=8, m=m)
                        else:
                            mask = mask_sb[:, 0:P].rearrange("p (o i) -> p o i", o=1)
                            got = ps[:, 4 - 4 * c:8 - 4 * c].rearrange("p q (k i) -> p (q k) i", k=4)
                        nc.vector.copy_predicated(to, mask.broadcast_to(list(to.shape)), got).then_inc(lvl_kept, 1)

                    keep(0, 0)
                    dve.wait_ge(proj_out, n * 5 + 5)
                    own.done(nc.vector.scalar_tensor_tensor(G[:], T2[:], 1.0, G[:], ALU.add, ALU.mult))
                    keep(0, 1)
                    dve.wait_ge(td_out, n + 1)
                    for lv, m in enumerate(LEVELS):
                        nb = T // (2 * m)
                        if lv >= 1:
                            dve.wait_ge(w_ready, n * NL + lv)
                        for c in range(DC):
                            dve.wait_ge(lvl_mm, n * PER + (lv + 1) * DC + c + 1)
                            second = Rp[:, c].rearrange("p a (b s m) -> p a b s m", s=2, m=m)[:, :, :, 1]
                            tw = level_decays(lv)[:, c:c + 1, :, 0].rearrange("p o (b m) -> p o b m", m=1)
                            nc.vector.tensor_tensor(second, second, tw.broadcast_to([P, 2, nb, m]), ALU.mult)\
                                .then_inc(r_decayed, 1)
                        for c in range(DC):
                            keep(lv + 1, c)
                    dve.wait_ge(w_ready, (n + 1) * NL)
                    dve.wait_ge(kv_mm, n + 1)
                    for j in range(CH - 1):
                        for c in range(DC):
                            for a in range(2):
                                r0, r1 = HS * a, HS * a + HS
                                ins = nc.vector.scalar_tensor_tensor(
                                    ST[r0:r1, j + 1, c, r0:r1], ST[r0:r1, j, c, r0:r1],
                                    W[r0:r1, c, base[NL] + j:base[NL] + j + 1],
                                    ps[r0:r1, (2 * j + c) // 4, P * ((2 * j + c) % 4) + r0:P * ((2 * j + c) % 4) + r1],
                                    ALU.mult, ALU.add)
                        own.done(ins)
                    beat().then_inc(state_ready, 1)
                    dve.wait_ge(out_copied, n + 1)
                    gn.dve_center(nc, dve, n, OUT, OUT, gn_mean)
                    gn.dve_scale(nc, dve, n, OUT, T2[:], col["gn_w"])
                    own.done(nc.vector.tensor_scalar(G[:], G[:], 0.5, None, ALU.mult))
                    for c in range(DC):
                        ins = nc.vector.scalar_tensor_tensor(OUT[:, c], OUT[:, c], col["gn_b"][:, c:c + 1], G[:, c],
                                                             ALU.add, ALU.mult)
                    ins.then_inc(gated, 1)
                    dve.wait_ge(wo_mm, n + 1)
                    dve.wait_ge(stored, n * 16)
                    nc.vector.tensor_tensor(X[:], XIN[:], flat(high4), ALU.add).then_inc(mid_ready, 1)
                    dve.wait_ge(mid_ready, n + 1)
                    ln2.dve_center(nc, dve, n, X[:], xl, stat0)
                    ln2.dve_scale(nc, dve, n, xl, T2[:, 0:1], col["ln2_w"])
                    own.done(nc.vector.tensor_tensor(SX[:], prev, xl, ALU.subtract))
                    mix_in(ZX[:, 0], "ck_maa").then_inc(ck_ready, 1)
                    mix_in(ZX[:, 1], "cr_maa").then_inc(ck_ready, 1)
                    for k in range(2 * FK):
                        dve.wait_ge(ck_out, n * 2 * FK + k + 1)
                        kk = K2[:, k // 2, 512 * (k % 2):512 * (k % 2) + 512]
                        nc.vector.tensor_tensor(kk, kk, kk, ALU.mult).then_inc(ck_sq, 1)
                    dve.wait_ge(cr_out, n + 1)
                    own.done(nc.vector.tensor_scalar(T1[:], T1[:], 0.5, 0.5, ALU.mult, ALU.add))
                    dve.wait_ge(cv_mm, n + 1)
                    own.done(nc.vector.tensor_tensor(T1[:], T1[:], flat(high4), ALU.mult))
                    nc.vector.tensor_tensor(X[:], X[:], T1[:], ALU.add).then_inc(x_ready, 1)
                    own.close()

        @block.tensor
        def _(pe):
            pe.wait_ge(consts, CONSTS)
            pe.wait_ge(consts_p, 2)
            with pe.Fori(0, L) as l:
                with pe.Fori(0, B) as b:
                    n = l * B + b
                    pe.wait_ge(weights_in, (l + 1) * NW)

                    def linear(dst, wt, src, rows=P, kc=DC):
                        for m in range((wt.shape[2] + P - 1) // P):
                            for half in range(2):
                                for c in range(kc):
                                    ins = nc.tensor.matmul(dst[0:rows, m, half], wt[:, c, m * P:m * P + rows],
                                                           src[:, c, 512 * half:512 * half + 512],
                                                           start=(c == 0), stop=(c == kc - 1))
                        return ins

                    pe.wait_ge(x_in, (n + 1) * 16)
                    pe.wait_ge(cr_out, n)
                    ln1.pe_mean(nc, pe, n, XIN, stat0)
                    ln1.pe_var(nc, pe, n, T1, stat1)
                    pe.wait_ge(mixin_ready, n + 1)
                    pe.wait_ge(x_ready, n)
                    for half in range(2):
                        for c in range(DC):
                            nc.tensor.matmul(ps[:, 4 + half], w["tm_w1"][:, c, 0:P],
                                             ZX[:, 1, c, 512 * half:512 * half + 512], start=(c == 0), stop=(c == DC - 1))
                        for c in range(DC):
                            ins = nc.tensor.matmul(ps[0:E, 6 + half], w["tm_w1"][:, c, P:P + E],
                                                   ZX[:, 1, c, 512 * half:512 * half + 512],
                                                   start=(c == 0), stop=(c == DC - 1))
                    ins.then_inc(mix_mm, 1)

                    def delta(f):
                        if f == 0:
                            pe.wait_ge(tanh_mix, n + 1)
                        else:
                            pe.wait_ge(delta_used, n * 5 + f)
                        for c in range(DC):
                            for half in range(2):
                                t0, t1 = 512 * half, 512 * half + 512
                                ins = nc.tensor.matmul(ps[:, 4 + 2 * c + half], w["tm_w2"][:, f, c * P:(c + 1) * P],
                                                       (MX if f < 4 else MX4)[:, t0:t1], start=True, stop=True)
                        ins.then_inc(delta_mm, 1)

                    def project(f):
                        pe.wait_ge(zx_ready, n * 5 + f + 1)
                        z = ZX[:, f % 2]
                        if f == 0:
                            linear(low4, w["td_w1"], z, rows=ED).then_inc(proj_mm, 1)
                            pe.wait_ge(proj_out, n * 5 + 1)
                            for m in range(DC):
                                for half in range(2):
                                    ins = nc.tensor.matmul(low4[:, m, half], w["td_w2"][:, m * P:(m + 1) * P],
                                                           TD[:, 512 * half:512 * half + 512], start=True, stop=True)
                            ins.then_inc(td_mm, 1)
                            return
                        if f == 1:
                            pe.wait_ge(td_out, n + 1)
                        else:
                            pe.wait_ge(proj_out, n * 5 + f)
                        if f == 2:
                            for j in range(CH):
                                for c in range(DC):
                                    ins = nc.tensor.matmul(ps[:, j // 2, D * (j % 2):D * (j % 2) + D],
                                                           z[:, c, j * P:(j + 1) * P], w["Wv"][:, c],
                                                           start=(c == 0), stop=(c == DC - 1))
                            ins.then_inc(proj_mm, 1)
                            return
                        linear(low4, w[[None, "Wk", None, "Wr", "Wg"][f]], z).then_inc(proj_mm, 1)

                    delta(0)
                    delta(1)
                    project(0)
                    for f in range(2, 5):
                        delta(f)
                        project(f - 1)
                    project(4)
                    pe.wait_ge(uk_ready, n + 1)
                    pe.wait_ge(delta_used, n * 5 + 5)
                    for c in range(DC):
                        if c == 1:
                            pe.wait_ge(proj_out, n * 5 + 5)
                        for j in range(CH):
                            ins = nc.tensor.matmul(
                                ps[:, 4 - 4 * c + j // 2, 256 * (j % 2):256 * (j % 2) + 256].rearrange("p (a i) -> p a i", a=2),
                                T1[:, c, j * P:(j + 1) * P], Rp[:, c, :, j * P:(j + 1) * P], start=True, stop=True)
                        ins.then_inc(lvl_mm, 1)
                    for lv in range(1, NL + 1):
                        m = LEVELS[lv - 1]
                        for c in range(DC):
                            if lv >= 2:
                                pe.wait_ge(r_decayed, n * NL * DC + (lv - 2) * DC + c + 1)
                                pe.wait_ge(k_decayed, n * NL * DC + (lv - 2) * DC + c + 1)
                            pe.wait_ge(lvl_kept, n * PER + ((lv - 2) * DC + c + 1 if lv >= 3 else lv))
                            for j in range(CH):
                                second = Rp[:, c, :, j * P:(j + 1) * P].rearrange("p a (b s m) -> p a b s m", s=2, m=m)
                                ins = nc.tensor.matmul(
                                    ps[:, level_bank(lv, c) + j // 4, P * (j % 4):P * (j % 4) + P]
                                    .rearrange("p (a b m) -> p a b m", a=2, m=m),
                                    K[:, c, j * P:(j + 1) * P], second[:, :, :, 1], start=True, stop=True)
                            ins.then_inc(lvl_mm, 1)
                    pe.wait_ge(r_decayed, (n + 1) * NL * DC)
                    pe.wait_ge(k_decayed, (n + 1) * NL * DC)
                    pe.wait_ge(lvl_kept, (n + 1) * PER)
                    for j in range(CH):
                        for c in range(DC):
                            k = 2 * j + c
                            ins = nc.tensor.transpose(ps[:, 4 + k // 4, P * (k % 4):P * (k % 4) + P],
                                                      K[:, c, j * P:(j + 1) * P], ident[:])
                    ins.then_inc(kT_mm, 1)
                    pe.wait_ge(kT_out, n + 1)
                    kt = ZX[:, 0].rearrange("p c t -> p (c t)").rearrange("p (j d) -> p j d", j=CH)
                    for j in range(CH):
                        for c in range(DC):
                            k = 2 * j + c
                            ins = nc.tensor.matmul(ps[:, k // 4, P * (k % 4):P * (k % 4) + P],
                                                   kt[:, j, c * P:(c + 1) * P], Vt[:, j, c * P:(c + 1) * P],
                                                   start=True, stop=True)
                    ins.then_inc(kv_mm, 1)
                    pe.wait_ge(state_ready, n + 1)
                    for c in range(DC):
                        for j in range(CH):
                            o = low4[:, c, j // 4, P * (j % 4):P * (j % 4) + P]
                            for a in range(2):
                                nc.tensor.matmul(o[HS * a:HS * a + HS], ST[:, j, c, HS * a:HS * a + HS],
                                                 Rp[:, c, a, j * P:(j + 1) * P], start=True, stop=False,
                                                 tile_position=(0, HS * a), skip_group_check=True)
                            for a in range(2):
                                ins = nc.tensor.matmul(o[HS * a:HS * a + HS], Vt[:, j, c * P + HS * a:c * P + HS * a + HS],
                                                       A[:, c, j, a], start=False, stop=True,
                                                       tile_position=(0, HS * a), skip_group_check=True)
                    ins.then_inc(out_mm, 1)
                    pe.wait_ge(out_copied, n + 1)
                    gn.pe_mean(nc, pe, n, OUT, gn_mean)
                    gn.pe_var(nc, pe, n, T1, gn_var)
                    pe.wait_ge(gated, n + 1)
                    linear(high4, w["Wo"], OUT).then_inc(wo_mm, 1)
                    pe.wait_ge(mid_ready, n + 1)
                    ln2.pe_mean(nc, pe, n, X, stat0)
                    ln2.pe_var(nc, pe, n, T1, stat1)
                    pe.wait_ge(ck_ready, 2 * n + 1)
                    for k in range(2 * FK):
                        if k >= 4:
                            pe.wait_ge(ck_out, n * 2 * FK + k - 3)
                        for c in range(DC):
                            ins = nc.tensor.matmul(ps[:, 4 + k % 4], w["cWk"][:, c, P * (k // 2):P * (k // 2) + P],
                                                   ZX[:, 0, c, 512 * (k % 2):512 * (k % 2) + 512],
                                                   start=(c == 0), stop=(c == DC - 1))
                        ins.then_inc(ck_mm, 1)
                    pe.wait_ge(ck_ready, 2 * n + 2)
                    linear(low4, w["cWr"], ZX[:, 1]).then_inc(cr_mm, 1)
                    pe.wait_ge(ck_sq, (n + 1) * 2 * FK)
                    linear(high4, w["cWv"], K2, kc=FK).then_inc(cv_mm, 1)


MOE_COLUMNS = ["ln_out_w", "ln1_g", "ln1_b", "ln2_g", "ln2_b", "bo", "bq", "bk"]


def sequence_attention(nc, x_fm, rwkv_fm, p, attended_fm, doubled_fm):
    NH, SLOT = 16, 32
    HD = D // NH
    G4 = NH // 4
    QT = T // P
    SCALE = HD ** -0.5
    CONSTS = 2
    VEC_STEPS = 5 * G4
    STACKS = 16 * 2 * 6
    with ExitStack() as ctx:
        sb, psum, sem = allocators(nc, ctx, "mo")
        XA = sb("XA", [P, DC, T])
        XB = sb("XB", [P, DC, T])
        HN = sb("HN", [P, DC, T])
        T1 = sb("T1", [P, DC, T])
        std = sb("std", [P, 1, T])
        QS = sb("QS", [P, NH, T], BF16)
        KS = sb("KS", [P, NH, T], BF16)
        VP = sb("VP", [P, QT, NH * SLOT])
        shared = sb("shared", [P, 6144])
        parts = shared[:].bitcast(BF16).rearrange("p (a s c t) -> p a s c t", a=2, s=3, c=DC)
        PT = shared[:, 0:4096].rearrange("p (k a t) -> p k a t", k=4, a=2)
        mx = sb("mx", [P, QT, 2, NH])
        mg = sb("mg", [P, QT, 4])
        NM = sb("NM", [P, QT, 3, 4], BF16)
        NMT = std[0:12, 0, 0:T // 2].bitcast(BF16)
        OP = sb("OP", [P, G4, T])
        QF, KF = T1, OP[:, 0:DC]
        DOUBLED, ATT = OP[:, 0:DC], OP[:, DC:2 * DC]
        wq = sb("wq", [P, DC, D])
        wk = sb("wk", [P, DC, D])
        wv = sb("wv", [P, DC, NH * SLOT])
        wo = sb("wo", [P, G4, D])
        bv = sb("bv", [P, NH * SLOT])
        cols = sb("cols", [P, len(MOE_COLUMNS), DC])
        col = {k: cols[:, i] for i, k in enumerate(MOE_COLUMNS)}
        ident = sb("ident", [P, P])
        identb = sb("identb", [P, P], BF16)
        sel = sb("sel", [P, P])
        ones = sb("ones", [P, P])
        eps = sb("eps", [P, 1])
        ps = psum("ps", [P, 8, 512])

        const_in = sem("const_in")
        consts = sem("consts")
        consts_p = sem("consts_p")
        ones_set = sem("ones_set")
        split_h = sem("split_h")
        split_r = sem("split_r")
        split_m = sem("split_m")
        split_l = sem("split_l")
        parts_out = sem("parts_out")
        stacked = [sem(f"stacked{g}") for g in range(G4)]
        nm_ready = sem("nm_ready")
        nmt_mm = sem("nmt_mm")
        nmt_out = sem("nmt_out")
        nm_out = sem("nm_out")
        nm_in = sem("nm_in")
        xa_in = sem("xa_in")
        xb_in = sem("xb_in")
        N_ = lambda k: FeatureNorm(sem, k, ones[:], eps[:, 0:1], 1)
        ln_out, ln_join, ln1 = N_("out"), N_("join"), N_("ln1")
        summed = sem("summed")
        hn_ready = sem("hn_ready")
        qk_mm = sem("qk_mm")
        qk_out = sem("qk_out")
        v_mm = sem("v_mm")
        v_out = sem("v_out")
        s_mm = sem("s_mm")
        s_max = sem("s_max")
        st_mm = sem("st_mm")
        probs = sem("probs")
        pv_mm = sem("pv_mm")
        o_out = sem("o_out")
        den_mm = sem("den_mm")
        den_log = sem("den_log")
        den_inverted = sem("den_inverted")
        o_normed = sem("o_normed")
        wo_mm = sem("wo_mm")
        att_ready = sem("att_ready")
        stored = sem("stored")
        vec = sem("vec")
        parts_dram = nc.dram_tensor("mo_parts", (2, 3, D, T), BF16, kind="Internal").ap()
        nm_dram = nc.dram_tensor("mo_maxima", (12, T), BF16, kind="Internal").ap()
        block = ctx.enter_context(nc.Block())

        fm = lambda a: a.rearrange("(c p) (b t) -> b p c t", p=P, t=T)
        x_v, r_v, a_v, d_v = fm(x_fm), fm(rwkv_fm), fm(attended_fm), fm(doubled_fm)
        seq = lambda v, b: v[bass.ds(b, 1)].rearrange("o p c t -> p (o c) t")
        stat0 = ps[:, 0:2].rearrange("p (g h) t -> p g h t", g=1)
        stat1 = ps[:, 2:4].rearrange("p (g h) t -> p g h t", g=1)
        low4 = ps[:, 0:4].rearrange("p (g h) t -> p g h t", g=DC)
        flat = lambda a: a.rearrange("p g h t -> p g (h t)")
        STEPS = [(g, qh, kt) for g in range(G4) for qh in range(2) for kt in range(QT)]
        NS = len(STEPS)
        PER_G = NS // G4
        MAXU = 4 * QT * 2
        NCONST = 16 * 6
        PAIRS = [(0, 0), (0, 1), (1, 0), (1, 1), (0, 2), (2, 0)]
        ROWS = HD * len(PAIRS)

        def max_units(step):
            k = step % PER_G
            return range(min(5 * k, MAXU), min(5 * k + 5, MAXU)) if step // PER_G < G4 - 1 else range(0)

        MAX_DONE, MAX_TURN = 12, 13

        @block.sync
        def _(sp):
            rows = lambda a: a.rearrange("(c p) n -> p c n", p=P)
            wide = lambda a: a.rearrange("(a n) -> a n", a=1).broadcast_to([P, a.shape[0]])
            for dst, src in ((wq, rows(p["wq"])), (wk, rows(p["wk"])), (wv, rows(p["wv"])), (wo, rows(p["wo"])),
                             (bv, wide(p["bv"])), (cols, p["moe_columns"])):
                sp.dma_start(dst[:], src).then_inc(const_in, 16)
            with sp.Fori(0, B) as b:
                sp.wait_ge(ln_join.centered, 2 * b)
                sp.dma_start(XB[:], seq(r_v, b)).then_inc(xb_in, 16)
                sp.wait_ge(summed, 2 * b)
                sp.dma_start(XA[:], seq(x_v, b)).then_inc(xa_in, 16)
                for part, ready in enumerate((split_h, split_m, split_l)):
                    for a in range(2):
                        sp.wait_ge(ready, b * 2 + a + 1)
                        sp.dma_start(parts_dram[a, part].rearrange("(c p) t -> p c t", p=P), parts[:, a, part])\
                            .then_inc(parts_out, 16)
                sp.wait_ge(parts_out, (b + 1) * 6 * 16)
                for g in range(G4):
                    for a, stack in enumerate((QS, KS)):
                        for k, pair in enumerate(PAIRS):
                            rows = parts_dram[a, pair[a], 4 * HD * g:4 * HD * (g + 1)]
                            sp.dma_start(stack[HD * k:HD * k + HD, 4 * g:4 * g + 4],
                                         rows.rearrange("(h r) t -> r h t", r=HD)).then_inc(stacked[g], 16)
                for g in range(G4):
                    sp.wait_ge(nmt_out, b * G4 + g + 1)
                    sp.dma_start(nm_dram, NMT).then_inc(nm_out, 16)
                    sp.wait_ge(nm_out, (b * G4 + g + 1) * 16)
                    sp.dma_start(QS[ROWS:ROWS + 3, 4 * g:4 * g + 4], nm_dram.rearrange("(k h) t -> k h t", k=3))\
                        .then_inc(nm_in, 16)

        @block.gpsimd
        def _(pool):
            pool.memset(ident[:], 0.0).then_inc(consts_p, 1)
            pool.memset(sel[:], 0.0).then_inc(consts_p, 1)
            pool.wait_ge(consts_p, 2)
            pool.affine_select(out=ident[:], in_=ident[:], compare_op=ALU.not_equal, fill=1.0, base=0,
                               pattern=[[-1, P]], channel_multiplier=1).then_inc(consts_p, 1)
            pool.affine_select(out=sel[:].rearrange("p (j r) -> p j r", r=SLOT),
                               in_=sel[:].rearrange("p (j r) -> p j r", r=SLOT), compare_op=ALU.not_equal,
                               fill=1.0, base=-HD, pattern=[[-SLOT, 4], [0, SLOT]], channel_multiplier=1)\
                .then_inc(consts_p, 1)
            pool.wait_ge(consts_p, 4)
            pool.tensor_copy(identb[:], ident[:]).then_inc(consts_p, 1)

        def take_output(act, b, o):
            act.wait_ge(pv_mm, b * NS + (o + 1) * QT)
            nc.scalar.activation(OP[:, o // 2, 512 * (o % 2):512 * (o % 2) + 512], ps[:, 7], ACT.Copy)\
                .then_inc(o_out, 1)

        @block.scalar
        def _(act):
            act.wait_ge(consts, CONSTS)
            act.wait_ge(const_in, NCONST)
            with act.Fori(0, B) as b:
                ln_out.act_square(nc, act, b, XB[:], T1[:])
                ln_out.act_rstd(nc, act, b, stat1, std[:])
                ln_join.act_square(nc, act, b, XA[:], T1[:])
                ln_join.act_rstd(nc, act, b, stat1, std[:])
                ln1.act_square(nc, act, b, HN[:], T1[:])
                ln1.act_rstd(nc, act, b, stat1, std[:])
                for a, (dst, bias) in enumerate(((QF, "bq"), (KF, "bk"))):
                    if a == 1:
                        act.wait_ge(stored, b * 32)
                    for c in range(DC):
                        act.wait_ge(qk_mm, b * 4 + 2 * a + c + 1)
                        nc.scalar.activation(dst[:, c], ps[:, 2 * c:2 * c + 2].rearrange("p h t -> p (h t)"),
                                             ACT.Identity, bias=col[bias][:, c:c + 1]).then_inc(qk_out, 1)
                    act.wait_ge(qk_out, b * 4 + 2 * a + 2)
                    nc.scalar.activation(parts[:, a, 0], dst[:], ACT.Copy).then_inc(split_h, 1)
                for a, dst in enumerate((QF, KF)):
                    act.wait_ge(split_r, b * 2 + a + 1)
                    nc.scalar.activation(parts[:, a, 1], dst[:], ACT.Copy).then_inc(split_m, 1)
                act.wait_ge(parts_out, (b + 1) * 6 * 16)
                for k, (g, qh, kt) in enumerate(STEPS):
                    for hp in range(2):
                        n = 2 * k + hp
                        act.wait_ge(st_mm, b * 2 * NS + n + 1)
                        if k >= 2:
                            act.wait_ge(pv_mm, b * NS + k - 1)
                        nc.scalar.activation(PT[:, n % 4], ps[:, 3 + 2 * hp:5 + 2 * hp], ACT.Exp, scale=SCALE)\
                            .then_inc(probs, 1)
                    if k % QT == 0 and k > 0:
                        take_output(act, b, k // QT - 1)
                take_output(act, b, 2 * G4 - 1)
                inv = T1[:].rearrange("p c (h t) -> p (c h) t", h=2)
                for k0 in (0, 4):
                    n = b * G4 * 2 + k0
                    act.wait_ge(den_mm, n + 4)
                    if k0:
                        act.wait_ge(o_normed, n)
                    nc.scalar.activation(inv, ps[:, 0:4], ACT.Ln).then_inc(den_log, 1)
                    act.wait_ge(den_log, b * 2 + k0 // 4 + 1)
                    nc.scalar.activation(inv, inv, ACT.Exp, scale=-1.0).then_inc(den_inverted, 1)
                act.wait_ge(att_ready, b + 1)
                act.dma_start(seq(a_v, b), ATT).then_inc(stored, 16)
                act.wait_ge(summed, 2 * b + 2)
                act.dma_start(seq(d_v, b), DOUBLED).then_inc(stored, 16)
            act.wait_ge(stored, B * 32)

        @block.vector
        def _(dve):
            for ins in (nc.vector.memset(eps[:], EPS), nc.vector.memset(ones[:], 1.0 / D)):
                ins.then_inc(consts, 1)
            dve.wait_ge(const_in, NCONST)
            nc.vector.memset(KS[ROWS:P], 1.0).then_inc(ones_set, 1)
            with dve.Fori(0, B) as b:
                own = Steps(dve, vec, VEC_STEPS, b)
                ln_out.dve_center(nc, dve, b, XB[:], XB[:], stat0)
                ln_out.dve_scale(nc, dve, b, XB[:], std[:], col["ln_out_w"])
                dve.wait_ge(xa_in, (b + 1) * 16)
                nc.vector.tensor_tensor(XA[:], XA[:], XB[:], ALU.add).then_inc(summed, 1)
                dve.wait_ge(summed, 2 * b + 1)
                ln_join.dve_center(nc, dve, b, XA[:], XA[:], stat0)
                ln_join.dve_scale(nc, dve, b, XA[:], std[:], None)
                ln1.dve_center(nc, dve, b, XA[:], HN[:], stat0)
                ln1.dve_scale(nc, dve, b, HN[:], std[:], col["ln1_g"])
                for c in range(DC):
                    ins = nc.vector.tensor_scalar(HN[:, c], HN[:, c], col["ln1_b"][:, c:c + 1], None, ALU.add)
                ins.then_inc(hn_ready, 1)
                for j in range(QT):
                    dve.wait_ge(v_mm, b * QT + j + 1)
                    nc.vector.tensor_tensor(VP[:, j], ps[:, 4 + j % 4], bv[:], ALU.add).then_inc(v_out, 1)
                for a, src in enumerate((QF, KF)):
                    dve.wait_ge(split_h, b * 2 + a + 1)
                    nc.vector.tensor_tensor(src[:], src[:], parts[:, a, 0], ALU.subtract).then_inc(split_r, 1)
                for a, src in enumerate((QF, KF)):
                    dve.wait_ge(split_m, b * 2 + a + 1)
                    nc.vector.tensor_tensor(parts[:, a, 2], src[:], parts[:, a, 1], ALU.subtract).then_inc(split_l, 1)

                def take_max(g, v):
                    j, qt, kh = v // 16, (v // 2) % QT, v % 2
                    dve.wait_ge(s_mm, (b * G4 + g) * MAXU + v + 1)
                    nc.vector.tensor_reduce(mx[:, qt, kh, 4 * g + j:4 * g + j + 1], ps[:, v % 2], AX.X, ALU.max)\
                        .then_inc(s_max, 1)

                def split_max(g):
                    dve.wait_ge(s_max, (b * G4 + g + 1) * MAXU)
                    if g > 0:
                        dve.wait_ge(nmt_mm, b * G4 + g)
                    own.done(nc.vector.tensor_tensor(mg[:], mx[:, :, 0, 4 * g:4 * g + 4], mx[:, :, 1, 4 * g:4 * g + 4],
                                                     ALU.max))
                    own.done(nc.vector.tensor_scalar(mg[:], mg[:], -1.0, None, ALU.mult))
                    own.done(nc.vector.tensor_copy(NM[:, :, 0], mg[:]))
                    own.done(nc.vector.tensor_tensor(mg[:], mg[:], NM[:, :, 0], ALU.subtract))
                    own.done(nc.vector.tensor_copy(NM[:, :, 1], mg[:]))
                    nc.vector.tensor_tensor(NM[:, :, 2], mg[:], NM[:, :, 1], ALU.subtract).then_inc(nm_ready, 1)

                def take_turned_max(g):
                    dve.wait_ge(nmt_mm, b * G4 + g + 1)
                    if g > 0:
                        dve.wait_ge(nm_in, (b * G4 + g) * 16)
                    nc.vector.tensor_copy(NMT, ps[0:12, 2].bitcast(BF16)).then_inc(nmt_out, 1)

                for v in range(MAXU):
                    take_max(0, v)
                split_max(0)
                take_turned_max(0)
                for k in range(NS):
                    for v in max_units(k):
                        take_max(k // PER_G + 1, v)
                    if k // PER_G < G4 - 1 and k % PER_G == MAX_DONE:
                        split_max(k // PER_G + 1)
                    if k // PER_G < G4 - 1 and k % PER_G == MAX_TURN:
                        take_turned_max(k // PER_G + 1)
                for k0 in (0, 4):
                    dve.wait_ge(den_inverted, b * 2 + k0 // 4 + 1)
                    o = OP[:, k0 // 2:k0 // 2 + 2]
                    nc.vector.tensor_tensor(o, o, T1[:], ALU.mult).then_inc(o_normed, 4)
                dve.wait_ge(wo_mm, b + 1)
                for c in range(DC):
                    ins = nc.vector.scalar_tensor_tensor(ATT[:, c], flat(low4)[:, c], col["bo"][:, c:c + 1], XA[:, c],
                                                         ALU.add, ALU.add)
                ins.then_inc(att_ready, 1)
                dve.wait_ge(att_ready, b + 1)
                nc.vector.tensor_tensor(DOUBLED, ATT, XA[:], ALU.add).then_inc(summed, 1)
                own.close()

        @block.tensor
        def _(pe):
            pe.wait_ge(consts, CONSTS)
            pe.wait_ge(consts_p, 5)
            pe.wait_ge(const_in, NCONST)
            pe.wait_ge(ones_set, 1)
            with pe.Fori(0, B) as b:
                pe.wait_ge(xb_in, (b + 1) * 16)
                pe.wait_ge(att_ready, b)
                ln_out.pe_mean(nc, pe, b, XB, stat0)
                ln_out.pe_var(nc, pe, b, T1, stat1)
                pe.wait_ge(summed, 2 * b + 1)
                ln_join.pe_mean(nc, pe, b, XA, stat0)
                ln_join.pe_var(nc, pe, b, T1, stat1)
                pe.wait_ge(ln_join.normed, b + 1)
                ln1.pe_mean(nc, pe, b, XA, stat0)
                ln1.pe_var(nc, pe, b, T1, stat1)
                pe.wait_ge(hn_ready, b + 1)
                for a, w in enumerate((wq, wk)):
                    for c in range(DC):
                        if a == 1:
                            pe.wait_ge(qk_out, b * 4 + c + 1)
                        for half in range(2):
                            for k in range(DC):
                                ins = nc.tensor.matmul(ps[:, 2 * c + half], w[:, k, c * P:(c + 1) * P],
                                                       HN[:, k, 512 * half:512 * half + 512],
                                                       start=(k == 0), stop=(k == DC - 1))
                        ins.then_inc(qk_mm, 1)
                for j in range(QT):
                    if j >= 4:
                        pe.wait_ge(v_out, b * QT + j - 3)
                    for c in range(DC):
                        ins = nc.tensor.matmul(ps[:, 4 + j % 4], HN[:, c, j * P:(j + 1) * P], wv[:, c],
                                               start=(c == 0), stop=(c == DC - 1))
                    ins.then_inc(v_mm, 1)
                pe.wait_ge(qk_out, (b + 1) * 4)
                pe.wait_ge(v_out, (b + 1) * QT)

                def scores_for_max(g, v):
                    j, qt, kh = v // 16, (v // 2) % QT, v % 2
                    if v == 0:
                        pe.wait_ge(stacked[g], (b + 1) * STACKS)
                    if g > 0 or v >= 2:
                        pe.wait_ge(s_max, (b * G4 + g) * MAXU + v - 1)
                    nc.tensor.matmul(ps[:, v % 2], QS[0:ROWS, 4 * g + j, qt * P:(qt + 1) * P],
                                     KS[0:ROWS, 4 * g + j, 512 * kh:512 * kh + 512], start=True, stop=True)\
                        .then_inc(s_mm, 1)

                def turn_max(g):
                    pe.wait_ge(nm_ready, b * G4 + g + 1)
                    if g > 0:
                        pe.wait_ge(nmt_out, b * G4 + g)
                    for qt in range(QT):
                        ins = nc.tensor.transpose(ps[0:12, 2].bitcast(BF16)[:, qt * P:(qt + 1) * P],
                                                  NM[:, qt].rearrange("p a h -> p (a h)"), identb[:])
                    ins.then_inc(nmt_mm, 1)

                def transposed_scores(k):
                    g, qh, kt = STEPS[k]
                    if k % PER_G == 0:
                        pe.wait_ge(nm_in, (b * G4 + g + 1) * 16)
                    for hp in range(2):
                        if k >= 1:
                            pe.wait_ge(probs, b * 2 * NS + 2 * k + hp - 1)
                        for a in range(2):
                            h = 4 * g + 2 * hp + a
                            ins = nc.tensor.matmul(ps[:, 3 + 2 * hp + a], KS[0:ROWS + 3, h, kt * P:(kt + 1) * P],
                                                   QS[0:ROWS + 3, h, 512 * qh:512 * qh + 512], start=True, stop=True)
                        ins.then_inc(st_mm, 1)

                def values(k):
                    g, qh, kt = STEPS[k]
                    if kt == 0 and k > 0:
                        pe.wait_ge(o_out, b * 2 * G4 + k // QT)
                    pe.wait_ge(probs, b * 2 * NS + 2 * k + 2)
                    for j in range(4):
                        r0 = SLOT * j
                        ins = nc.tensor.matmul(ps[r0:r0 + SLOT, 7], VP[:, kt, g * P + r0:g * P + r0 + SLOT],
                                               PT[:, (2 * k + j // 2) % 4, j % 2], start=(kt == 0),
                                               stop=(kt == QT - 1), tile_position=(0, r0), skip_group_check=True)
                    ins.then_inc(pv_mm, 1)

                for v in range(MAXU):
                    scores_for_max(0, v)
                turn_max(0)
                for k in range(NS + 1):
                    if k < NS:
                        transposed_scores(k)
                        for v in max_units(k):
                            scores_for_max(k // PER_G + 1, v)
                        if k // PER_G < G4 - 1 and k % PER_G == MAX_TURN:
                            turn_max(k // PER_G + 1)
                    if k >= 1:
                        values(k - 1)
                for k in range(G4 * 2):
                    pe.wait_ge(o_out, b * 2 * G4 + k + 1)
                    if k >= 4:
                        pe.wait_ge(den_log, 2 * b + 1)
                    nc.tensor.matmul(ps[:, k % 4], sel[:], OP[:, k // 2, 512 * (k % 2):512 * (k % 2) + 512],
                                     start=True, stop=True).then_inc(den_mm, 1)
                pe.wait_ge(o_normed, (b + 1) * 2 * G4)
                for m in range(DC):
                    for half in range(2):
                        for g in range(G4):
                            ins = nc.tensor.matmul(low4[:, m, half], wo[:, g, m * P:(m + 1) * P],
                                                   OP[:, g, 512 * half:512 * half + 512],
                                                   start=(g == 0), stop=(g == G4 - 1))
                ins.then_inc(wo_mm, 1)


def experts(nc, attended_fm, doubled_fm, p, out_fm):
    F32R = mybir.dt.float32r
    QT = T // P
    NE, FE = 8, 1024
    FM = FE // P
    UNITS = FM * 2
    MIDS, RAWS, LATE = 8, 4, 3
    CONSTS = 6 + NE
    SILENT = -2.0 ** 127
    VEC_STEPS = 6
    PRODUCTS = [(0, 0), (0, 1), (1, 0)]
    with ExitStack() as ctx:
        sb, psum, sem = allocators(nc, ctx, "ex")
        X = sb("X", [P, DC, T])
        RES = sb("RES", [P, DC, T])
        HN = sb("HN", [P, DC, T])
        HNP = sb("HNP", [P, 2, DC, T], F32R)
        T1 = sb("T1", [P, DC, T])
        rstd = sb("rstd", [P, 1, T])
        OHT = sb("OHT", [P, T])
        OFF = sb("OFF", [P, T], BF16)
        silence = sb("silence", [P, NE, P], BF16)
        gw = sb("gw", [P, DC, NE])
        gb = sb("gb", [P, NE])
        b2 = sb("b2", [P, D])
        cols = sb("cols", [P, len(MOE_COLUMNS), DC])
        col = {k: cols[:, i] for i, k in enumerate(MOE_COLUMNS)}
        w1 = sb("w1", [P, DC, FE])
        w2 = sb("w2", [P, FM, D])
        b1 = sb("b1", [P, FM])
        b1p = sb("b1p", [P, 2, FM])
        w1p = sb("w1p", [P, 2, 2, DC, FE], F32R)
        w2p = sb("w2p", [P, 2, 2, FM, D], F32R)
        MID = sb("MID", [P, RAWS, 512])
        MIDP = sb("MIDP", [P, 2, MIDS, 512], F32R)
        LG = sb("LG", [P, QT, NE])
        OH = sb("OH", [P, QT, NE])
        top = sb("top", [P, QT])
        spare = sb("spare", [P, 1])
        order = sb("order", [P, NE])
        ident = sb("ident", [P, P])
        ones = sb("ones", [P, P])
        eps = sb("eps", [P, 1])
        one = sb("one", [P, 1])
        ps = psum("ps", [P, 8, 512])

        const_in = sem("const_in")
        consts = sem("consts")
        consts_p = sem("consts_p")
        x_in = sem("x_in")
        res_in = sem("res_in")
        ln2 = FeatureNorm(sem, "ln2", ones[:], eps[:, 0:1], 1)
        ln_end = FeatureNorm(sem, "end", ones[:], eps[:, 0:1], 1)
        hn_ready = sem("hn_ready")
        hn_high = sem("hn_high")
        hn_low = sem("hn_low")
        lg_mm = sem("lg_mm")
        oh_ready = sem("oh_ready")
        oht_mm = sem("oht_mm")
        oht_out = sem("oht_out")
        w_in = sem("w_in")
        w_high = sem("w_high")
        w_low = sem("w_low")
        mid_mm = sem("mid_mm")
        mid_high = sem("mid_high")
        mid_low = sem("mid_low")
        back_mm = sem("back_mm")
        total_ready = sem("total_ready")
        stored = sem("stored")
        vec = sem("vec")
        block = ctx.enter_context(nc.Block())

        fm = lambda a: a.rearrange("(c p) (b t) -> b p c t", p=P, t=T)
        a_v, d_v, o_v = fm(attended_fm), fm(doubled_fm), fm(out_fm)
        seq = lambda v, b: v[bass.ds(b, 1)].rearrange("o p c t -> p (o c) t")
        stat0 = ps[:, 0:2].rearrange("p (g h) t -> p g h t", g=1)
        stat1 = ps[:, 2:4].rearrange("p (g h) t -> p g h t", g=1)
        low4 = ps[:, 0:4].rearrange("p (g h) t -> p g h t", g=DC)
        NCONST = 16 * 4

        @block.sync
        def _(sp):
            sp.wait_ge(consts, CONSTS)
            for dst, src in ((gw[:], p["gate_w"].rearrange("(c p) n -> p c n", p=P)),
                             (gb[:], p["gate_b"].rearrange("(a n) -> a n", a=1).broadcast_to([P, NE])),
                             (cols[:], p["moe_columns"]), (b2[0:NE], p["b2"])):
                sp.dma_start(dst, src).then_inc(const_in, 16)
            with sp.Fori(0, B) as b:
                sp.wait_ge(ln_end.centered, 2 * b)
                sp.dma_start(X[:], seq(a_v, b)).then_inc(x_in, 16)
                sp.dma_start(RES[:], seq(d_v, b)).then_inc(res_in, 16)
                with sp.Fori(0, NE // 2) as e2:
                    for u in range(2):
                        ne = b * NE + e2 * 2 + u
                        sp.wait_ge(w_low, ne)
                        e = e2 * 2 + u
                        sp.dma_start(w1[:], p["w1"][bass.ds(e, 1)].rearrange("o (c p) f -> p (o c) f", p=P))\
                            .then_inc(w_in, 16)
                        sp.dma_start(w2[:], p["w2"][bass.ds(e, 1)].rearrange("o (c p) f -> p (o c) f", p=P))\
                            .then_inc(w_in, 16)
                        sp.dma_start(b1[:], p["b1_col"][bass.ds(e, 1)].rearrange("o p f -> (o p) f"))\
                            .then_inc(w_in, 16)

        @block.gpsimd
        def _(pool):
            pool.memset(ident[:], 0.0).then_inc(consts_p, 1)
            pool.memset(silence[:], 0.0).then_inc(consts_p, 1)
            pool.wait_ge(consts_p, 2)
            pool.affine_select(out=ident[:], in_=ident[:], compare_op=ALU.not_equal, fill=1.0, base=0,
                               pattern=[[-1, P]], channel_multiplier=1).then_inc(consts_p, 1)
            pool.affine_select(out=silence[:], in_=silence[:], compare_op=ALU.not_equal, fill=SILENT, base=0,
                               pattern=[[-1, NE], [0, P]], channel_multiplier=1).then_inc(consts_p, 1)
            with pool.Fori(0, B) as b, pool.Fori(0, NE // 2) as e2:
                for u in range(2):
                    ne = b * NE + e2 * 2 + u
                    pool.wait_ge(w_high, 3 * ne + 3)
                    pool.tensor_tensor(w1p[:, u, 1], w1[:], w1p[:, u, 0], ALU.subtract)
                    pool.tensor_tensor(w2p[:, u, 1], w2[:], w2p[:, u, 0], ALU.subtract).then_inc(w_low, 1)

        @block.scalar
        def _(act):
            act.wait_ge(consts, CONSTS)
            act.wait_ge(const_in, NCONST)

            def split_weights(ne, u):
                act.wait_ge(w_in, (ne + 1) * 48)
                nc.scalar.activation(b1p[:, u], b1[:], ACT.Copy).then_inc(w_high, 1)
                nc.scalar.activation(w1p[:, u, 0], w1[:], ACT.Copy).then_inc(w_high, 1)
                nc.scalar.activation(w2p[:, u, 0], w2[:], ACT.Copy).then_inc(w_high, 1)

            with act.Fori(0, B) as b:
                split_weights(b * NE, 0)
                ln2.act_square(nc, act, b, HN[:], T1[:])
                ln2.act_rstd(nc, act, b, stat1, rstd[:])
                act.wait_ge(hn_ready, b + 1)
                nc.scalar.activation(HNP[:, 0], HN[:], ACT.Copy).then_inc(hn_high, 1)
                act.wait_ge(oht_mm, b + 1)
                rows = ps[0:NE, 0:2].rearrange("p h t -> p (h t)")
                nc.scalar.activation(OHT[0:NE], rows, ACT.Copy)
                nc.scalar.activation(OFF[0:NE], rows, ACT.Identity, scale=-1.0, bias=one[0:NE, 0:1])\
                    .then_inc(oht_out, 1)

                def expert(e, u, split_next):
                    ne = b * NE + e
                    for k in range(UNITS):
                        n = ne * UNITS + k
                        act.wait_ge(mid_mm, n + 1)
                        if k >= RAWS:
                            act.wait_ge(mid_low, n - RAWS + 1)
                        if k >= MIDS:
                            act.wait_ge(back_mm, n - MIDS + 1)
                        bias = b1p[:, u, k // 2:k // 2 + 1]
                        nc.scalar.activation(MID[:, k % RAWS], ps[:, 4 + k % 4], ACT.Relu, bias=bias)
                        nc.scalar.activation(MIDP[:, 0, k % MIDS], ps[:, 4 + k % 4], ACT.Relu, bias=bias)\
                            .then_inc(mid_high, 1)
                        if k == 4 and split_next:
                            split_weights(ne + 1, 1 - u)

                with act.Fori(0, NE // 2 - 1) as e2:
                    for u in range(2):
                        expert(e2 * 2 + u, u, True)
                expert(NE - 2, 0, True)
                expert(NE - 1, 1, False)
                ln_end.act_square(nc, act, b, HN[:], T1[:])
                ln_end.act_rstd(nc, act, b, stat1, rstd[:])
                act.wait_ge(ln_end.normed, b + 1)
                act.dma_start(seq(o_v, b), HN[:]).then_inc(stored, 16)
            act.wait_ge(stored, B * 16)

        @block.vector
        def _(dve):
            for ins in (nc.vector.memset(eps[:], EPS), nc.vector.memset(ones[:], 1.0 / D), nc.vector.memset(one[:], 1.0),
                        nc.vector.memset(OHT[:], 0.0), nc.vector.memset(OFF[:], 0.0), nc.vector.memset(b2[:], 0.0)):
                ins.then_inc(consts, 1)
            for e in range(NE):
                nc.vector.memset(order[:, e:e + 1], float(NE - e)).then_inc(consts, 1)
            dve.wait_ge(const_in, NCONST)
            dve.wait_ge(consts, CONSTS)
            with dve.Fori(0, B) as b:
                own = Steps(dve, vec, VEC_STEPS, b)
                dve.wait_ge(stored, b * 16)
                ln2.dve_center(nc, dve, b, X[:], HN[:], stat0)
                ln2.dve_scale(nc, dve, b, HN[:], rstd[:], col["ln2_g"])
                for c in range(DC):
                    ins = nc.vector.tensor_scalar(HN[:, c], HN[:, c], col["ln2_b"][:, c:c + 1], None, ALU.add)
                ins.then_inc(hn_ready, 1)
                dve.wait_ge(hn_high, b + 1)
                nc.vector.tensor_tensor(HNP[:, 1], HN[:], HNP[:, 0], ALU.subtract).then_inc(hn_low, 1)
                dve.wait_ge(lg_mm, b + 1)
                lg = ps[:, 0, 0:QT * NE].rearrange("p (q e) -> p q e", e=NE)
                own.done(nc.vector.tensor_tensor(LG[:], lg, gb[:].rearrange("p (o e) -> p o e", o=1)
                                                 .broadcast_to([P, QT, NE]), ALU.add))
                wide = lambda t: t[:].rearrange("p (q o) -> p q o", o=1).broadcast_to([P, QT, NE])
                own.done(nc.vector.tensor_reduce(top[:], LG[:], AX.X, ALU.max))
                own.done(nc.vector.tensor_tensor(OH[:], LG[:], wide(top), ALU.is_ge))
                own.done(nc.vector.tensor_tensor(LG[:], OH[:], order[:].rearrange("p (o e) -> p o e", o=1)
                                                 .broadcast_to([P, QT, NE]), ALU.mult))
                own.done(nc.vector.tensor_reduce(top[:], LG[:], AX.X, ALU.max))
                own.done(nc.vector.tensor_tensor(OH[:], LG[:], wide(top), ALU.is_equal))
                beat = nc.vector.memset(spare[:], 0.0)
                beat.then_inc(oh_ready, 1)
                with dve.Fori(0, NE) as e:
                    for k in range(UNITS):
                        dve.wait_ge(mid_high, (b * NE + e) * UNITS + k + 1)
                        nc.vector.tensor_tensor(MIDP[:, 1, k % MIDS], MID[:, k % RAWS], MIDP[:, 0, k % MIDS],
                                                ALU.subtract).then_inc(mid_low, 1)
                dve.wait_ge(back_mm, (b + 1) * NE * UNITS)
                dve.wait_ge(res_in, (b + 1) * 16)
                nc.vector.tensor_tensor(X[:], RES[:], low4.rearrange("p g h t -> p g (h t)"), ALU.add)\
                    .then_inc(total_ready, 1)
                dve.wait_ge(total_ready, b + 1)
                ln_end.dve_center(nc, dve, b, X[:], HN[:], stat0)
                ln_end.dve_scale(nc, dve, b, HN[:], rstd[:], None)
                own.close()

        @block.tensor
        def _(pe):
            pe.wait_ge(consts, CONSTS)
            pe.wait_ge(consts_p, 4)
            pe.wait_ge(const_in, NCONST)
            with pe.Fori(0, B) as b:
                pe.wait_ge(x_in, (b + 1) * 16)
                ln2.pe_mean(nc, pe, b, X, stat0)
                ln2.pe_var(nc, pe, b, T1, stat1)
                pe.wait_ge(hn_ready, b + 1)
                for qt in range(QT):
                    for c in range(DC):
                        ins = nc.tensor.matmul(ps[:, 0, NE * qt:NE * qt + NE], HN[:, c, qt * P:(qt + 1) * P], gw[:, c],
                                               start=(c == 0), stop=(c == DC - 1))
                ins.then_inc(lg_mm, 1)
                pe.wait_ge(oh_ready, b + 1)
                for qt in range(QT):
                    ins = nc.tensor.transpose(ps[0:NE, qt // 4, P * (qt % 4):P * (qt % 4) + P], OH[:, qt], ident[:])
                ins.then_inc(oht_mm, 1)
                pe.wait_ge(oht_out, b + 1)
                pe.wait_ge(hn_low, b + 1)
                for m in range(DC):
                    for half in range(2):
                        nc.tensor.matmul(low4[:, m, half], b2[:, m * P:(m + 1) * P],
                                         OHT[:, 512 * half:512 * half + 512], start=True, stop=False,
                                         skip_group_check=True)
                with pe.Fori(0, NE // 2) as e2:
                    for u in range(2):
                        ne = b * NE + e2 * 2 + u
                        pe.wait_ge(w_low, ne + 1)

                        def hidden(k):
                            f, half = k // 2, k % 2
                            if k >= 4:
                                pe.wait_ge(mid_high, ne * UNITS + k - 3)
                            for c in range(DC):
                                for a, x in PRODUCTS:
                                    nc.tensor.matmul(ps[:, 4 + k % 4], w1p[:, u, a, c, f * P:(f + 1) * P],
                                                     HNP[:, x, c, 512 * half:512 * half + 512],
                                                     start=(c == 0 and a == 0 and x == 0), stop=False,
                                                     skip_group_check=True)
                            nc.tensor.matmul(ps[:, 4 + k % 4],
                                             silence[:, bass.ds(e2 * 2 + u, 1)].rearrange("p o f -> p (o f)"),
                                             OFF[:, 512 * half:512 * half + 512], start=False, stop=True,
                                             skip_group_check=True).then_inc(mid_mm, 1)

                        def back(k):
                            f, half = k // 2, k % 2
                            pe.wait_ge(mid_low, ne * UNITS + k + 1)
                            for m in range(DC):
                                for a, x in PRODUCTS:
                                    ins = nc.tensor.matmul(low4[:, m, half], w2p[:, u, a, f, m * P:(m + 1) * P],
                                                           MIDP[:, x, k % MIDS], start=False, stop=True,
                                                           skip_group_check=True)
                            ins.then_inc(back_mm, 1)

                        for k in range(UNITS + LATE):
                            if k < UNITS:
                                hidden(k)
                            if k >= LATE:
                                back(k - LATE)
                pe.wait_ge(total_ready, b + 1)
                ln_end.pe_mean(nc, pe, b, X, stat0)
                ln_end.pe_var(nc, pe, b, T1, stat1)


def slots(a, mark=0.0):
    out = np.zeros(a.shape[:-1] + (16, 32), a.dtype)
    out[..., 0:16] = np.reshape(a, a.shape[:-1] + (16, 16))
    out[..., 16] = mark
    return out.reshape(a.shape[:-1] + (512,))


def moe_inputs(i):
    f = lambda k: i["L0_ffn_" + k]
    out = {k: f(k) for k in ("wq", "wk", "gate_w", "gate_b", "b2", "w1", "w2")}
    out["wv"], out["bv"], out["wo"] = slots(f("wv")), slots(f("bv"), 1.0), slots(f("wo").T).T
    vectors = [i["L0_attn_ln_out_w"]] + [f(k) for k in MOE_COLUMNS[1:]]
    out["moe_columns"] = np.stack([a.reshape(DC, P).T for a in vectors], 1)
    out["b1_col"] = f("b1").reshape(8, 8, P).transpose(0, 2, 1)
    return {k: np.ascontiguousarray(v) for k, v in out.items()}


def quantized_mlp(nc, x_tm, w_gate, w_up, w_down, out_tm):
    F = w_gate.shape[0]
    BLK = 16
    WR = 8
    WP = F // WR
    FULL = F // P
    FK = [P] * FULL + ([F - FULL * P] if F % P else [])
    NK = len(FK)
    U = 2
    TILES = N // P
    MID_HIGH = (5.0, 3.5, 2.5)
    MID_LOW = (1.75, 1.25, 0.75, 0.25)
    SCALE_STEPS, ROUND_STEPS = 3, 9

    with ExitStack() as ctx:
        sb, psum, sem = allocators(nc, ctx, "qm")
        wg_r = sb("wg_r", [WP, WR, D])
        wu_r = sb("wu_r", [WP, WR, D])
        wd_r = sb("wd_r", [P, DC, F])
        wT = sb("wT", [P, 2, DC, F])
        wdT = sb("wdT", [P, NK, D])
        ident = sb("ident", [P, P])
        eps = sb("eps", [P, 1])
        x = sb("x", [P, U, D])
        xr = sb("xr", [P, U, D])
        xq = sb("xq", [P, U, D])
        xqT = sb("xqT", [P, U, D])
        th = sb("th", [P, F])
        h = sb("h", [P, U, F])
        hqT = sb("hqT", [P, U, NK, P])
        FMAX = WR * D
        tmp_h = [sb(f"{k}_h", [P, n]) for k, n in zip("qn qa qs qt amax rsc".split(), [FMAX] * 4 + [FMAX // BLK] * 2)]
        tmp_x = [sb(f"{k}_x", [P, n]) for k, n in zip("qn qa qs qt amax rsc".split(), [D] * 4 + [D // BLK] * 2)]
        y = sb("y", [P, D])
        stats = sb("stats", [P, 6])
        spare = sb("spare", [P, 1])
        mv = sb("mv", [P, 2])
        std = sb("std", [P, 1])
        rstd = sb("rstd", [P, 1])
        yn = sb("yn", [P, U, D])
        gate = psum("gate", [P, 1024])
        up = psum("up", [P, 1024])
        xt_ps = psum("xt_ps", [P, 512])
        ht_ps = psum("ht_ps", [P, 1024])
        y_ps = psum("y_ps", [P, 512])
        turn_ps = [gate[:, 0:512], gate[:, 512:1024], up[:, 0:512], up[:, 512:1024]]

        weights_in = sem("weights_in")
        consts = sem("consts")
        eps_set = sem("eps_set")
        wvec = sem("wvec")
        w_scaled = sem("w_scaled")
        w_signed = sem("w_signed")
        w_quant = sem("w_quant")
        w_mm = sem("w_mm")
        w_out = sem("w_out")
        x_in = [sem(f"x_in{u}") for u in range(U)]
        xr_in = [sem(f"xr_in{u}") for u in range(U)]
        x_scaled = sem("x_scaled")
        x_signed = sem("x_signed")
        h_scaled = sem("h_scaled")
        h_signed = sem("h_signed")
        xq_ready = sem("xq_ready")
        xT_mm = sem("xT_mm")
        xT_out = sem("xT_out")
        gate_mm = sem("gate_mm")
        tanh_out = sem("tanh_out")
        h_ready = sem("h_ready")
        hq_ready = sem("hq_ready")
        hT_mm = sem("hT_mm")
        hT_out = sem("hT_out")
        y_mm = sem("y_mm")
        y_ready = sem("y_ready")
        var_ready = sem("var_ready")
        std_ready = sem("std_ready")
        yn_ready = sem("yn_ready")
        stored = [sem(f"stored{u}") for u in range(U)]
        vec_xs, vec_xr, vec_hs, vec_hr = sem("vec_xs"), sem("vec_xr"), sem("vec_hs"), sem("vec_hr")
        silu_half = sem("silu_half")
        stats_ready = sem("stats_ready")
        inverted = sem("inverted")
        block = ctx.enter_context(nc.Block())

        W_JOBS = [(wg_r, WP, FMAX), (wu_r, WP, FMAX), (wd_r, P, DC * F)]
        W_TURNS = []
        for k, w_r in enumerate((wg_r, wu_r)):
            for r in range(WR):
                for c in range(DC):
                    W_TURNS.append((w_r[:, r, c * P:(c + 1) * P], WP, P, wT[:, k, c, r:F:WR], k))
        for c in range(DC):
            for k in range(NK):
                W_TURNS.append((wd_r[:, c, k * P:k * P + FK[k]], P, FK[k], wdT[0:FK[k], k, c * P:(c + 1) * P], 2))

        @block.sync
        def _(sp):
            sp.dma_start(wg_r[:], w_gate.rearrange("(p r) k -> p r k", r=WR)).then_inc(weights_in, 16)
            sp.dma_start(wu_r[:], w_up.rearrange("(p r) k -> p r k", r=WR)).then_inc(weights_in, 16)
            sp.dma_start(wd_r[:], w_down.rearrange("(c p) k -> p c k", p=P)).then_inc(weights_in, 16)

            def load(dst, arrived, n, u):
                sp.dma_start(dst[:, u], x_tm[bass.ds(n * P, P), :]).then_inc(arrived[u], 16)

            def load_x(n, u):
                sp.wait_ge(x_scaled, n - 1)
                load(x, x_in, n, u)

            def load_xr(n, u):
                sp.wait_ge(y_ready, n - 1)
                load(xr, xr_in, n, u)

            for u in range(U):
                load(x, x_in, u, u)
                load(xr, xr_in, u, u)
            load_x(2, 0)
            with sp.Fori(0, TILES // U - 2) as i:
                n = i * U + 3
                load_x(n, 1)
                load_xr(n - 1, 0)
                load_x(n + 1, 0)
                load_xr(n, 1)
            load_x(TILES - 1, 1)
            load_xr(TILES - 2, 0)
            load_xr(TILES - 1, 1)

        def over_steps(eng, step):
            step(0, 0)
            step(1, 1)
            with eng.Fori(0, TILES // U - 2) as i:
                for u in range(U):
                    step((i + 1) * U + u, u)
            step(TILES - 2, 0)
            step(TILES - 1, 1)

        def has(n, ahead):
            return not isinstance(n, int) or 0 <= n + ahead < TILES

        @block.gpsimd
        def _(pool):
            pool.memset(ident[:], 0.0).then_inc(consts, 1)
            pool.wait_ge(consts, 1)
            pool.affine_select(out=ident[:], in_=ident[:], compare_op=ALU.not_equal, fill=1.0, base=0,
                               pattern=[[-1, P]], channel_multiplier=1).then_inc(consts, 1)

        blocks = lambda t: t.rearrange("p (b k) -> p b k", k=BLK)

        def wide(t):
            return t.rearrange("p (b o) -> p b o", o=1).broadcast_to([t.shape[0], t.shape[1], BLK])

        def scale_blocks(own, tmp, src, rows, n, scaled):
            qn, _, _, _, amax, rsc = tmp
            nb = n // BLK
            own.done(nc.vector.tensor_reduce(amax[0:rows, 0:nb], blocks(src), AX.X, ALU.max,
                                             apply_absolute_value=True))
            own.done(nc.vector.tensor_scalar(amax[0:rows, 0:nb], amax[0:rows, 0:nb], 1.0 / 6.0, 1e-12,
                                             ALU.mult, ALU.max))
            own.done(nc.vector.reciprocal(rsc[0:rows, 0:nb], amax[0:rows, 0:nb]))
            nc.vector.tensor_tensor(blocks(qn[0:rows, 0:n]), blocks(src), wide(rsc[0:rows, 0:nb]),
                                    ALU.mult).then_inc(scaled, 1)

        def round_blocks(own, tmp, dst, rows, n, signed, at):
            _, qa, qs, qt, amax, _ = tmp
            own.eng.wait_ge(signed, at + 1)
            a, t, sg = qa[0:rows, 0:n], qt[0:rows, 0:n], qs[0:rows, 0:n]
            own.done(nc.vector.tensor_scalar(t, a, MID_HIGH[0], 2.0, ALU.is_gt, ALU.mult))
            for m in MID_HIGH[1:]:
                own.done(nc.vector.scalar_tensor_tensor(t, a, m, t, ALU.is_gt, ALU.add))
            own.done(nc.vector.tensor_scalar(t, t, 2.0, None, ALU.mult))
            for m in MID_LOW:
                own.done(nc.vector.scalar_tensor_tensor(t, a, m, t, ALU.is_gt, ALU.add))
            own.done(nc.vector.scalar_tensor_tensor(blocks(sg), blocks(sg), 0.5, wide(amax[0:rows, 0:n // BLK]),
                                                    ALU.mult, ALU.mult))
            return nc.vector.tensor_tensor(dst, t, sg, ALU.mult)

        def magnitude_and_sign(act, tmp, rows, n, scaled, signed, at):
            qn, qa, qs = tmp[:3]
            act.wait_ge(scaled, at + 1)
            nc.scalar.activation(qa[0:rows, 0:n], qn[0:rows, 0:n], ACT.Abs)
            nc.scalar.activation(qs[0:rows, 0:n], qn[0:rows, 0:n], ACT.Sign).then_inc(signed, 1)

        @block.scalar
        def _(act):
            def turned_x(n, u):
                act.wait_ge(xT_mm, n + 1)
                nc.scalar.activation(xqT[:, u], xt_ps[:, 0:D], ACT.Copy).then_inc(xT_out, 1)

            def gate_tanh(n):
                act.wait_ge(gate_mm, n + 1)
                nc.scalar.activation(th[:], gate[:, 0:F], ACT.Tanh, scale=0.5).then_inc(tanh_out, 1)

            def turned_h(n, u):
                act.wait_ge(hT_mm, n + 1)
                nc.scalar.activation(hqT[:, u, 0:FULL].rearrange("p k t -> p (k t)"), ht_ps[:, 0:FULL * P], ACT.Copy)
                nc.scalar.activation(hqT[0:FK[-1], u, NK - 1], ht_ps[0:FK[-1], FULL * P:NK * P], ACT.Copy)\
                    .then_inc(hT_out, 1)

            def finish(n, u):
                act.wait_ge(var_ready, n + 1)
                nc.scalar.activation(std[:], mv[:, 1:2], ACT.Sqrt, bias=eps[:, 0:1]).then_inc(std_ready, 1)
                act.wait_ge(yn_ready, n + 1)
                act.dma_start(out_tm[bass.ds(n * P, P), :], yn[:, u]).then_inc(stored[u], 16)

            def step(n, u):
                magnitude_and_sign(act, tmp_h, P, F, h_scaled, h_signed, n)
                if has(n, 2):
                    magnitude_and_sign(act, tmp_x, P, D, x_scaled, x_signed, n + 2)
                if has(n, 1):
                    turned_x(n + 1, 1 - u)
                if has(n, -1):
                    turned_h(n - 1, 1 - u)
                if has(n, 1):
                    gate_tanh(n + 1)
                if has(n, -1):
                    finish(n - 1, 1 - u)

            for k, (w_r, rows, n) in enumerate(W_JOBS):
                magnitude_and_sign(act, tmp_h, rows, n, w_scaled, w_signed, k)
            act.wait_ge(eps_set, 1)
            magnitude_and_sign(act, tmp_x, P, D, x_scaled, x_signed, 0)
            turned_x(0, 0)
            gate_tanh(0)
            magnitude_and_sign(act, tmp_x, P, D, x_scaled, x_signed, 1)
            over_steps(act, step)
            turned_h(TILES - 1, 1)
            finish(TILES - 1, 1)
            for u in range(U):
                act.wait_ge(stored[u], 16 * TILES // U)

        @block.vector
        def _(dve):
            nc.vector.memset(eps[:], EPS).then_inc(eps_set, 1)
            dve.wait_ge(weights_in, 16 * 3)
            own = Steps(dve, wvec, 3 * (SCALE_STEPS + ROUND_STEPS), 0)
            for k, (w_r, rows, n) in enumerate(W_JOBS):
                flat = w_r[:].rearrange("p r k -> p (r k)")
                scale_blocks(own, tmp_h, flat, rows, n, w_scaled)
                round_blocks(own, tmp_h, flat, rows, n, w_signed, k).then_inc(w_quant, 1)
                dve.wait_ge(w_quant, k + 1)
            for k, (src, kp, m, dst, job) in enumerate(W_TURNS):
                dve.wait_ge(w_mm, k + 1)
                nc.vector.tensor_copy(dst, turn_ps[k % 4][0:m, 0:kp]).then_inc(w_out, 1)

            def scale_x(n, u, loads):
                dve.wait_ge(x_in[u], 16 * loads)
                scale_blocks(Steps(dve, vec_xs, SCALE_STEPS, n), tmp_x, x[:, u], P, D, x_scaled)

            def round_x(n, u):
                round_blocks(Steps(dve, vec_xr, ROUND_STEPS, n), tmp_x, xq[:, u], P, D, x_signed, n)\
                    .then_inc(xq_ready, 1)
                dve.wait_ge(xq_ready, n + 1)

            def hidden(n, u):
                dve.wait_ge(tanh_out, n + 1)
                nc.vector.scalar_tensor_tensor(h[:, u], th[:], 1.0, gate[:, 0:F], ALU.add, ALU.mult)\
                    .then_inc(silu_half, 1)
                dve.wait_ge(silu_half, n + 1)
                nc.vector.scalar_tensor_tensor(h[:, u], h[:, u], 0.5, up[:, 0:F], ALU.mult, ALU.mult)\
                    .then_inc(h_ready, 1)

            def join(n, u, loads):
                dve.wait_ge(y_mm, n + 1)
                dve.wait_ge(xr_in[u], 16 * loads)
                nc.vector.tensor_tensor(y[:], xr[:, u], y_ps[:, 0:D], ALU.add).then_inc(y_ready, 1)
                dve.wait_ge(y_ready, n + 1)
                nc.vector.bn_stats(stats[:], y[:]).then_inc(stats_ready, 1)
                dve.wait_ge(stats_ready, n + 1)
                nc.vector.memset(spare[:], 0.0)
                nc.vector.bn_aggr(mv[:], stats[:]).then_inc(var_ready, 1)

            def norm(n, u, stores):
                dve.wait_ge(std_ready, n + 1)
                nc.vector.reciprocal(rstd[:], std[:]).then_inc(inverted, 1)
                dve.wait_ge(inverted, n + 1)
                if stores is not None:
                    dve.wait_ge(stored[u], 16 * stores)
                nc.vector.tensor_scalar(yn[:, u], y[:], mv[:, 0:1], rstd[:, 0:1], ALU.subtract, ALU.mult)\
                    .then_inc(yn_ready, 1)

            def step(n, u, before):
                dve.wait_ge(h_ready, n + 1)
                scale_blocks(Steps(dve, vec_hs, SCALE_STEPS, n), tmp_h, h[:, u], P, F, h_scaled)
                if has(n, 2):
                    scale_x(n + 2, u, before + 2)
                round_blocks(Steps(dve, vec_hr, ROUND_STEPS, n), tmp_h, h[:, u], P, F, h_signed, n)\
                    .then_inc(hq_ready, 1)
                if has(n, 2):
                    round_x(n + 2, u)
                if has(n, -1):
                    join(n - 1, 1 - u, before + u)
                if has(n, 1):
                    hidden(n + 1, 1 - u)
                if has(n, -1):
                    norm(n - 1, 1 - u, before + u - 1 if has(n, -3) else None)

            scale_x(0, 0, 1)
            round_x(0, 0)
            scale_x(1, 1, 1)
            round_x(1, 1)
            hidden(0, 0)
            step(0, 0, 0)
            step(1, 1, 0)
            with dve.Fori(0, TILES // U - 2) as i:
                for u in range(U):
                    step((i + 1) * U + u, u, i + 1)
            step(TILES - 2, 0, TILES // U - 1)
            step(TILES - 1, 1, TILES // U - 1)
            join(TILES - 1, 1, TILES // U)
            norm(TILES - 1, 1, TILES // U - 1)

        @block.tensor
        def _(pe):
            pe.wait_ge(consts, 2)
            for k, (src, kp, m, dst, job) in enumerate(W_TURNS):
                pe.wait_ge(w_quant, job + 1)
                if k >= 4:
                    pe.wait_ge(w_out, k - 3)
                nc.tensor.transpose(turn_ps[k % 4][0:m, 0:kp], src, ident[0:kp, 0:kp])\
                    .then_inc(w_mm, 1)
            pe.wait_ge(w_out, len(W_TURNS))

            def turn_x(n, u):
                pe.wait_ge(xq_ready, n + 1)
                for c in range(DC):
                    ins = nc.tensor.transpose(xt_ps[:, c * P:(c + 1) * P], xq[:, u, c * P:(c + 1) * P], ident[:])
                ins.then_inc(xT_mm, 1)

            def expand(n, u):
                pe.wait_ge(xT_out, n + 1)
                if has(n, -1):
                    pe.wait_ge(h_ready, n)
                for k, dst in ((0, gate), (1, up)):
                    for lo, hi in ((0, 512), (512, F)):
                        for c in range(DC):
                            ins = nc.tensor.matmul(dst[:, lo:hi], xqT[:, u, c * P:(c + 1) * P], wT[:, k, c, lo:hi],
                                                   start=(c == 0), stop=(c == DC - 1))
                ins.then_inc(gate_mm, 1)

            def turn_h(n, u):
                pe.wait_ge(hq_ready, n + 1)
                for k in range(NK):
                    ins = nc.tensor.transpose(ht_ps[0:FK[k], k * P:(k + 1) * P], h[:, u, k * P:k * P + FK[k]], ident[:])
                ins.then_inc(hT_mm, 1)

            def contract(n, u):
                pe.wait_ge(hT_out, n + 1)
                if has(n, -1):
                    pe.wait_ge(y_ready, n)
                for k in range(NK):
                    ins = nc.tensor.matmul(y_ps[:, 0:D], hqT[0:FK[k], u, k], wdT[0:FK[k], k],
                                           start=(k == 0), stop=(k == NK - 1))
                ins.then_inc(y_mm, 1)

            def step(n, u):
                if has(n, 1):
                    turn_x(n + 1, 1 - u)
                if has(n, -1):
                    turn_h(n - 1, 1 - u)
                    contract(n - 1, 1 - u)
                if has(n, 1):
                    expand(n + 1, 1 - u)

            turn_x(0, 0)
            expand(0, 0)
            over_steps(pe, step)
            turn_h(TILES - 1, 1)
            contract(TILES - 1, 1)


def rwkv_inputs(i):
    f = lambda k: i["L0_attn_" + k]
    names = ["tm_w1", "tm_w2", "td_w1", "td_w2", "Wr", "Wk", "Wv", "Wo", "Wg", "cWk", "cWv", "cWr"]
    out = {k: f(k) for k in names}
    out["columns"] = np.stack([f(k).reshape(2, DC, P).transpose(0, 2, 1) for k in RWKV_COLUMNS], 2)
    key, query = np.arange(P)[:, None], np.arange(P)[None]
    masks = [key == query]
    for m in (1, 2, 4, 8, 16, 32, 64):
        second = query[:, query[0] // m % 2 == 1]
        masks.append((key // (2 * m) == second // (2 * m)) & (key // m % 2 == 0))
    out["masks"] = np.concatenate(masks, 1).astype(np.float32)
    return {k: np.ascontiguousarray(v) for k, v in out.items()}


def program(nc, x_fm, rwkv_in, moe_in, fa_in, qm_in, work, out):
    rwkv(nc, x_fm, rwkv_in["masks"], rwkv_in, work[0])
    sequence_attention(nc, x_fm, work[0], moe_in, work[1], work[2])
    experts(nc, work[1], work[2], moe_in, work[3])
    feature_attention(nc, work[3], *fa_in, work[4])
    quantized_mlp(nc, work[4], *qm_in, out)


def kernel(**inputs):
    import concourse.bacc as _bacc
    from concourse.bass_utils import run_bass_kernel_spmd as _run

    nc = _bacc.Bacc("TRN2", target_bir_lowering=False, num_devices=1)
    i = {k: np.asarray(v) for k, v in inputs.items()}
    arrays = {}

    def inn(name, a):
        name = "in_" + name
        arrays[name] = np.ascontiguousarray(a)
        return nc.dram_tensor(name, a.shape, mybir.dt.from_np(a.dtype), kind="ExternalInput").ap()

    x_fm = inn("x_fm", i["L0_attn_x"].reshape(N, D).T)
    rwkv_in = {k: inn("rwkv_" + k, a) for k, a in rwkv_inputs(i).items()}
    moe_in = {k: inn("moe_" + k, a) for k, a in moe_inputs(i).items()}
    fa_in = [inn("fa_" + k, i["L1_attn_" + k]) for k in ("Wq", "bq", "Wk", "bk", "Wv", "bv", "Wo", "bo")]
    qm_in = [inn("qm_" + k, i["L1_ffn_" + k]) for k in ("w_gate", "w_up", "w_down")]
    work = [nc.dram_tensor(f"work{k}", (D, N) if k < 4 else (N, D), F32, kind="Internal").ap() for k in range(5)]
    out = nc.dram_tensor("out", (N, D), F32, kind="ExternalOutput").ap()
    program(nc, x_fm, rwkv_in, moe_in, fa_in, qm_in, work, out)
    r = _run(nc, [arrays], core_ids=[0])
    return r.results[0]["out"].reshape(B, T, D)
```
